# Optimizing a Trainium2 kernel written in Bass

```python
import numpy as np
import jax
import jax.numpy as jnp

def _softmax(x, axis=-1):
    return jax.nn.softmax(x, axis=axis)

def _gelu(x):
    return jax.nn.gelu(x, approximate=True)

def _silu(x):
    return jax.nn.silu(x)

def _sigmoid(x):
    return jax.nn.sigmoid(x)

def _layernorm(x, axis=-1, eps=1e-05):
    m = jnp.mean(x, axis=axis, keepdims=True)
    v = jnp.var(x, axis=axis, keepdims=True)
    return (x - m) / jnp.sqrt(v + eps)

def _scatter_add(tgt, idx, src, axis=0):
    return tgt.at[idx].add(src)

def _segment_sum(src, seg, n):
    return jax.ops.segment_sum(src, seg, n)
kernel_name = 'mk_perceiver_d2_seqx_r8_75a08e'

def setup_inputs(seed: int=0):
    np.random.seed(seed)
    _w = jnp.asarray

    def _rec_inputs():
        import jax
        import jax.numpy as jnp
        _rk = jax.random.key(seed)
        x = -4.161e-06 + 1 * jax.random.normal(jax.random.fold_in(_rk, 1), (8, 32, 256), jnp.float32)
        _lenS = 32 - jax.random.randint(jax.random.fold_in(_rk, 7), (8,), 0, max(1, 32 // 4) + 1, jnp.int32)
        _lenS2 = 512 - jax.random.randint(jax.random.fold_in(_rk, 8), (8,), 0, max(1, 512 // 4) + 1, jnp.int32)
        _ctx_2048P = jax.random.normal(jax.random.fold_in(_rk, 11), (8, 16, 256), jnp.float32)
        _ctx_2048c = jax.random.dirichlet(jax.random.fold_in(_rk, 511), 0.3 * jnp.ones((16,), jnp.float32), (8, 512))
        _ctx_2048t = jnp.einsum('bsk,bkd->bsd', _ctx_2048c, _ctx_2048P)
        _ctx_2048t = _ctx_2048t * jax.lax.rsqrt(jnp.mean(jnp.square(_ctx_2048t)) + 1e-12) * 0.953939
        ctx_2048 = -0.000192764 + 0.999654 * (_ctx_2048t + 0.3 * jax.random.normal(jax.random.fold_in(_rk, 611), (8, 512, 256), jnp.float32))
        _validS = jnp.arange(32)[None, :] < _lenS[:, None]
        _validS2 = jnp.arange(512)[None, :] < _lenS2[:, None]
        _causal = jnp.tril(jnp.ones((32, 32), dtype=bool))
        mask_BxS2_bk0 = jnp.logical_not(jnp.broadcast_to(_validS2[:, :], (8, 512)))
        return (x, ctx_2048, mask_BxS2_bk0)
    x, ctx_2048, mask_BxS2_bk0 = _rec_inputs()

    def _L0_xattn_setup():
        import jax, jax.numpy as jnp
        import numpy as np
        FP8_MAX = 448.0
        EPS = 1e-05

        def _fp8_roundtrip(x):
            return x.astype(jnp.float8_e4m3fn).astype(jnp.float32)

        def _div_clamp_fp8(x, scale):
            y = jnp.clip(x.astype(jnp.float32) / scale, -FP8_MAX, FP8_MAX)
            y = y.astype(jnp.bfloat16).astype(jnp.float32)
            return _fp8_roundtrip(y)

        def _ln(x, w, b):
            mu = jnp.mean(x, axis=-1, keepdims=True)
            var = jnp.mean(jnp.square(x - mu), axis=-1, keepdims=True)
            return (x - mu) * jax.lax.rsqrt(var + EPS) * w + b

        def _fp8_linear_pertensor(x, wq, w_scale, in_scale):
            xq = _div_clamp_fp8(x, in_scale)
            return jnp.einsum('bsi,oi->bso', xq * in_scale, wq) * w_scale

        def _gqa(q, k, v):
            scale = 1.0 / np.sqrt(q.shape[-1])
            scores = jnp.einsum('bsghd,btgd->bghst', q, k) * scale
            p = jax.nn.softmax(scores, axis=-1)
            return jnp.einsum('bghst,btgd->bsghd', p, v)
        key = jax.random.key(seed)
        ks = jax.random.split(key, 8)
        B, S, SC, H, NH, G, D = (2, 256, 64, 256, 16, 8, 128)

        def qw(k, out_f, in_f):
            w = jax.random.normal(k, (out_f, in_f), jnp.float32) * 0.02
            sc = jnp.max(jnp.abs(w)) / FP8_MAX
            return (_fp8_roundtrip(w / sc), sc.astype(jnp.float32))
        wq, wq_s = qw(ks[0], NH * D, H)
        wqx, wqx_s = qw(ks[1], NH * D, H)
        wk, wk_s = qw(ks[2], G * D, H)
        wv, wv_s = qw(ks[3], G * D, H)
        wproj, wp_s = qw(ks[4], H, 2 * NH * D)
        return {'hidden_states': jax.random.normal(ks[5], (B, S, H), jnp.float32), 'cond': jax.random.normal(ks[6], (B, SC, H), jnp.float32), 'ln_w': jnp.ones((H,), jnp.float32), 'ln_b': jnp.zeros((H,), jnp.float32), 'wq': wq, 'wq_scale': wq_s, 'q_in_scale': jnp.full((H,), 0.05, jnp.float32), 'wqx': wqx, 'wqx_scale': wqx_s, 'qx_in_scale': jnp.full((H,), 0.05, jnp.float32), 'wk': wk, 'wk_scale': wk_s, 'k_in_scale': jnp.full((H,), 0.05, jnp.float32), 'wv': wv, 'wv_scale': wv_s, 'v_in_scale': jnp.full((H,), 0.05, jnp.float32), 'w_kv_x': jax.random.normal(ks[7], (2 * G * D, H), jnp.float32) * 0.02, 'qln_w': jnp.ones((D,), jnp.float32), 'qln_b': jnp.zeros((D,), jnp.float32), 'kln_w': jnp.ones((D,), jnp.float32), 'kln_b': jnp.zeros((D,), jnp.float32), 'qxln_w': jnp.ones((D,), jnp.float32), 'qxln_b': jnp.zeros((D,), jnp.float32), 'kxln_w': jnp.ones((D,), jnp.float32), 'kxln_b': jnp.zeros((D,), jnp.float32), 'wproj': wproj, 'proj_w_scale': wp_s, 'proj_in_scale': jnp.asarray(0.05, jnp.float32), 'proj_smooth': jnp.full((2 * NH * D,), 0.05, jnp.float32)}
    _L0_xattn_all = _L0_xattn_setup()
    _L0_xattn_in = {k: v for k, v in _L0_xattn_all.items() if k in ('ln_w', 'ln_b', 'wq', 'wq_scale', 'q_in_scale', 'wqx', 'wqx_scale', 'qx_in_scale', 'wk', 'wk_scale', 'k_in_scale', 'wv', 'wv_scale', 'v_in_scale', 'w_kv_x', 'qln_w', 'qln_b', 'kln_w', 'kln_b', 'qxln_w', 'qxln_b', 'kxln_w', 'kxln_b', 'wproj', 'proj_w_scale', 'proj_in_scale', 'proj_smooth')}
    del _L0_xattn_all

    def _L0_attn_setup():
        import jax, jax.numpy as jnp
        import numpy as np
        from jax import lax

        def _causal_depthwise_conv(x, conv_w, conv_b):
            K = conv_w.shape[-1]
            xc = jnp.transpose(x, (0, 2, 1))
            xc = jnp.pad(xc, ((0, 0), (0, 0), (K - 1, 0)))
            D = xc.shape[1]
            y = lax.conv_general_dilated(xc, conv_w, window_strides=(1,), padding='VALID', dimension_numbers=('NCH', 'OIH', 'NCH'), feature_group_count=D)
            y = y + conv_b[None, :, None]
            return jnp.transpose(y, (0, 2, 1))
        key = jax.random.key(seed)
        ks = jax.random.split(key, 7)
        B, L, Dm, S, K = (4, 512, 256, 64, 4)
        s = 0.02
        x = jax.random.normal(ks[0], (B, L, Dm), dtype=jnp.float32)
        Wxproj = jax.random.normal(ks[1], (2 * S + 1, Dm), dtype=jnp.float32) * s
        Winproj = jax.random.normal(ks[2], (S, Dm), dtype=jnp.float32) * s
        Woutproj = jax.random.normal(ks[3], (Dm, S), dtype=jnp.float32) * s
        conv_w = jax.random.normal(ks[4], (Dm, 1, K), dtype=jnp.float32) * 0.5
        conv_b = jax.random.normal(ks[5], (Dm,), dtype=jnp.float32) * 0.02
        A_log = jnp.log(jnp.arange(1, S + 1, dtype=jnp.float32))
        D = jnp.ones((Dm,), dtype=jnp.float32)
        return {'x': x, 'Wxproj': Wxproj, 'Winproj': Winproj, 'Woutproj': Woutproj, 'conv_w': conv_w, 'conv_b': conv_b, 'A_log': A_log, 'D': D}
    _L0_attn_all = _L0_attn_setup()
    _L0_attn_in = {k: v for k, v in _L0_attn_all.items() if k in ('Wxproj', 'Winproj', 'Woutproj', 'conv_w', 'conv_b', 'A_log', 'D')}
    del _L0_attn_all

    def _L0_ffn_setup():
        import jax, jax.numpy as jnp
        import numpy as np
        NUM_EXPERTS = 8
        TOP_K = 2
        HIDDEN = 256
        INTER = 256
        SWIGLU_LIMIT = 7.0
        BATCH, SEQ = (4, 256)
        key = jax.random.key(seed)
        k0, k1, k2, k3, k4 = jax.random.split(key, 5)
        x = jax.random.normal(k0, (BATCH, SEQ, HIDDEN), jnp.float32)
        Wr = jax.random.normal(k1, (HIDDEN, NUM_EXPERTS), jnp.float32) * 0.02
        Wg = jax.random.normal(k2, (NUM_EXPERTS, HIDDEN, INTER), jnp.float32) * 0.02
        Wu = jax.random.normal(k3, (NUM_EXPERTS, HIDDEN, INTER), jnp.float32) * 0.02
        Wd = jax.random.normal(k4, (NUM_EXPERTS, INTER, HIDDEN), jnp.float32) * 0.02
        return {'hidden_states': x, 'Wr': Wr, 'Wg': Wg, 'Wu': Wu, 'Wd': Wd}
    _L0_ffn_all = _L0_ffn_setup()
    _L0_ffn_in = {k: v for k, v in _L0_ffn_all.items() if k in ('Wr', 'Wg', 'Wu', 'Wd')}
    del _L0_ffn_all

    def _L1_xattn_setup():
        import jax, jax.numpy as jnp
        import numpy as np
        key = jax.random.key(seed)
        k1, k2, k3 = jax.random.split(key, 3)
        B, S, D, M = (8, 256, 256, 128)
        hidden_states = jax.random.normal(k1, (B, S, D), dtype=jnp.float32)
        memory_tokens = jax.random.normal(k2, (B, M, D), dtype=jnp.float32)
        memory_mask = jax.random.randint(k3, (B, M), 0, 2).astype(jnp.bool_)
        return {'hidden_states': hidden_states, 'memory_tokens': memory_tokens, 'memory_mask': memory_mask}
    _L1_xattn_all = _L1_xattn_setup()
    _L1_xattn_in = {k: v for k, v in _L1_xattn_all.items() if k in ()}
    del _L1_xattn_all

    def _L1_attn_setup():
        import jax, jax.numpy as jnp
        import numpy as np
        HIDDEN = 256
        N_HEADS = 16
        N_KV_HEADS = 4
        HEAD_DIM = HIDDEN // N_HEADS
        ROPE_THETA = 10000.0
        B, S = (1, 256)

        def _apply_rope(x, position_ids, theta=ROPE_THETA):
            b, s, h, hd = x.shape
            dim_half = hd // 2
            inv_freq = 1.0 / theta ** (jnp.arange(0, dim_half, 2, dtype=jnp.float32) / dim_half)
            freqs = position_ids[:, :, None].astype(jnp.float32) * inv_freq[None, None, :]
            cos = jnp.cos(freqs)[:, :, None, :]
            sin = jnp.sin(freqs)[:, :, None, :]
            x_rot = x[..., :dim_half].reshape(b, s, h, dim_half // 2, 2)
            x0, x1 = (x_rot[..., 0], x_rot[..., 1])
            rotated = jnp.stack([x0 * cos - x1 * sin, x0 * sin + x1 * cos], axis=-1)
            rotated = rotated.reshape(b, s, h, dim_half)
            return jnp.concatenate([rotated, x[..., dim_half:]], axis=-1)
        key = jax.random.key(seed)
        k0, k1, k2, k3, k4 = jax.random.split(key, 5)
        std = 0.02
        return {'hidden_states': jax.random.normal(k0, (B, S, HIDDEN), dtype=jnp.float32), 'Wq': jax.random.normal(k1, (HIDDEN, N_HEADS * HEAD_DIM), dtype=jnp.float32) * std, 'Wk': jax.random.normal(k2, (HIDDEN, N_KV_HEADS * HEAD_DIM), dtype=jnp.float32) * std, 'Wv': jax.random.normal(k3, (HIDDEN, N_KV_HEADS * HEAD_DIM), dtype=jnp.float32) * std, 'Wo': jax.random.normal(k4, (HIDDEN, HIDDEN), dtype=jnp.float32) * std}
    _L1_attn_all = _L1_attn_setup()
    _L1_attn_in = {k: v for k, v in _L1_attn_all.items() if k in ('Wq', 'Wk', 'Wv', 'Wo')}
    del _L1_attn_all

    def _L1_ffn_setup():
        import jax, jax.numpy as jnp
        import numpy as np
        HIDDEN = 256
        INTER = 688
        LUT_SIZE = 16

        def _ghost_linear(x, idx, lut):
            w = lut[idx]
            return jnp.einsum('bsh,oh->bso', x, w)
        key = jax.random.key(seed)
        k_x, k_lut, k_g, k_u, k_d = jax.random.split(key, 5)
        x = jax.random.normal(k_x, (2, 512, HIDDEN), dtype=jnp.float32)
        lut = jax.random.normal(k_lut, (LUT_SIZE,), dtype=jnp.float32) * 0.02
        gate_idx = jax.random.randint(k_g, (INTER, HIDDEN), 0, LUT_SIZE, dtype=jnp.int32)
        up_idx = jax.random.randint(k_u, (INTER, HIDDEN), 0, LUT_SIZE, dtype=jnp.int32)
        down_idx = jax.random.randint(k_d, (HIDDEN, INTER), 0, LUT_SIZE, dtype=jnp.int32)
        return {'x': x, 'lut': lut, 'gate_idx': gate_idx, 'up_idx': up_idx, 'down_idx': down_idx}
    _L1_ffn_all = _L1_ffn_setup()
    _L1_ffn_in = {k: v for k, v in _L1_ffn_all.items() if k in ('lut', 'gate_idx', 'up_idx', 'down_idx')}
    del _L1_ffn_all
    return {'x': x, 'ctx_2048': ctx_2048, 'mask_BxS2_bk0': mask_BxS2_bk0, 'L0_xattn_ln_w': _L0_xattn_in['ln_w'], 'L0_xattn_ln_b': _L0_xattn_in['ln_b'], 'L0_xattn_wq': _L0_xattn_in['wq'], 'L0_xattn_wq_scale': _L0_xattn_in['wq_scale'], 'L0_xattn_q_in_scale': _L0_xattn_in['q_in_scale'], 'L0_xattn_wqx': _L0_xattn_in['wqx'], 'L0_xattn_wqx_scale': _L0_xattn_in['wqx_scale'], 'L0_xattn_qx_in_scale': _L0_xattn_in['qx_in_scale'], 'L0_xattn_wk': _L0_xattn_in['wk'], 'L0_xattn_wk_scale': _L0_xattn_in['wk_scale'], 'L0_xattn_k_in_scale': _L0_xattn_in['k_in_scale'], 'L0_xattn_wv': _L0_xattn_in['wv'], 'L0_xattn_wv_scale': _L0_xattn_in['wv_scale'], 'L0_xattn_v_in_scale': _L0_xattn_in['v_in_scale'], 'L0_xattn_w_kv_x': _L0_xattn_in['w_kv_x'], 'L0_xattn_qln_w': _L0_xattn_in['qln_w'], 'L0_xattn_qln_b': _L0_xattn_in['qln_b'], 'L0_xattn_kln_w': _L0_xattn_in['kln_w'], 'L0_xattn_kln_b': _L0_xattn_in['kln_b'], 'L0_xattn_qxln_w': _L0_xattn_in['qxln_w'], 'L0_xattn_qxln_b': _L0_xattn_in['qxln_b'], 'L0_xattn_kxln_w': _L0_xattn_in['kxln_w'], 'L0_xattn_kxln_b': _L0_xattn_in['kxln_b'], 'L0_xattn_wproj': _L0_xattn_in['wproj'], 'L0_xattn_proj_w_scale': _L0_xattn_in['proj_w_scale'], 'L0_xattn_proj_in_scale': _L0_xattn_in['proj_in_scale'], 'L0_xattn_proj_smooth': _L0_xattn_in['proj_smooth'], 'L0_attn_Wxproj': _L0_attn_in['Wxproj'], 'L0_attn_Winproj': _L0_attn_in['Winproj'], 'L0_attn_Woutproj': _L0_attn_in['Woutproj'], 'L0_attn_conv_w': _L0_attn_in['conv_w'], 'L0_attn_conv_b': _L0_attn_in['conv_b'], 'L0_attn_A_log': _L0_attn_in['A_log'], 'L0_attn_D': _L0_attn_in['D'], 'L0_ffn_Wr': _L0_ffn_in['Wr'], 'L0_ffn_Wg': _L0_ffn_in['Wg'], 'L0_ffn_Wu': _L0_ffn_in['Wu'], 'L0_ffn_Wd': _L0_ffn_in['Wd'], 'L1_attn_Wq': _L1_attn_in['Wq'], 'L1_attn_Wk': _L1_attn_in['Wk'], 'L1_attn_Wv': _L1_attn_in['Wv'], 'L1_attn_Wo': _L1_attn_in['Wo'], 'L1_ffn_lut': _L1_ffn_in['lut'], 'L1_ffn_gate_idx': _L1_ffn_in['gate_idx'], 'L1_ffn_up_idx': _L1_ffn_in['up_idx'], 'L1_ffn_down_idx': _L1_ffn_in['down_idx']}

def reference(x, ctx_2048, mask_BxS2_bk0, L0_xattn_ln_w, L0_xattn_ln_b, L0_xattn_wq, L0_xattn_wq_scale, L0_xattn_q_in_scale, L0_xattn_wqx, L0_xattn_wqx_scale, L0_xattn_qx_in_scale, L0_xattn_wk, L0_xattn_wk_scale, L0_xattn_k_in_scale, L0_xattn_wv, L0_xattn_wv_scale, L0_xattn_v_in_scale, L0_xattn_w_kv_x, L0_xattn_qln_w, L0_xattn_qln_b, L0_xattn_kln_w, L0_xattn_kln_b, L0_xattn_qxln_w, L0_xattn_qxln_b, L0_xattn_kxln_w, L0_xattn_kxln_b, L0_xattn_wproj, L0_xattn_proj_w_scale, L0_xattn_proj_in_scale, L0_xattn_proj_smooth, L0_attn_Wxproj, L0_attn_Winproj, L0_attn_Woutproj, L0_attn_conv_w, L0_attn_conv_b, L0_attn_A_log, L0_attn_D, L0_ffn_Wr, L0_ffn_Wg, L0_ffn_Wu, L0_ffn_Wd, L1_attn_Wq, L1_attn_Wk, L1_attn_Wv, L1_attn_Wo, L1_ffn_lut, L1_ffn_gate_idx, L1_ffn_up_idx, L1_ffn_down_idx):
    import jax
    import jax.numpy as jnp

    def _L0_xattn_ref(hidden_states, cond, ln_w, ln_b, wq, wq_scale, q_in_scale, wqx, wqx_scale, qx_in_scale, wk, wk_scale, k_in_scale, wv, wv_scale, v_in_scale, w_kv_x, qln_w, qln_b, kln_w, kln_b, qxln_w, qxln_b, kxln_w, kxln_b, wproj, proj_w_scale, proj_in_scale, proj_smooth):
        import jax, jax.numpy as jnp
        import numpy as np
        FP8_MAX = 448.0
        EPS = 1e-05

        def _fp8_roundtrip(x):
            return x.astype(jnp.float8_e4m3fn).astype(jnp.float32)

        def _div_clamp_fp8(x, scale):
            y = jnp.clip(x.astype(jnp.float32) / scale, -FP8_MAX, FP8_MAX)
            y = y.astype(jnp.bfloat16).astype(jnp.float32)
            return _fp8_roundtrip(y)

        def _ln(x, w, b):
            mu = jnp.mean(x, axis=-1, keepdims=True)
            var = jnp.mean(jnp.square(x - mu), axis=-1, keepdims=True)
            return (x - mu) * jax.lax.rsqrt(var + EPS) * w + b

        def _fp8_linear_pertensor(x, wq, w_scale, in_scale):
            xq = _div_clamp_fp8(x, in_scale)
            return jnp.einsum('bsi,oi->bso', xq * in_scale, wq) * w_scale

        def _gqa(q, k, v):
            scale = 1.0 / np.sqrt(q.shape[-1])
            scores = jnp.einsum('bsghd,btgd->bghst', q, k) * scale
            p = jax.nn.softmax(scores, axis=-1)
            return jnp.einsum('bghst,btgd->bsghd', p, v)
        b, s, _ = hidden_states.shape
        sc = cond.shape[1]
        d = qln_w.shape[0]
        nh = wq.shape[0] // d
        g = wk.shape[0] // d
        hpg = nh // g
        ln_out = _ln(hidden_states, ln_w, ln_b)
        q = _fp8_linear_pertensor(ln_out, wq, wq_scale, q_in_scale).reshape(b, s, g, hpg, d)
        q = _ln(q, qln_w, qln_b)
        k = _fp8_linear_pertensor(ln_out, wk, wk_scale, k_in_scale).reshape(b, s, g, d)
        k = _ln(k, kln_w, kln_b)
        v = _fp8_linear_pertensor(ln_out, wv, wv_scale, v_in_scale).reshape(b, s, g, d)
        core = _gqa(q, k, v).reshape(b, s, nh * d)
        qx = _fp8_linear_pertensor(ln_out, wqx, wqx_scale, qx_in_scale).reshape(b, s, g, hpg, d)
        qx = _ln(qx, qxln_w, qxln_b)
        kvx = jnp.einsum('bsi,oi->bso', cond, w_kv_x)
        kx, vx = jnp.split(kvx, 2, axis=-1)
        kx = _ln(kx.reshape(b, sc, g, d), kxln_w, kxln_b)
        vx = vx.reshape(b, sc, g, d)
        xout = _gqa(qx, kx, vx).reshape(b, s, nh * d)
        cat = jnp.concatenate([core, xout], axis=-1)
        catq = _div_clamp_fp8(cat, proj_smooth)
        return jnp.einsum('bsi,oi->bso', catq, wproj) * (proj_in_scale * proj_w_scale)

    def _L0_attn_ref(x, Wxproj, Winproj, Woutproj, conv_w, conv_b, A_log, D):
        import jax, jax.numpy as jnp
        import numpy as np
        from jax import lax

        def _causal_depthwise_conv(x, conv_w, conv_b):
            K = conv_w.shape[-1]
            xc = jnp.transpose(x, (0, 2, 1))
            xc = jnp.pad(xc, ((0, 0), (0, 0), (K - 1, 0)))
            D = xc.shape[1]
            y = lax.conv_general_dilated(xc, conv_w, window_strides=(1,), padding='VALID', dimension_numbers=('NCH', 'OIH', 'NCH'), feature_group_count=D)
            y = y + conv_b[None, :, None]
            return jnp.transpose(y, (0, 2, 1))
        S = A_log.shape[0]
        x_conv = _causal_depthwise_conv(x, conv_w, conv_b)
        ssm_params = jnp.einsum('bld,pd->blp', x, Wxproj)
        Bmat = ssm_params[..., :S]
        Cmat = ssm_params[..., S:2 * S]
        delta = jax.nn.softplus(ssm_params[..., 2 * S:])
        A = -jnp.exp(A_log)
        deltaA = jnp.exp(A[None, None, :] * delta)
        x_state = jnp.einsum('bld,sd->bls', x_conv, Winproj)
        Bu = delta * Bmat * x_state

        def combine(c1, c2):
            a1, b1 = c1
            a2, b2 = c2
            return (a1 * a2, a2 * b1 + b2)
        _, h = lax.associative_scan(combine, (deltaA, Bu), axis=1)
        h_mod = Cmat * h
        out = jnp.einsum('bls,ds->bld', h_mod, Woutproj) + D[None, None, :] * x_conv
        return out

    def _L0_ffn_ref(hidden_states, Wr, Wg, Wu, Wd):
        import jax, jax.numpy as jnp
        import numpy as np
        NUM_EXPERTS = 8
        TOP_K = 2
        HIDDEN = 256
        INTER = 256
        SWIGLU_LIMIT = 7.0
        BATCH, SEQ = (4, 256)
        router_logits = jnp.einsum('bsh,he->bse', hidden_states, Wr)
        topk_logits, selected = jax.lax.top_k(router_logits, TOP_K)
        router_probs = jax.nn.softmax(topk_logits, axis=-1)
        out = jnp.zeros_like(hidden_states)
        for e in range(NUM_EXPERTS):
            w_e = jnp.where(selected == e, router_probs, 0.0).sum(axis=-1, keepdims=True)
            g = jnp.einsum('bsh,hi->bsi', hidden_states, Wg[e])
            g = jnp.clip(jax.nn.silu(g), -SWIGLU_LIMIT, SWIGLU_LIMIT)
            u = jnp.einsum('bsh,hi->bsi', hidden_states, Wu[e])
            h = jnp.einsum('bsi,ih->bsh', g * u, Wd[e])
            out = out + h * w_e
        return out

    def _L1_xattn_ref(hidden_states, memory_tokens, memory_mask):
        import jax, jax.numpy as jnp
        import numpy as np
        B, S, D = hidden_states.shape
        scale = 1.0 / jnp.sqrt(jnp.asarray(D, hidden_states.dtype))
        scores = jnp.einsum('bsd,bmd->bsm', hidden_states, memory_tokens) * scale
        neg_inf = jnp.asarray(-1e+30, scores.dtype)
        scores = jnp.where(memory_mask[:, None, :], scores, neg_inf)
        attn = jax.nn.softmax(scores, axis=-1)
        readout = jnp.einsum('bsm,bmd->bsd', attn, memory_tokens)
        valid_b = jnp.any(memory_mask, axis=-1)
        out = jnp.where(valid_b[:, None, None], readout, jnp.zeros_like(readout))
        return out

    def _L1_attn_ref(hidden_states, Wq, Wk, Wv, Wo):
        import jax, jax.numpy as jnp
        import numpy as np
        HIDDEN = 256
        N_HEADS = 16
        N_KV_HEADS = 4
        HEAD_DIM = HIDDEN // N_HEADS
        ROPE_THETA = 10000.0
        B, S = (1, 256)

        def _apply_rope(x, position_ids, theta=ROPE_THETA):
            b, s, h, hd = x.shape
            dim_half = hd // 2
            inv_freq = 1.0 / theta ** (jnp.arange(0, dim_half, 2, dtype=jnp.float32) / dim_half)
            freqs = position_ids[:, :, None].astype(jnp.float32) * inv_freq[None, None, :]
            cos = jnp.cos(freqs)[:, :, None, :]
            sin = jnp.sin(freqs)[:, :, None, :]
            x_rot = x[..., :dim_half].reshape(b, s, h, dim_half // 2, 2)
            x0, x1 = (x_rot[..., 0], x_rot[..., 1])
            rotated = jnp.stack([x0 * cos - x1 * sin, x0 * sin + x1 * cos], axis=-1)
            rotated = rotated.reshape(b, s, h, dim_half)
            return jnp.concatenate([rotated, x[..., dim_half:]], axis=-1)
        b, s, _ = hidden_states.shape
        groups = N_HEADS // N_KV_HEADS
        q = (hidden_states @ Wq).reshape(b, s, N_HEADS, HEAD_DIM)
        k = (hidden_states @ Wk).reshape(b, s, N_KV_HEADS, HEAD_DIM)
        v = (hidden_states @ Wv).reshape(b, s, N_KV_HEADS, HEAD_DIM)
        position_ids = jnp.broadcast_to(jnp.arange(s)[None, :], (b, s))
        q = _apply_rope(q, position_ids)
        k = _apply_rope(k, position_ids)
        if groups > 1:
            k = jnp.repeat(k, groups, axis=2)
            v = jnp.repeat(v, groups, axis=2)
        scale = 1.0 / jnp.sqrt(jnp.float32(HEAD_DIM))
        scores = jnp.einsum('bshd,bthd->bhst', q, k) * scale
        attn = jax.nn.softmax(scores, axis=-1)
        out = jnp.einsum('bhst,bthd->bshd', attn, v)
        out = out.reshape(b, s, HIDDEN)
        return out @ Wo

    def _L1_ffn_ref(x, lut, gate_idx, up_idx, down_idx):
        import jax, jax.numpy as jnp
        import numpy as np
        HIDDEN = 256
        INTER = 688
        LUT_SIZE = 16

        def _ghost_linear(x, idx, lut):
            w = lut[idx]
            return jnp.einsum('bsh,oh->bso', x, w)
        gate = _ghost_linear(x, gate_idx, lut)
        up = _ghost_linear(x, up_idx, lut)
        h = jax.nn.silu(gate) * up
        return _ghost_linear(h, down_idx, lut)
    x = x + _L0_xattn_ref(_layernorm(x, axis=-1), ctx_2048, L0_xattn_ln_w, L0_xattn_ln_b, L0_xattn_wq, L0_xattn_wq_scale, L0_xattn_q_in_scale, L0_xattn_wqx, L0_xattn_wqx_scale, L0_xattn_qx_in_scale, L0_xattn_wk, L0_xattn_wk_scale, L0_xattn_k_in_scale, L0_xattn_wv, L0_xattn_wv_scale, L0_xattn_v_in_scale, L0_xattn_w_kv_x, L0_xattn_qln_w, L0_xattn_qln_b, L0_xattn_kln_w, L0_xattn_kln_b, L0_xattn_qxln_w, L0_xattn_qxln_b, L0_xattn_kxln_w, L0_xattn_kxln_b, L0_xattn_wproj, L0_xattn_proj_w_scale, L0_xattn_proj_in_scale, L0_xattn_proj_smooth)
    x = x + _L0_attn_ref(_layernorm(x, axis=-1), L0_attn_Wxproj, L0_attn_Winproj, L0_attn_Woutproj, L0_attn_conv_w, L0_attn_conv_b, L0_attn_A_log, L0_attn_D)
    x = x + _L0_ffn_ref(_layernorm(x, axis=-1), L0_ffn_Wr, L0_ffn_Wg, L0_ffn_Wu, L0_ffn_Wd)
    x = x + _L1_xattn_ref(_layernorm(x, axis=-1), ctx_2048, mask_BxS2_bk0)
    x = x + _L1_attn_ref(_layernorm(x, axis=-1), L1_attn_Wq, L1_attn_Wk, L1_attn_Wv, L1_attn_Wo)
    x = x + _L1_ffn_ref(_layernorm(x, axis=-1), L1_ffn_lut, L1_ffn_gate_idx, L1_ffn_up_idx, L1_ffn_down_idx)
    return x

_drawn_inputs = setup_inputs


def setup_inputs(seed=0):
    import zlib

    import numpy as np

    out = dict(_drawn_inputs(seed))
    spreads = {'L0_xattn_ln_w': (1.0, 0.2),
     'L0_xattn_ln_b': (0.0, 0.303),
     'L0_xattn_q_in_scale': (0.05000000074505806, 0.6),
     'L0_xattn_qx_in_scale': (0.05000000074505806, 0.6),
     'L0_xattn_k_in_scale': (0.05000000074505806, 0.6),
     'L0_xattn_v_in_scale': (0.05000000074505806, 0.6),
     'L0_xattn_qln_w': (1.0, 0.6),
     'L0_xattn_qln_b': (0.0, 0.8),
     'L0_xattn_kln_w': (1.0, 0.6),
     'L0_xattn_kln_b': (0.0, 2.0),
     'L0_xattn_qxln_w': (1.0, 0.6),
     'L0_xattn_qxln_b': (0.0, 0.8),
     'L0_xattn_kxln_w': (1.0, 0.6),
     'L0_xattn_kxln_b': (0.0, 2.0),
     'L0_xattn_proj_smooth': (0.05000000074505806, 0.2),
     'L0_attn_D': (1.0, 0.6)}
    factors = {'L0_attn_Wxproj': 8.0,
     'L0_attn_Winproj': 8.0,
     'L0_attn_Woutproj': 8.0,
     'L0_attn_conv_b': 3.838,
     'L0_attn_A_log': 8.0,
     'L0_ffn_Wr': 8.0,
     'L0_ffn_Wg': 7.079,
     'L0_ffn_Wu': 7.048,
     'L0_ffn_Wd': 7.092,
     'L1_attn_Wq': 64.0,
     'L1_attn_Wk': 64.0,
     'L1_attn_Wv': 8.0,
     'L1_attn_Wo': 8.0,
     'L1_ffn_lut': 8.0}
    for name, (base, spread) in spreads.items():
        noise = np.random.default_rng([zlib.crc32(name.encode()), seed]).standard_normal(out[name].shape)
        drawn = base * np.exp(spread * noise) if base else spread * noise
        out[name] = jnp.asarray(drawn.astype(out[name].dtype))
    for name, factor in factors.items():
        out[name] = (out[name] * factor).astype(out[name].dtype)
    return out
```

```python
from contextlib import ExitStack

import concourse.bass as bass
from concourse import mybir

fp32 = mybir.dt.float32
bf16 = mybir.dt.bfloat16
u16 = mybir.dt.uint16
u8 = mybir.dt.uint8
i32 = mybir.dt.int32
ALU = mybir.AluOpType
ACT = mybir.ActivationFunctionType
AX = mybir.AxisListType.X
DS = bass.DynSlice

B, S, C, NK = 8, 32, 256, 512
T = B * S
TT, CT, KT = T // 128, C // 128, NK // 128
G, HPG, D = 8, 2, 128
NH = G * HPG
NCH = 6
VARIANT = [0, 0, 1, 2, 3, 3]
EPS = 1e-5
SSM = 64
NE = 8
INTER, IPAD = 688, 768
IT = IPAD // 128
LUTN = 16
NLUT = 3 * CT * IPAD
FP8_MAX = 448.0
ROUND = 1.5 * 2.0 ** 20
FP8_MIN_NORMAL = 2.0 ** -6

COL, _n = {}, 0
for _name, _w in [("ln_w", CT), ("ln_b", CT), ("in_scale", 4 * CT), ("qln_w", 1), ("qln_b", 1), ("kln_w", 1),
                  ("kln_b", 1), ("qxln_w", 1), ("qxln_b", 1), ("kxln_w", 1), ("kxln_b", 1), ("smooth", 2 * NH),
                  ("conv_w", 4 * CT), ("conv_b", CT), ("ssm_d", CT), ("w_scale", 4), ("proj_w_scale", 1),
                  ("proj_in_scale", 1), ("lut", LUTN), ("a_log", 1)]:
    COL[_name] = slice(_n, _n + _w)
    _n += _w
NVEC = _n

CONST, _n = {}, 0
for _name, _w in [("ident", 128), ("ones", 128), ("center", 128), ("cos", T), ("sin", T), ("iota", LUTN)]:
    CONST[_name] = slice(_n, _n + _w)
    _n += _w
NCONST = _n

FRONT, LOOP, TAIL, LATE = range(4)
WORDS = [
    ("consts", NCONST, FRONT, LATE), ("vec", NVEC, FRONT, LATE), ("small", 1152, FRONT, LATE),
    ("x", TT * C, FRONT, LATE), ("core", TT * C, FRONT, LATE), ("ctxT_ring", 2 * CT * NK, FRONT, LOOP),
    ("ctx_ring", 2 * KT * C, FRONT, LOOP), ("wkT", CT * G * D, FRONT, LOOP), ("wvT", CT * G * D, FRONT, LOOP),
    ("A", CT * NH * T, FRONT, LOOP), ("beta", NH * T, FRONT, LOOP), ("qtmp", 2560, FRONT, LOOP),
    ("lutw", NLUT, LOOP, LATE), ("wpx", NH * C, LOOP, TAIL), ("catx", NH * T // 2, LOOP, TAIL),
    ("idx", NLUT // 4, LOOP, LOOP), ("luttmp", 2 * CT * IPAD, LOOP, LOOP),
    ("s", 2 * KT * NK, LOOP, LOOP), ("sq", 2 * 1024, LOOP, LOOP), ("vecs", 6 * NK, LOOP, LOOP),
    ("px", CT * NH * 64, LOOP, LOOP),
    ("wch", 2 * CT * 1024, FRONT, FRONT), ("raw", 2 * TT * 1024, FRONT, FRONT), ("lnT", CT * T, FRONT, FRONT),
    ("xs", 4 * CT * T, FRONT, FRONT), ("zlnT", 8 * T, FRONT, FRONT), ("uT", 8 * T, FRONT, FRONT),
    ("kT", G * T, FRONT, FRONT), ("v", TT * 1024, FRONT, FRONT), ("wkc", G * C, FRONT, FRONT),
    ("attn", 1024, FRONT, FRONT), ("catc", NH * T, FRONT, FRONT),
    ("keysT", CT * B * NK, TAIL, LATE), ("keys", B * KT * C, TAIL, LATE), ("mask", 2 * TT * NK, TAIL, LATE),
    ("h", TT * C, TAIL, LATE), ("hT", CT * T, TAIL, LATE),
    ("ssm", 5200, TAIL, TAIL), ("catf", NH * T, TAIL, LATE), ("experts", 2 * 3 * CT * C, TAIL, TAIL), ("moe", 2 * 2 * CT * T, TAIL, TAIL),
    ("rot", 2 * 2 * 512 + 2 * 2 * 128 + 2 * 128 + 4 * C, LATE, LATE), ("rotact", 4 * 1024, LATE, LATE),
    ("probs", 2 * TT * NK, LATE, LATE),
]


def place():
    at, done = {}, []
    for name, words, first, last in WORDS:
        words += -words % 8
        near = sorted((p, p + w) for p, w, a, z in done if a <= last and z >= first)
        spot = 0
        for p, q in near:
            if p - spot >= words:
                break
            spot = max(spot, q)
        at[name] = spot
        done.append((spot, words, first, last))
    return at, max(p + w for p, w, _, _ in done)



RING = [("center", 4, "act"), ("lnT", 4, "dve")]
for _n in (0, 1):
    RING += [(f"turn{_n}", 4, "dve"), (f"beta{_n}", 4, "act"), (f"A{_n}", 8, "act")]
RING += [("turn2", 4, "dve")]
for _n in (4, 5):
    RING += [(f"turn{_n}", 4, "dve"), (f"scores{_n}", 4, "dve"), (f"mix{_n}", 4, "dve")]
RING += [("core", 1, "act")]
RING_AT, RING_OWNER = {}, []
for _name, _w, _who in RING:
    RING_AT[_name] = len(RING_OWNER)
    RING_OWNER += [_who] * _w
ZORDER = [0, 1, 2, 4, 5]


def build(nc, io, out):
    ctx = ExitStack()
    with ctx:
        at, words = place()
        arena = ctx.enter_context(nc.sbuf_tensor("arena", [128, words], fp32))
        PS = ctx.enter_context(nc.psum_tensor("PS", [128, 4096], fp32))

        def sem(name):
            return ctx.enter_context(nc.semaphore(name))

        def buf(name, *dims, skip=0, dtype=fp32):
            n = 1
            for d in dims:
                n *= d
            wide = {fp32: 1, i32: 1, bf16: 2, u8: 4}[dtype]
            v = arena[:, at[name] + skip:at[name] + skip + -(-n // wide)]
            if dtype != fp32:
                v = v.bitcast(dtype)
            if len(dims) == 2:
                return v.rearrange("p (a b) -> p a b", a=dims[0])
            if len(dims) == 3:
                return v.rearrange("p (a b c) -> p a b c", a=dims[0], b=dims[1])
            return v

        def bank(n, *dims):
            v = PS[:, n * 512:(n + 1) * 512]
            if len(dims) == 2:
                return v[:, 0:dims[0] * dims[1]].rearrange("p (a b) -> p a b", a=dims[0])
            if len(dims) == 3:
                return v[:, 0:dims[0] * dims[1] * dims[2]].rearrange("p (a b c) -> p a b c", a=dims[0], b=dims[1])
            return v

        consts, vec = buf("consts", NCONST), buf("vec", NVEC)

        def const(name):
            return consts[:, CONST[name]]

        def col(name, i=0):
            return vec[:, COL[name].start + i:COL[name].start + i + 1]

        ident, ones = const("ident"), const("ones")
        _at = [0]

        def small(*dims):
            n = 1
            for d in dims:
                n *= d
            v = buf("small", *dims, skip=_at[0])
            _at[0] += n
            return v

        st, mv = small(NH, 6), small(NH, 2)
        var, rs0, rs, nt = small(32), small(32), small(32), small(32)
        inv_scale, inv_smooth = small(4 * CT), small(2 * NH)
        amax, asum = small(32), small(32)
        ssq, kvar, krs0, krs, knt = small(G), small(G), small(G), small(G), small(G)
        mcol = small(4)
        pscale = small(1)
        negA = small(1)
        logit, eq, cand = small(TT, NE), small(TT, NE), small(TT, NE)
        oh = [small(TT, NE), small(TT, NE)]
        top, best, gate2, prob = small(2, TT), small(2, TT), small(2, TT), small(2, TT)
        mixw, mixt = small(TT, NE), small(TT, NE)
        iota8, wide = small(TT, NE), small(128)
        assert _at[0] <= 1152, _at

        x = buf("x", TT, C)
        core = buf("core", TT, C)
        h, hT = buf("h", TT, C), buf("hT", CT, T)

        ld_const, ld_x, ld_wkn, ld_wkT, ld_wvT = (sem(n) for n in ("ld_const", "ld_x", "ld_wkn", "ld_wkT", "ld_wvT"))
        ld_chunk = [sem("ld_chunk0"), sem("ld_chunk1")]
        ld_wpc, ld_wpx = sem("ld_wpc"), sem("ld_wpx")
        ld_idx = [sem("ld_idx0"), sem("ld_idx1")]
        dve_step, act_step, pool_step = sem("dve_step"), sem("act_step"), sem("pool_step")
        ln_var, ln_rstd, ln_done = sem("ln_var"), sem("ln_rstd"), sem("ln_done")
        xs_ready, wk_centered, bk_ready = sem("xs_ready"), sem("wk_centered"), sem("bk_ready")
        proj_full, proj_read = sem("proj_full"), sem("proj_read")
        z_ready = sem("z_ready")
        ring_full = sem("ring_full")
        ring_read = {"act": sem("ring_read_act"), "dve": sem("ring_read_dve")}
        shifted_core, exp_core, pbd_ready, catc_ready = (sem(n) for n in ("shifted_core", "exp_core", "pbd_ready",
                                                                          "catc_ready"))
        front_over, loop_over = sem("front_over"), sem("loop_over")
        ld_ctxT, ld_ctx = [sem("ld_ctxT0"), sem("ld_ctxT1")], [sem("ld_ctx0"), sem("ld_ctx1")]
        kx_full, sq_ready, ssq_done, kvar_ready, krstd_ready = (sem(n) for n in (
            "kx_full", "sq_ready", "ssq_done", "kvar_ready", "krstd_ready"))
        st_full, scaled, mx_ready, mxf_ready, tr_full, m_ready, diag_ready, mb_full = (sem(n) for n in (
            "st_full", "scaled", "mx_ready", "mxf_ready", "tr_full", "m_ready", "diag_ready", "mb_full"))
        shifted, p_ready, psum_ready, sum_full, r_ready, pctx, px_ready = (sem(n) for n in (
            "shifted", "p_ready", "psum_ready", "sum_full", "r_ready", "pctx", "px_ready"))
        v_full, v_read, catx_ready = sem("v_full"), sem("v_read"), sem("catx_ready")
        idx_ready, lut_term, lut_added = sem("idx_ready"), sem("lut_term"), sem("lut_added")

        class Steps:

            def __init__(self, eng, s):
                self.eng, self.s, self.base, self.k = eng, s, 0, 0

            def __call__(self, ins):
                ins.then_inc(self.s, 1)
                self.k += 1
                self.eng.wait_ge(self.s, self.base + self.k)

            def loop(self, i, first, per):
                self.start, self.per, self.first = self.base + self.k, per, first
                self.base, self.k = (i - first) * per + self.start, 0

            def over(self, turns):
                assert self.k == self.per, self.k
                self.base, self.k = self.start + turns * self.per, 0

        def newton(dve, step, r, r0, v, t):
            step(nc.vector.tensor_tensor(t, r0, r0, ALU.mult))
            step(nc.vector.scalar_tensor_tensor(t, t, -0.5, v, ALU.mult, ALU.mult))
            step(nc.vector.scalar_tensor_tensor(r, t, 1.5, r0, ALU.add, ALU.mult))

        def stats(dve, step, n, srcs, k):
            for i, src in enumerate(srcs):
                last = nc.vector.bn_stats(st[:, i, :], src)
            step(last)
            for i in range(n):
                last = nc.vector.bn_aggr(mv[:, i, :], st[:, i, :])
            step(last)
            nc.vector.tensor_scalar(var[:, 0:n], mv[:, 0:n, 1], EPS, None, ALU.add).then_inc(ln_var, 1)
            dve.wait_ge(ln_rstd, k + 1)
            newton(dve, step, rs[:, 0:n], rs0[:, 0:n], var[:, 0:n], nt[:, 0:n])

        def act_rstd(act, step, n, k):
            act.wait_ge(ln_var, k + 1)
            step(nc.scalar.activation(rs0[:, 0:n], var[:, 0:n], ACT.Ln))
            nc.scalar.activation(rs0[:, 0:n], rs0[:, 0:n], ACT.Exp, scale=-0.5).then_inc(ln_rstd, 1)

        def token_norm(dve, step, src, dst, k):
            stats(dve, step, TT, [src[:, j, :] for j in range(TT)], k)
            for j in range(TT):
                last = nc.vector.tensor_scalar(dst[:, j, :], src[:, j, :], mv[:, j, 0:1], rs[:, j:j + 1],
                                               ALU.subtract, ALU.mult)
            return last

        qt = buf("qtmp", 2560)
        y_bf = buf("qtmp", 1024, dtype=bf16)
        e_bf = buf("qtmp", 1024, skip=512, dtype=bf16)
        m_bf = buf("qtmp", 1024, skip=1024, dtype=bf16)
        t_fp = buf("qtmp", 1024, skip=1536)

        def round_fp8(step, n, dst):
            step(nc.vector.tensor_scalar(e_bf[:, 0:n].bitcast(u16), y_bf[:, 0:n].bitcast(u16), 0x7F80, None,
                                         ALU.bitwise_and))
            step(nc.vector.tensor_scalar(m_bf[:, 0:n], e_bf[:, 0:n], FP8_MIN_NORMAL, ROUND, ALU.max, ALU.mult))
            step(nc.vector.tensor_tensor(t_fp[:, 0:n], y_bf[:, 0:n], m_bf[:, 0:n], ALU.add))
            return nc.vector.tensor_tensor(dst, t_fp[:, 0:n], m_bf[:, 0:n], ALU.subtract)

        def quantize(dve, step, src, inv, n, m, dst, read=None):
            ins = nc.vector.tensor_tensor(y_bf.rearrange("p (n m) -> p n m", n=n), src,
                                          inv.unsqueeze(2).broadcast_to([128, n, m]), ALU.mult)
            if read is None:
                step(ins)
            else:
                s, by, total = read
                ins.then_inc(s, by)
                dve.wait_ge(s, total)
            step(nc.vector.tensor_scalar(y_bf, y_bf, FP8_MAX, -FP8_MAX, ALU.min, ALU.max))
            return round_fp8(step, n * m, dst)

        wkn = buf("raw", G * C, skip=2048)
        wkc = buf("wkc", G, C)
        wkT, wvT = buf("wkT", CT, G * D), buf("wvT", CT, G * D)
        wch = [buf("wch", CT, 1024), buf("wch", CT, 1024, skip=2048)]
        wpc = buf("wch", NH, C)
        raw = [buf("raw", TT, 1024), buf("raw", TT, 1024, skip=2048)]
        RAW_SLOT = {0: 0, 1: 1, 2: 0, 4: 1, 5: 0}
        lnT, xs = buf("lnT", CT, T), buf("xs", 4, CT, T)
        zlnT, uT, kT, v = buf("zlnT", 8, T), buf("uT", 8, T), buf("kT", G, T), buf("v", TT, 1024)
        pbd = buf("uT", 8, 2, 128)
        at_s, at_p = buf("attn", 16, 32), buf("attn", 16, 32, skip=512)
        bk = wide
        catc = buf("catc", NH, T)
        A, beta = buf("A", CT, NH, T), buf("beta", NH, T)

        ctxT = [buf("ctxT_ring", CT, NK), buf("ctxT_ring", CT, NK, skip=CT * NK)]
        keysr = [buf("ctx_ring", KT, C), buf("ctx_ring", KT, C, skip=KT * C)]
        sS = [buf("s", KT, NK), buf("s", KT, NK, skip=KT * NK)]
        sq = [buf("sq", 1024), buf("sq", 1024, skip=1024)]
        mx, nm, R = buf("vecs", 512), buf("vecs", 512, skip=512), buf("vecs", 512, skip=1536)
        diag = buf("vecs", 4, 128, skip=1024)
        ps2 = buf("vecs", 2, 512, skip=2048)
        px = buf("px", CT, NH, 64)
        catx = buf("catx", NH, T, dtype=bf16)
        idx = buf("idx", 3, CT * IPAD, dtype=u8)
        lutt = [buf("luttmp", CT * IPAD), buf("luttmp", CT * IPAD, skip=CT * IPAD)]
        idx_raw = buf("luttmp", 2, CT * IPAD, dtype=i32)
        idx_raw2 = buf("s", CT * IPAD, skip=KT * NK, dtype=i32)
        lutw = buf("lutw", 3, CT * IPAD)
        wpx = buf("wpx", NH, C)
        SCALE = D ** -0.5

        def loop_pe(pe):
            def step(b, k, pair=None, prev=True):
                pe.wait_ge(ld_ctxT[k], 8 * (b - k) + 16)
                for t in range(KT):
                    n = 4 * b + t
                    for hf in range(2):
                        if not (prev is False and t == 0):
                            pe.wait_ge(sq_ready, 2 * n + hf - 1)
                        for c in range(CT):
                            last = nc.tensor.matmul(bank(hf), ctxT[k][:, c, t * 128:t * 128 + 128],
                                                    wkT[:, c, hf * 512:hf * 512 + 512],
                                                    start=c == 0, stop=c == CT - 1)
                        last.then_inc(kx_full, 1)
                    if not (prev is False and t < 2):
                        pe.wait_ge(scaled, n - 1)
                    for c in range(CT):
                        last = nc.tensor.matmul(bank(2 + t % 2), ctxT[k][:, c, t * 128:t * 128 + 128],
                                                A[:, c, :, DS(b * S, S)], start=c == 0, stop=c == CT - 1)
                    last.then_inc(st_full, 1)
                    if prev and t == 0:
                        maxima(b - 1)
                        if pair is not None:
                            values(pair, 0)
                    if prev and t == 1:
                        spread(b - 1)
                    if pair is not None and t == 2:
                        values(pair, 1)
                if prev:
                    mix(b - 1, 1 - k)

            def maxima(b):
                pe.wait_ge(mxf_ready, b + 1)
                if not (isinstance(b, int) and b == 0):
                    pe.wait_ge(px_ready, 2 * b)
                for j in range(4):
                    last = nc.tensor.transpose(bank(4, 4, 128)[:, j, :], mx[:, j * 128:j * 128 + 128], ident)
                last.then_inc(tr_full, 1)

            def spread(b):
                pe.wait_ge(diag_ready, b + 1)
                nc.tensor.matmul(bank(4), ones, diag.rearrange("p a q -> p (a q)"), start=True,
                                 stop=True).then_inc(mb_full, 1)

            def mix(b, k):
                pe.wait_ge(psum_ready, b + 1)
                nc.tensor.matmul(bank(4), ones, ps2[:, 0, :], start=True, stop=True).then_inc(sum_full, 1)
                pe.wait_ge(ld_ctx[k], 8 * (b - k) + 16)
                for c in range(CT):
                    for t in range(KT):
                        last = nc.tensor.matmul(bank(5 + c), keysr[k][:, t, c * 128:c * 128 + 128], sS[k][:, t, :],
                                                start=t == 0, stop=t == KT - 1)
                    last.then_inc(pctx, 1)

            def values(p, hf):
                if hf == 0:
                    pe.wait_ge(px_ready, 4 * p + 4)
                pe.wait_ge(v_read, 2 * p + hf + 1)
                for g in range(4 * hf, 4 * hf + 4):
                    for c in range(CT):
                        last = nc.tensor.matmul(bank(7)[:, (g % 4) * 128:(g % 4 + 1) * 128],
                                                wvT[:, c, g * D:(g + 1) * D], px[:, c, 2 * g:2 * g + 2, :],
                                                start=c == 0, stop=c == CT - 1)
                last.then_inc(v_full, 1)

            pe.wait_ge(front_over, 4)
            pe.wait_ge(wk_centered, 1)
            pe.wait_ge(ld_wvT, 16)
            step(0, 0, prev=False)
            step(1, 1)
            with pe.Fori(1, 4) as i:
                step(2 * i, 0)
                step(2 * i + 1, 1, pair=i - 1)
            maxima(7)
            spread(7)
            mix(7, 1)
            values(3, 0)
            values(3, 1)
            nc.tensor.matmul(bank(0)[:, 0:128], ident, ident, start=True, stop=True).then_inc(loop_over, 1)

        def loop_act(act, self_step):
            def step(b, k, prev=True):
                for t in range(KT):
                    n = 4 * b + t
                    if not (prev is False and t < 2):
                        act.wait_ge(ssq_done, n - 1)
                    for hf in range(2):
                        act.wait_ge(kx_full, 2 * n + hf + 1)
                        nc.scalar.activation(sq[t % 2][:, hf * 512:hf * 512 + 512], bank(hf), ACT.Square)\
                            .then_inc(sq_ready, 1)
                    if prev and t == 2:
                        exponentials(b - 1, 1 - k)
                    act.wait_ge(kvar_ready, n + 1)
                    self_step(nc.scalar.activation(krs0, kvar, ACT.Ln))
                    nc.scalar.activation(krs0, krs0, ACT.Exp, scale=-0.5).then_inc(krstd_ready, 1)
                if prev:
                    inverse(b - 1)

            def exponentials(b, k):
                act.wait_ge(shifted, b + 1)
                nc.scalar.activation(sS[k], sS[k], ACT.Exp, scale=SCALE).then_inc(p_ready, 1)

            def inverse(b):
                act.wait_ge(sum_full, b + 1)
                self_step(nc.scalar.activation(R, bank(4), ACT.Ln))
                nc.scalar.activation(R, R, ACT.Exp, scale=-1.0).then_inc(r_ready, 1)

            step(0, 0, prev=False)
            step(1, 1)
            with act.Fori(1, 4) as i:
                self_step.loop(i, 1, 10)
                step(2 * i, 0)
                step(2 * i + 1, 1)
                self_step.over(3)
            exponentials(7, 1)
            inverse(7)
            nc.scalar.activation(nt[:, 31:32], nt[:, 0:1], ACT.Copy).then_inc(loop_over, 1)

        LUT_STEP = 6

        def loop_pool(pool, self_step):
            def step(b, k, prev=True, own=True):
                if prev:
                    pool.wait_ge(m_ready, b)
                    nc.gpsimd.tensor_tensor(diag, ident.unsqueeze(1).broadcast_to([128, 4, 128]),
                                            mcol.unsqueeze(2).broadcast_to([128, 4, 128]), ALU.mult)\
                        .then_inc(diag_ready, 1)
                    if own:
                        terms(b, range(0, 2))
                    pool.wait_ge(p_ready, b)
                    pk = sS[1 - k]
                    self_step(nc.gpsimd.tensor_tensor(ps2, pk[:, 0:2, :], pk[:, 2:4, :], ALU.add))
                    nc.gpsimd.tensor_tensor(ps2[:, 0, :], ps2[:, 0, :], ps2[:, 1, :], ALU.add)\
                        .then_inc(psum_ready, 1)
                elif own:
                    terms(b, range(0, 2))
                if own:
                    terms(b, range(2, 4))
                    pool.wait_ge(mx_ready, b + 1)
                    nc.gpsimd.tensor_tensor(mx, mx, beta[:, :, DS(b * S, S)], ALU.add).then_inc(mxf_ready, 1)
                    terms(b, range(4, LUT_STEP))

            def terms(b, which):
                for q in which:
                    n = LUT_STEP * b + q
                    pool.wait_ge(lut_term, n + 1)
                    nc.gpsimd.tensor_tensor(lutw[:, q % 3, :], lutw[:, q % 3, :], lutt[q % 2], ALU.add)\
                        .then_inc(lut_added, 1)

            step(0, 0, prev=False)
            step(1, 1)
            with pool.Fori(1, 4) as i:
                self_step.loop(i, 1, 2)
                step(2 * i, 0)
                step(2 * i + 1, 1)
                self_step.over(3)
            step(8, 0, own=False)
            self_step(nc.gpsimd.memset(nt[:, 30:31], 0.0))
            nc.gpsimd.memset(nt[:, 30:31], 0.0).then_inc(loop_over, 1)

        def loop_dve(dve, self_step):
            def step(b, k, pair=None, prev=True):
                for t in range(KT):
                    n = 4 * b + t
                    dve.wait_ge(sq_ready, 2 * n + 2)
                    nc.vector.tensor_reduce(ssq, sq[t % 2].rearrange("p (g d) -> p g d", g=G), AX, ALU.add)\
                        .then_inc(ssq_done, 1)
                    dve.wait_ge(ssq_done, n + 1)
                    nc.vector.tensor_scalar(kvar, ssq, 1.0 / D, EPS, ALU.mult, ALU.add).then_inc(kvar_ready, 1)
                    dve.wait_ge(krstd_ready, n + 1)
                    newton(dve, self_step, krs, krs0, kvar, knt)
                    dve.wait_ge(st_full, n + 1)
                    if t == 0 and prev and not (isinstance(b, int) and b < 2):
                        dve.wait_ge(pctx, 2 * b - 2)
                    nc.vector.tensor_tensor(sS[k][:, t, :].rearrange("p (g q) -> p g q", g=G), bank(2 + t % 2, G, 64),
                                            krs.unsqueeze(2).broadcast_to([128, G, 64]), ALU.mult)\
                        .then_inc(scaled, 1)
                    if prev and t == 0:
                        maxima(b - 1)
                    if prev and t == 1:
                        shift(b - 1, 1 - k)
                    if pair is not None and t == 1:
                        quantize_values(pair, 0)
                    if pair is not None and t == 3:
                        quantize_values(pair, 1)
                    if t == 1:
                        terms(b, range(0, 2))
                    if t == 2:
                        terms(b, range(2, 4))
                dve.wait_ge(scaled, 4 * b + 4)
                if prev:
                    dve.wait_ge(tr_full, b)
                nc.vector.tensor_reduce(mx, sS[k].rearrange("p t q -> p q t"), AX, ALU.max).then_inc(mx_ready, 1)
                terms(b, range(4, LUT_STEP))
                if prev:
                    normalise(b - 1, 1 - k)

            def terms(b, which):
                for q in which:
                    n = LUT_STEP * b + q
                    j = q // 3
                    dve.wait_ge(idx_ready, 2)
                    if not (isinstance(b, int) and b == 0 and q < 2):
                        dve.wait_ge(lut_added, n - 1)
                    jc = CONST["iota"].start
                    jl = COL["lut"].start
                    nc.vector.tensor_scalar(lutt[q % 2], idx[:, q % 3, :], consts[:, DS(2 * b + (jc + j), 1)],
                                            vec[:, DS(2 * b + (jl + j), 1)], ALU.is_equal, ALU.mult)\
                        .then_inc(lut_term, 1)

            def maxima(b):
                dve.wait_ge(tr_full, b + 1)
                nc.vector.tensor_reduce(mcol, bank(4, 4, 128), AX, ALU.max).then_inc(m_ready, 1)

            def shift(b, k):
                dve.wait_ge(mb_full, b + 1)
                self_step(nc.vector.tensor_tensor(nm.rearrange("p (a q) -> p a q", a=NH), bank(4, NH, S),
                                                  beta[:, :, DS(b * S, S)], ALU.subtract))
                nc.vector.tensor_tensor(sS[k], sS[k], nm.unsqueeze(1).broadcast_to([128, KT, 512]), ALU.subtract)\
                    .then_inc(shifted, 1)

            def normalise(b, k):
                dve.wait_ge(r_ready, b + 1)
                self_step(nc.vector.scalar_tensor_tensor(nm, bank(4), -1.0, R, ALU.mult, ALU.mult))
                self_step(nc.vector.scalar_tensor_tensor(R, nm, 2.0, R, ALU.add, ALU.mult))
                dve.wait_ge(pctx, 2 * b + 2)
                if k == 0 and not (isinstance(b, int) and b == 0):
                    dve.wait_ge(v_full, b)
                for c in range(CT):
                    nc.vector.tensor_tensor(px[:, c, :, k * S:(k + 1) * S], bank(5 + c, NH, S),
                                            R.rearrange("p (a q) -> p a q", a=NH), ALU.mult).then_inc(px_ready, 1)

            def quantize_values(p, hf):
                dve.wait_ge(v_full, 2 * p + hf + 1)
                src = bank(7, 8, 64)
                heads = slice(8 * hf, 8 * hf + 8)
                y = y_bf[:, 0:512].rearrange("p (a q) -> p a q", a=8)
                nc.vector.tensor_tensor(y, src, inv_smooth[:, NH + 8 * hf:NH + 8 * hf + 8].unsqueeze(2)
                                        .broadcast_to([128, 8, 64]), ALU.mult).then_inc(v_read, 1)
                dve.wait_ge(v_read, 2 * p + hf + 2)
                self_step(nc.vector.tensor_scalar(y_bf[:, 0:512], y_bf[:, 0:512], FP8_MAX, -FP8_MAX, ALU.min, ALU.max))
                dst = catx[:, heads, DS(2 * S * p, 2 * S)]
                self_step(nc.vector.tensor_scalar(e_bf[:, 0:512].bitcast(u16), y_bf[:, 0:512].bitcast(u16), 0x7F80,
                                                  None, ALU.bitwise_and))
                self_step(nc.vector.tensor_scalar(m_bf[:, 0:512], e_bf[:, 0:512], FP8_MIN_NORMAL, ROUND, ALU.max,
                                                  ALU.mult))
                self_step(nc.vector.tensor_tensor(t_fp[:, 0:512], y_bf[:, 0:512], m_bf[:, 0:512], ALU.add))
                nc.vector.tensor_tensor(dst, t_fp[:, 0:512].rearrange("p (a q) -> p a q", a=8),
                                        m_bf[:, 0:512].rearrange("p (a q) -> p a q", a=8), ALU.subtract)\
                    .then_inc(catx_ready, 1)

            dve.wait_ge(front_over, 4)
            nc.vector.memset(nt[:, 29:30], 0.0).then_inc(v_read, 1)
            step(0, 0, prev=False)
            step(1, 1)
            with dve.Fori(1, 4) as i:
                self_step.loop(i, 1, 2 * (12 + 3) + 8)
                step(2 * i, 0)
                step(2 * i + 1, 1, pair=i - 1)
                self_step.over(3)
            maxima(7)
            shift(7, 1)
            normalise(7, 1)
            quantize_values(3, 0)
            quantize_values(3, 1)
            dve.wait_ge(catx_ready, 8)
            nc.vector.memset(nt[:, 29:30], 0.0).then_inc(loop_over, 1)

        keysT_all, keys_all = buf("keysT", CT, B, NK), buf("keys", B, KT, C)
        catf = buf("catf", NH, T)
        o_ = [0]

        def ssm(*dims):
            n = 1
            for d in dims:
                n *= d
            view = buf("ssm", *dims, skip=o_[0])
            o_[0] += n
            return view

        w_ssm, w_ssmo = ssm(CT, 4 * SSM), ssm(C)[0:SSM, :]
        hpad, xc, diagD = ssm(CT, B, S + 3), ssm(CT, T), ssm(CT, 128)
        sx, sy, sz, su, sa = (ssm(T)[0:SSM, :] for _ in range(5))
        wr = ssm(CT, NE)
        assert o_[0] <= 5200, o_
        we = [[buf("experts", CT, C, skip=(3 * k + i) * CT * C) for i in range(3)] for k in range(2)]
        we_all = [buf("experts", 3, CT, C, skip=3 * k * CT * C) if False else
                  buf("experts", 3 * CT * C, skip=3 * k * CT * C) for k in range(2)]
        sg = [buf("moe", CT * T, skip=2 * k * CT * T) for k in range(2)]
        am = [buf("moe", CT, T, skip=(2 * k + 1) * CT * T) for k in range(2)]
        mask = buf("mask", TT, NK)
        negm = buf("mask", TT, NK, skip=TT * NK)
        mask_u8 = buf("h", TT, NK, dtype=u8)
        mask_raw = buf("h", TT, NK // 4, dtype=i32)
        pr = buf("probs", TT, NK)
        pT = buf("probs", TT, KT * 128, skip=TT * NK)
        r_ = [0]

        def rot(*dims):
            n = 1
            for d in dims:
                n *= d
            view = buf("rot", *dims, skip=r_[0])
            r_[0] += n
            return view

        wq_r, wk_r, wv_r, wo_r = rot(2 * CT, 512), rot(2 * CT, 128), rot(CT, 128), rot(4, C)
        qr, qt2 = buf("rotact", 4, T), buf("rotact", 4, T, skip=1024)
        kr, kt2 = buf("rotact", T, skip=2048), buf("rotact", T, skip=2304)
        vr = buf("rotact", TT, 128, skip=2560)
        rs_ = buf("probs", 32, 32)
        rp_ = buf("rotact", 32, 32, skip=3072)
        oT = buf("probs", 4, T, skip=1024)
        sgf, hm = buf("catf", IT, T), buf("catf", IT, T, skip=IT * T)
        ld_w = {n: sem("ld_" + n) for n in ("ssm", "keysT", "keys", "mask", "rot")}
        ld_e = [sem("ld_experts0"), sem("ld_experts1")]
        cat_ready, proj_out, x_ready, turned, hT_ready, diag_d, hpad_zero = (sem(n) for n in (
            "cat_ready", "proj_out", "x_ready", "turned", "hT_ready", "diag_d", "hpad_zero"))
        ssm_p, conv_ready, ssm_x, soft_in, soft_out, decay, hm_ready, ssm_out_full = (sem(n) for n in (
            "ssm_p", "conv_ready", "ssm_x", "soft_in", "soft_out", "decay", "hm_ready", "ssm_out_full"))
        route_full, gap_ready, gap_exp, gu_full, silu_ready, act_ready, down_full, moe_added = (sem(n) for n in (
            "route_full", "gap_ready", "gap_exp", "gu_full", "silu_ready", "act_ready", "down_full", "moe_added"))
        mask_ready, sc_full, sc_shift, sc_exp, pt_full, pt_ready, read_full = (sem(n) for n in (
            "mask_ready", "sc_full", "sc_shift", "sc_exp", "pt_full", "pt_ready", "read_full"))
        qkv_full, rot_ready, v_ready, rsc_full, rsc_shift, rsc_exp, rp_ready, rmix_full, oT_ready, wo_full = (
            sem(n) for n in ("qkv_full", "rot_ready", "v_ready", "rsc_full", "rsc_shift", "rsc_exp", "rp_ready",
                             "rmix_full", "oT_ready", "wo_full"))
        ffn_full, ffn_silu, ffn_ready, ffn_out, stored = (sem(n) for n in (
            "ffn_full", "ffn_silu", "ffn_ready", "ffn_out", "stored"))
        XC = {"proj": 1, "ssm": 2, "moe": 3, "read": 4, "rot": 5, "ffn": 6}

        def tail_sync(sp):
            sp.wait_ge(loop_over, 4)
            sp.dma_start(w_ssm, io["ssm_in"]).then_inc(ld_w["ssm"], 16)
            sp.dma_start(w_ssmo, io["ssm_out"]).then_inc(ld_w["ssm"], 16)
            sp.dma_start(wr, io["router"]).then_inc(ld_w["ssm"], 16)
            for k in range(2):
                sp.dma_start(we_all[k], io["experts"][k].rearrange("p a c n -> p (a c n)")).then_inc(ld_e[k], 16)
            for j in range(TT):
                for b4 in range(4):
                    sp.dma_start(mask_raw[32 * b4:32 * b4 + 32, j, :],
                                 io["mask"][4 * j + b4:4 * j + b4 + 1, :].broadcast_to([32, NK // 4])).then_inc(ld_w["mask"], 16)
            for b in range(B):
                sp.dma_start(keysT_all[:, :, b, :], io["ctxT"][b]).then_inc(ld_w["keysT"], 16)
            for b in range(B):
                sp.dma_start(keys_all[:, b, :, :], io["ctx"][b]).then_inc(ld_w["keys"], 16)

            def load_expert(e, k):
                sp.wait_ge(down_full, e - 1)
                sp.dma_start(we_all[k], io["experts"][DS(e, 1)].rearrange("o p a c n -> (o p) (a c n)"))\
                    .then_inc(ld_e[k], 16)

            with sp.Fori(1, 4) as i:
                load_expert(2 * i, 0)
                load_expert(2 * i + 1, 1)
            sp.wait_ge(x_ready, XC["moe"])
            sp.dma_start(wq_r.rearrange("p (a c) n -> p a c n", a=2), io["wq_rot"]).then_inc(ld_w["rot"], 16)
            sp.dma_start(wk_r.rearrange("p (a c) n -> p a c n", a=2), io["wk_rot"]).then_inc(ld_w["rot"], 16)
            sp.dma_start(wv_r, io["wv_rot"]).then_inc(ld_w["rot"], 16)
            sp.dma_start(wo_r, io["wo_rot"]).then_inc(ld_w["rot"], 16)
            sp.wait_ge(x_ready, XC["ffn"])
            sp.dma_start(out, x).then_inc(stored, 16)
            sp.wait_ge(stored, 16)

        def tail_pe(pe):
            def turn_norm(k, nb):
                pe.wait_ge(ln_done, k + 1)
                o = bank(nb, CT, T)
                for i in range(4):
                    j, c = i // CT, i % CT
                    last = nc.tensor.transpose(o[:, c, j * 128:j * 128 + 128], h[:, j, c * 128:c * 128 + 128], ident)
                last.then_inc(turned, 1)

            pe.wait_ge(ld_wpx, 16)
            o = bank(0, TT, C)
            for j in range(TT):
                for i in range(NH):
                    if j == 0 and i % 4 == 0:
                        pe.wait_ge(cat_ready, i // 4 + 1)
                    last = nc.tensor.matmul(o[:, j, :], catf[:, i, j * 128:j * 128 + 128], wpx[:, i, :],
                                            start=i == 0, stop=i == NH - 1)
            last.then_inc(proj_out, 1)
            turn_norm(1, 1)
            pe.wait_ge(ld_w["ssm"], 48)
            pe.wait_ge(hT_ready, 1)
            for i in range(3):
                o = bank(2 + i // 2)[0:SSM, (i % 2) * T:(i % 2) * T + T]
                for c in range(CT):
                    last = nc.tensor.matmul(o, w_ssm[:, c, i * SSM:(i + 1) * SSM], hpad[:, c, :, 3:S + 3],
                                            start=c == 0, stop=c == CT - 1)
            last.then_inc(ssm_p, 1)
            pe.wait_ge(conv_ready, 1)
            for c in range(CT):
                last = nc.tensor.matmul(bank(4)[0:SSM, 0:T], w_ssm[:, c, 3 * SSM:4 * SSM], xc[:, c, :],
                                        start=c == 0, stop=c == CT - 1)
            last.then_inc(ssm_x, 1)
            pe.wait_ge(diag_d, 1)
            pe.wait_ge(hm_ready, 1)
            o = bank(5, TT, C)
            for j in range(TT):
                nc.tensor.matmul(o[:, j, :], sz[:, j * 128:j * 128 + 128], w_ssmo, start=True, stop=False,
                                 skip_group_check=True)
                for c in range(CT):
                    last = nc.tensor.matmul(o[:, j, c * 128:c * 128 + 128], xc[:, c, j * 128:j * 128 + 128],
                                            diagD[:, c, :], start=False, stop=c == CT - 1, skip_group_check=True)
            last.then_inc(ssm_out_full, 1)
            turn_norm(2, 6)
            pe.wait_ge(hT_ready, 2)
            o = bank(7, TT, NE)
            for j in range(TT):
                for c in range(CT):
                    last = nc.tensor.matmul(o[:, j, :], hT[:, c, j * 128:j * 128 + 128], wr[:, c, :],
                                            start=c == 0, stop=c == CT - 1)
            last.then_inc(route_full, 1)

            def gate_up(e, k):
                pe.wait_ge(ld_e[k], 8 * (e - k) + 16)
                if not (isinstance(e, int) and e < 2):
                    pe.wait_ge(act_ready, e - 1)
                for i in range(2):
                    o = bank(2 * k + i, CT, T)
                    for m in range(CT):
                        for c in range(CT):
                            last = nc.tensor.matmul(o[:, m, :], we[k][i][:, c, m * 128:m * 128 + 128], hT[:, c, :],
                                                    start=c == 0, stop=c == CT - 1)
                    last.then_inc(gu_full, 1)

            def down(e, k):
                pe.wait_ge(act_ready, e + 1)
                if not (isinstance(e, int) and e == 0):
                    pe.wait_ge(moe_added, e)
                o = bank(4 + k, TT, C)
                for j in range(TT):
                    for m in range(CT):
                        last = nc.tensor.matmul(o[:, j, :], am[k][:, m, j * 128:j * 128 + 128], we[k][2][:, m, :],
                                                start=m == 0, stop=m == CT - 1)
                last.then_inc(down_full, 1)

            gate_up(0, 0)
            gate_up(1, 1)
            down(0, 0)
            with pe.Fori(1, 4) as i:
                gate_up(2 * i, 0)
                down(2 * i - 1, 1)
                gate_up(2 * i + 1, 1)
                down(2 * i, 0)
            down(7, 1)
            turn_norm(3, 6)
            pe.wait_ge(hT_ready, 3)
            pe.wait_ge(ld_w["keysT"], 16 * B)
            for b in range(B):
                q0 = 32 * (b % 4)
                for c in range(CT):
                    last = nc.tensor.matmul(bank(b // 4)[q0:q0 + 32, :], hT[:, c, b * S:b * S + S], keysT_all[:, c, b, :],
                                            start=c == 0, stop=c == CT - 1)
                if b % 4 == 3:
                    last.then_inc(sc_full, 1)
            for j in range(TT):
                pe.wait_ge(sc_exp, j + 1)
                for t in range(KT):
                    last = nc.tensor.transpose(bank(2 + j, KT, 128)[:, t, :], pr[:, j, t * 128:t * 128 + 128], ident)
                last.then_inc(pt_full, 1)
            pe.wait_ge(ld_w["keys"], 16 * B)
            for b in range(B):
                j, q0 = b // 4, 32 * (b % 4)
                if q0 == 0:
                    pe.wait_ge(pt_ready, j + 1)
                for t in range(KT):
                    last = nc.tensor.matmul(bank(4 + j)[q0:q0 + 32, 0:C], pT[:, j, t * 128 + q0:t * 128 + q0 + 32],
                                            keys_all[:, b, t, :], start=t == 0, stop=t == KT - 1)
            last.then_inc(read_full, 1)
            turn_norm(4, 6)
            pe.wait_ge(hT_ready, 4)
            pe.wait_ge(ld_w["rot"], 64)
            for i in range(5):
                o = bank(i, 2, T)
                for sw in range(2):
                    for c in range(CT):
                        w = wq_r[:, sw * CT + c, i * 128:i * 128 + 128] if i < 4 else wk_r[:, sw * CT + c, :]
                        last = nc.tensor.matmul(o[:, sw, :], w, hT[:, c, :], start=c == 0, stop=c == CT - 1)
                last.then_inc(qkv_full, 1)
            o = bank(5, TT, 128)
            for j in range(TT):
                for c in range(CT):
                    last = nc.tensor.matmul(o[:, j, :], hT[:, c, j * 128:j * 128 + 128], wv_r[:, c, :],
                                            start=c == 0, stop=c == CT - 1)
            last.then_inc(qkv_full, 1)
            pe.wait_ge(rot_ready, 1)
            for g in range(4):
                for b in range(B):
                    q0 = 32 * (b % 4)
                    last = nc.tensor.matmul(bank(g)[q0:q0 + 32, (b // 4) * 128:(b // 4) * 128 + 128],
                                            kr[32 * g:32 * g + 32, b * S:b * S + S],
                                            qr[32 * g:32 * g + 32, :, b * S:b * S + S], start=True, stop=True)
            last.then_inc(rsc_full, 1)
            pe.wait_ge(rp_ready, 1)
            pe.wait_ge(v_ready, 1)
            rpv = rs_.rearrange("p (g j a) q -> p g j (a q)", g=4, j=TT)
            for b4 in range(4):
                q0 = 32 * b4
                for j in range(TT):
                    for g in range(4):
                        last = nc.tensor.matmul(bank(4 + b4)[32 * g:32 * g + 32, j * 128:j * 128 + 128],
                                                vr[q0:q0 + 32, j, 32 * g:32 * g + 32], rpv[q0:q0 + 32, g, j, :],
                                                start=True, stop=True)
            last.then_inc(rmix_full, 1)
            pe.wait_ge(oT_ready, 1)
            o = bank(0, TT, C)
            for j in range(TT):
                for a in range(4):
                    last = nc.tensor.matmul(o[:, j, :], oT[:, a, j * 128:j * 128 + 128], wo_r[:, a, :],
                                            start=a == 0, stop=a == 3)
            last.then_inc(wo_full, 1)
            turn_norm(5, 6)
            pe.wait_ge(hT_ready, 5)
            for i in range(IT // 2):
                for m in range(2):
                    o = bank(2 * i + m, 2, T)
                    for a in range(2):
                        for c in range(CT):
                            w0 = c * IPAD + (2 * i + a) * 128
                            last = nc.tensor.matmul(o[:, a, :], lutw[:, m, w0:w0 + 128], hT[:, c, :],
                                                    start=c == 0, stop=c == CT - 1)
                    last.then_inc(ffn_full, 1)
            for j in range(TT):
                o = bank(7, TT, C)
                for i in range(IT):
                    if j == 0 and i % 2 == 0:
                        pe.wait_ge(ffn_ready, i // 2 + 1)
                    last = nc.tensor.matmul(o[:, j, :], hm[:, i, j * 128:j * 128 + 128],
                                            lutw[:, 2, i * C:(i + 1) * C], start=i == 0, stop=i == IT - 1)
            last.then_inc(ffn_out, 1)

        def tail_act(act, step):
            act.wait_ge(loop_over, 4)
            for i in range(4):
                nc.scalar.activation(catf[:, 4 * i:4 * i + 4, :], catx[:, 4 * i:4 * i + 4, :], ACT.Copy)\
                    .then_inc(cat_ready, 1)
            act_rstd(act, step, TT, 7)
            act.wait_ge(ssm_p, 1)
            nc.scalar.activation(sx, bank(3)[0:SSM, 0:T], ACT.Copy).then_inc(soft_in, 1)
            step(nc.scalar.activation(negA[0:SSM, :], col("a_log")[0:SSM, :], ACT.Exp))
            act.wait_ge(soft_in, 2)
            step(nc.scalar.activation(sy, sy, ACT.Exp))
            step(nc.scalar.activation(sy, sy, ACT.Ln, bias=ones[0:SSM, 0:1]))
            nc.scalar.activation(sa, sx, ACT.Copy).then_inc(soft_out, 1)
            act.wait_ge(soft_in, 3)
            nc.scalar.activation(sa, sx, ACT.Exp, scale=negA[0:SSM, :]).then_inc(decay, 1)
            act_rstd(act, step, TT, 8)
            act.wait_ge(gap_ready, 1)
            nc.scalar.activation(gate2[:, 0, :], gate2[:, 1, :], ACT.Exp).then_inc(gap_exp, 1)

            def silu(e, k):
                act.wait_ge(gu_full, 2 * e + 1)
                if not (isinstance(e, int) and e < 2):
                    act.wait_ge(act_ready, e - 1)
                nc.scalar.activation(sg[k], bank(2 * k), ACT.Silu).then_inc(silu_ready, 1)

            nc.scalar.preload_act_table(ACT.Silu)
            silu(0, 0)
            silu(1, 1)
            with act.Fori(1, 4) as i:
                silu(2 * i, 0)
                silu(2 * i + 1, 1)
            nc.scalar.preload_act_table_set("natural_log_exp_and_others")
            act_rstd(act, step, TT, 9)
            for j in range(TT):
                act.wait_ge(sc_shift, j + 1)
                nc.scalar.activation(pr[:, j, :], pr[:, j, :], ACT.Exp, bias=amax[:, j:j + 1],
                                     accum_out=asum[:, j:j + 1]).then_inc(sc_exp, 1)
            act_rstd(act, step, TT, 10)
            act.wait_ge(qkv_full, 6)
            nc.scalar.activation(vr, bank(5, TT, 128), ACT.Copy).then_inc(v_ready, 1)
            act.wait_ge(rsc_shift, 1)
            nc.scalar.activation(rs_, rs_, ACT.Exp, scale=0.25).then_inc(rsc_exp, 1)
            act_rstd(act, step, TT, 11)
            nc.scalar.preload_act_table(ACT.Silu)
            for i in range(IT // 2):
                act.wait_ge(ffn_full, 2 * i + 1)
                nc.scalar.activation(sgf[:, 2 * i:2 * i + 2, :], bank(2 * i, 2, T), ACT.Silu).then_inc(ffn_silu, 1)

        def tail_pool(pool, step):
            pool.wait_ge(loop_over, 4)
            nc.gpsimd.memset(hpad[:, :, :, 0:3], 0.0).then_inc(hpad_zero, 1)
            for c in range(CT):
                last = nc.gpsimd.tensor_tensor(diagD[:, c, :], ident, col("ssm_d", c).broadcast_to([128, 128]), ALU.mult)
            last.then_inc(diag_d, 1)
            pool.wait_ge(ld_w["mask"], 16 * B)
            step(nc.gpsimd.tensor_copy(mask, mask_u8))
            nc.gpsimd.tensor_scalar(negm, mask, -1.0, 1e30, ALU.add, ALU.mult).then_inc(mask_ready, 1)

        def tail_dve(dve, step):
            def norm(k):
                dve.wait_ge(x_ready, k)
                token_norm(dve, step, x, h, 6 + k).then_inc(ln_done, 1)
                dve.wait_ge(turned, k)

            dve.wait_ge(loop_over, 4)
            step(nc.vector.tensor_tensor(pscale, col("proj_w_scale"), col("proj_in_scale"), ALU.mult))
            dve.wait_ge(proj_out, 1)
            step(nc.vector.tensor_tensor(core, core, bank(0, TT, C), ALU.add))
            nc.vector.scalar_tensor_tensor(x, core, pscale, x, ALU.mult, ALU.add).then_inc(x_ready, 1)
            dve.wait_ge(mask_ready, 1)
            norm(1)
            dve.wait_ge(hpad_zero, 1)
            o = bank(1, CT, T)
            for c in range(CT):
                last = nc.vector.tensor_copy(hpad[:, c, :, 3:S + 3], o[:, c, :].rearrange("p (b s) -> p b s", b=B))
            last.then_inc(hT_ready, 1)
            dve.wait_ge(hT_ready, 1)
            xcv = xc.rearrange("p c (b s) -> p c b s", b=B)
            for c in range(CT):
                last = nc.vector.tensor_scalar(xcv[:, c], hpad[:, c, :, 0:S], col("conv_w", 4 * c), col("conv_b", c),
                                               ALU.mult, ALU.add)
            step(last)
            for k in range(1, 4):
                for c in range(CT):
                    last = nc.vector.scalar_tensor_tensor(xcv[:, c], hpad[:, c, :, k:S + k], col("conv_w", 4 * c + k),
                                                          xcv[:, c], ALU.mult, ALU.add)
                if k < 3:
                    step(last)
            last.then_inc(conv_ready, 1)
            dve.wait_ge(soft_in, 1)
            nc.vector.scalar_tensor_tensor(sy, sx, -1.0, sx, ALU.mult, ALU.min).then_inc(soft_in, 1)
            dve.wait_ge(soft_out, 1)
            step(nc.vector.tensor_scalar(negA[0:SSM, :], negA[0:SSM, :], -1.0, None, ALU.mult))
            nc.vector.scalar_tensor_tensor(sx, sx, 0.0, sy, ALU.max, ALU.add).then_inc(soft_in, 1)
            dve.wait_ge(soft_in, 3)
            step(nc.vector.tensor_tensor(su, sx, bank(2)[0:SSM, 0:T], ALU.mult))
            dve.wait_ge(ssm_x, 1)
            step(nc.vector.tensor_tensor(su, su, bank(4)[0:SSM, 0:T], ALU.mult))
            dve.wait_ge(decay, 1)
            step(nc.vector.memset(sa.rearrange("p (b s) -> p b s", b=B)[:, :, 0:1], 0.0))
            step(nc.vector.tensor_tensor_scan(sy, sa, su, 0.0, ALU.mult, ALU.add))
            nc.vector.tensor_tensor(sz, sy, bank(2)[0:SSM, T:2 * T], ALU.mult).then_inc(hm_ready, 1)
            dve.wait_ge(ssm_out_full, 1)
            nc.vector.tensor_tensor(x, x, bank(5, TT, C), ALU.add).then_inc(x_ready, 1)
            norm(2)
            nc.vector.tensor_copy(hT, bank(6, CT, T)).then_inc(hT_ready, 1)
            dve.wait_ge(route_full, 1)
            iota = const("iota")[:, 0:NE].unsqueeze(1).broadcast_to([128, TT, NE])
            step(nc.vector.tensor_scalar(iota8, iota, float(NE), None, ALU.add))
            step(nc.vector.tensor_copy(logit, bank(7, TT, NE)))

            def over(a):
                return a.unsqueeze(2).broadcast_to([128, TT, NE])

            for k in range(2):
                step(nc.vector.tensor_reduce(top[:, k, :], logit, AX, ALU.max))
                step(nc.vector.tensor_tensor(eq, logit, over(top[:, k, :]), ALU.is_equal))
                step(nc.vector.scalar_tensor_tensor(cand, eq, -float(NE), iota8, ALU.mult, ALU.add))
                step(nc.vector.tensor_reduce(best[:, k, :], cand, AX, ALU.min))
                step(nc.vector.tensor_tensor(oh[k], cand, over(best[:, k, :]), ALU.is_equal))
                if k == 0:
                    step(nc.vector.scalar_tensor_tensor(logit, oh[k], -3.0e38, logit, ALU.mult, ALU.add))
            nc.vector.tensor_tensor(gate2[:, 1, :], top[:, 1, :], top[:, 0, :], ALU.subtract).then_inc(gap_ready, 1)
            dve.wait_ge(gap_exp, 1)
            step(nc.vector.tensor_scalar(gate2[:, 1, :], gate2[:, 0, :], 1.0, None, ALU.add))
            step(nc.vector.reciprocal(prob[:, 0, :], gate2[:, 1, :]))
            step(nc.vector.tensor_tensor(prob[:, 1, :], prob[:, 0, :], gate2[:, 0, :], ALU.mult))
            step(nc.vector.tensor_tensor(mixw, oh[0], over(prob[:, 0, :]), ALU.mult))
            step(nc.vector.tensor_tensor(mixt, oh[1], over(prob[:, 1, :]), ALU.mult))
            nc.vector.tensor_tensor(mixw, mixw, mixt, ALU.add).then_inc(moe_added, 1)

            def activate(e, k):
                dve.wait_ge(silu_ready, e + 1)
                step(nc.vector.tensor_scalar(sg[k], sg[k], 7.0, -7.0, ALU.min, ALU.max))
                dve.wait_ge(gu_full, 2 * e + 2)
                if not (isinstance(e, int) and e < 2):
                    dve.wait_ge(down_full, e - 1)
                nc.vector.tensor_tensor(am[k], sg[k].rearrange("p (m t) -> p m t", m=CT), bank(2 * k + 1, CT, T),
                                        ALU.mult).then_inc(act_ready, 1)

            def add_expert(e, k):
                dve.wait_ge(down_full, e + 1)
                dve.wait_ge(moe_added, e + 1)
                o = bank(4 + k, TT, C)
                for j in range(TT):
                    last = nc.vector.scalar_tensor_tensor(x[:, j, :], o[:, j, :],
                                                          mixw.rearrange("p j e -> p (j e)")[:, DS(e + j * NE, 1)],
                                                          x[:, j, :], ALU.mult, ALU.add)
                last.then_inc(moe_added, 1)

            activate(0, 0)
            activate(1, 1)
            add_expert(0, 0)
            with dve.Fori(1, 4) as i:
                step.loop(i, 1, 2)
                activate(2 * i, 0)
                add_expert(2 * i - 1, 1)
                activate(2 * i + 1, 1)
                add_expert(2 * i, 0)
                step.over(3)
            add_expert(7, 1)
            dve.wait_ge(moe_added, 9)
            nc.vector.memset(nt[:, 29:30], 0.0).then_inc(x_ready, 1)
            norm(3)
            nc.vector.tensor_copy(hT, bank(6, CT, T)).then_inc(hT_ready, 1)
            step(nc.vector.tensor_reduce(top[:, 0, :], mask, AX, ALU.max))
            for j in range(TT):
                dve.wait_ge(sc_full, j + 1)
                step(nc.vector.scalar_tensor_tensor(pr[:, j, :], bank(j), C ** -0.5, mask[:, j, :], ALU.mult, ALU.mult))
                step(nc.vector.tensor_tensor(pr[:, j, :], pr[:, j, :], negm[:, j, :], ALU.add))
                nc.vector.tensor_reduce(amax[:, j:j + 1], pr[:, j, :], AX, ALU.max, negate=True).then_inc(sc_shift, 1)
            dve.wait_ge(sc_exp, 2)
            step(nc.vector.reciprocal(asum[:, 0:TT], asum[:, 0:TT]))
            step(nc.vector.tensor_tensor(asum[:, 0:TT], asum[:, 0:TT], top[:, 0, :], ALU.mult))
            for j in range(TT):
                dve.wait_ge(pt_full, j + 1)
                nc.vector.tensor_copy(pT[:, j, :], bank(2 + j)).then_inc(pt_ready, 1)
            dve.wait_ge(read_full, 1)
            for j in range(TT):
                last = nc.vector.scalar_tensor_tensor(x[:, j, :], bank(4 + j)[:, 0:C], asum[:, j:j + 1], x[:, j, :],
                                                      ALU.mult, ALU.add)
            last.then_inc(x_ready, 1)
            norm(4)
            nc.vector.tensor_copy(hT, bank(6, CT, T)).then_inc(hT_ready, 1)
            cos, sin = const("cos"), const("sin")
            for i in range(5):
                dve.wait_ge(qkv_full, i + 1)
                o = bank(i, 2, T)
                q1, q2 = (qr[:, i, :], qt2[:, i, :]) if i < 4 else (kr, kt2)
                nc.vector.tensor_tensor(q1, o[:, 0, :], cos, ALU.mult)
                last = nc.vector.tensor_tensor(q2, o[:, 1, :], sin, ALU.mult)
            step(last)
            nc.vector.tensor_tensor(kr, kr, kt2, ALU.add)
            nc.vector.tensor_tensor(qr, qr, qt2, ALU.add).then_inc(rot_ready, 1)
            dve.wait_ge(rsc_full, 1)
            src = PS[:, 0:2048].rearrange("p (g q) -> p g q", g=4)[:, :, 0:256]
            step(nc.vector.transpose(rs_.rearrange("p (g a) q -> p g (a q)", g=4), src))
            step(nc.vector.tensor_reduce(amax, rs_, AX, ALU.max))
            nc.vector.tensor_tensor(rs_, rs_, amax.unsqueeze(2).broadcast_to([128, 32, 32]), ALU.subtract)\
                .then_inc(rsc_shift, 1)
            dve.wait_ge(rsc_exp, 1)
            step(nc.vector.tensor_reduce(asum, rs_, AX, ALU.add))
            step(nc.vector.reciprocal(asum, asum))
            step(nc.vector.tensor_tensor(rp_, rs_, asum.unsqueeze(2).broadcast_to([128, 32, 32]), ALU.mult))
            nc.vector.transpose(rs_, rp_).then_inc(rp_ready, 1)
            dve.wait_ge(rmix_full, 1)
            for b4 in range(4):
                src = bank(4 + b4, TT, 4, S)
                dst = oT.rearrange("p a (j q) -> p j a q", j=TT)[:, :, :, 32 * b4:32 * b4 + 32]
                for j in range(TT):
                    last = nc.vector.tensor_copy(dst[:, j], src[:, j])
            last.then_inc(oT_ready, 1)
            dve.wait_ge(wo_full, 1)
            nc.vector.tensor_tensor(x, x, bank(0, TT, C), ALU.add).then_inc(x_ready, 1)
            norm(5)
            nc.vector.tensor_copy(hT, bank(6, CT, T)).then_inc(hT_ready, 1)
            for i in range(IT // 2):
                dve.wait_ge(ffn_silu, i + 1)
                dve.wait_ge(ffn_full, 2 * i + 2)
                nc.vector.tensor_tensor(hm[:, 2 * i:2 * i + 2, :], sgf[:, 2 * i:2 * i + 2, :], bank(2 * i + 1, 2, T),
                                        ALU.mult).then_inc(ffn_ready, 1)
            dve.wait_ge(ffn_out, 1)
            nc.vector.tensor_tensor(x, x, bank(7, TT, C), ALU.add).then_inc(x_ready, 1)

        block = ctx.enter_context(nc.Block())

        @block.sync
        def _(sp):
            sp.dma_start(consts, io["consts"]).then_inc(ld_const, 16)
            sp.dma_start(vec, io["vectors"]).then_inc(ld_const, 16)
            sp.dma_start(x, io["x"]).then_inc(ld_x, 16)
            sp.dma_start(wkn, io["wk_nat"]).then_inc(ld_wkn, 16)
            for n in range(2):
                sp.dma_start(wch[n], io["chunks"][n]).then_inc(ld_chunk[n], 16)
            sp.dma_start(wkT, io["wkT"]).then_inc(ld_wkT, 16)
            for n in range(2, NCH):
                sp.wait_ge(proj_full, 4 * (n - 1))
                sp.dma_start(wch[n % 2], io["chunks"][n]).then_inc(ld_chunk[n % 2], 16)
                if n == 3:
                    for b in range(2):
                        sp.dma_start(ctxT[b], io["ctxT"][b]).then_inc(ld_ctxT[b], 16)
                        sp.dma_start(keysr[b], io["ctx"][b]).then_inc(ld_ctx[b], 16)
                    sp.dma_start(wvT, io["wvT"]).then_inc(ld_wvT, 16)
            sp.wait_ge(proj_full, 4 * NCH)
            sp.dma_start(wpc, io["wproj"][:, 0:NH, :]).then_inc(ld_wpc, 16)
            sp.wait_ge(front_over, 4)
            sp.dma_start(idx_raw, io["idx"][:, 0:2, :]).then_inc(ld_idx[0], 16)
            sp.dma_start(idx_raw2, io["idx"][:, 2, :]).then_inc(ld_idx[1], 16)
            sp.dma_start(wpx, io["wproj"][:, NH:2 * NH, :]).then_inc(ld_wpx, 16)

            def load_ctxT(b, k):
                sp.wait_ge(st_full, 4 * b - 4)
                sp.dma_start(ctxT[k], io["ctxT"][DS(b, 1)].rearrange("o p c n -> (o p) c n")).then_inc(ld_ctxT[k], 16)

            def load_ctx(b, k):
                sp.wait_ge(pctx, 2 * b - 2)
                sp.dma_start(keysr[k], io["ctx"][DS(b, 1)].rearrange("o p c n -> (o p) c n")).then_inc(ld_ctx[k], 16)

            load_ctxT(2, 0)
            with sp.Fori(1, 3) as i:
                load_ctxT(2 * i + 1, 1)
                load_ctx(2 * i, 0)
                load_ctxT(2 * i + 2, 0)
                load_ctx(2 * i + 1, 1)
            load_ctxT(7, 1)
            load_ctx(6, 0)
            load_ctx(7, 1)
            tail_sync(sp)

        @block.tensor
        def _(pe):
            def ring(name, i=0):
                u = RING_AT[name] + i
                if u >= 4:
                    who = RING_OWNER[u - 4]
                    pe.wait_ge(ring_read[who], RING_OWNER[:u - 3].count(who))
                return 4 + u % 4

            pe.wait_ge(ld_const, 32)
            pe.wait_ge(ld_wkn, 16)
            for i in range(4):
                nc.tensor.matmul(bank(ring("center", i)), const("center"), wkn[:, i * 512:(i + 1) * 512],
                                 start=True, stop=True).then_inc(ring_full, 1)
            pe.wait_ge(ln_done, 1)
            o = bank(ring("lnT"), CT, T)
            for i in range(4):
                j, c = i // CT, i % CT
                last = nc.tensor.transpose(o[:, c, j * 128:j * 128 + 128], raw[0][:, j, c * 128:c * 128 + 128], ident)
            last.then_inc(ring_full, 4)

            def project(n):
                pe.wait_ge(xs_ready, VARIANT[n] + 1)
                pe.wait_ge(ld_chunk[n % 2], 16 * (n // 2 + 1))
                for q in range(4):
                    j, hf = q // 2, q % 2
                    if n:
                        pe.wait_ge(proj_read, 4 * n - 3 + q)
                    for c in range(CT):
                        last = nc.tensor.matmul(bank(q), xs[:, VARIANT[n], c, j * 128:j * 128 + 128],
                                                wch[n % 2][:, c, hf * 512:hf * 512 + 512],
                                                start=c == 0, stop=c == CT - 1)
                    last.then_inc(proj_full, 1)

            def turn(n):
                pe.wait_ge(z_ready, ZORDER.index(n) + 1)
                for i in range(4):
                    o = bank(ring(f"turn{n}", i), 2, T)
                    for k in range(4):
                        hd, j = k // 2, k % 2
                        c0 = (2 * i + hd) * 128
                        last = nc.tensor.transpose(o[:, hd, j * 128:j * 128 + 128],
                                                   raw[RAW_SLOT[n]][:, j, c0:c0 + 128], ident)
                    last.then_inc(ring_full, 1)

            def cross_queries(n):
                done = RING_OWNER[:RING_AT[f"turn{n}"] + 4].count("dve")
                pe.wait_ge(ring_read["dve"], done)
                pe.wait_ge(bk_ready, 1)
                for i in range(4):
                    nc.tensor.matmul(bank(ring(f"beta{n}", i)), bk, zlnT[:, 2 * i:2 * i + 2, :],
                                     start=True, stop=True).then_inc(ring_full, 1)
                for i in range(8):
                    g, c = i // CT, i % CT
                    nc.tensor.matmul(bank(ring(f"A{n}", i)), wkc[:, 4 * n + g, c * 128:c * 128 + 128],
                                     uT[:, 2 * g:2 * g + 2, :], start=True, stop=True).then_inc(ring_full, 1)

            def attend(n):
                first = n == 4
                pe.wait_ge(ring_read["dve"], RING_OWNER[:RING_AT[f"turn{n}"] + 4].count("dve"))
                for i in range(4):
                    g = i if first else 4 + i
                    o = bank(ring(f"scores{n}", i), TT, 256)
                    for j in range(TT):
                        last = nc.tensor.matmul(o[:, j, :], kT[:, g, j * 128:j * 128 + 128],
                                                zlnT[:, 2 * i:2 * i + 2, j * 128:j * 128 + 128],
                                                start=True, stop=True)
                    last.then_inc(ring_full, 1)
                pe.wait_ge(pbd_ready, 1 if first else 2)
                pe.wait_ge(proj_read, 16)
                for i in range(4):
                    g = i if first else 4 + i
                    o = bank(ring(f"mix{n}", i), HPG, T)
                    for j in range(TT):
                        last = nc.tensor.matmul(o[:, :, j * 128:j * 128 + 128], v[:, j, g * D:(g + 1) * D],
                                                pbd[:, 2 * i + j, :, :], start=True, stop=True)
                    last.then_inc(ring_full, 1)

            project(0)
            project(1)
            turn(0)
            cross_queries(0)
            project(2)
            turn(1)
            cross_queries(1)
            project(3)
            turn(2)
            project(4)
            project(5)
            turn(4)
            attend(4)
            turn(5)
            attend(5)
            pe.wait_ge(ld_wpc, 16)
            pe.wait_ge(catc_ready, 4)
            o = bank(ring("core"), TT, C)
            for j in range(TT):
                for i in range(NH):
                    last = nc.tensor.matmul(o[:, j, :], catc[:, i, j * 128:j * 128 + 128], wpc[:, i, :],
                                            start=i == 0, stop=i == NH - 1)
            last.then_inc(ring_full, 1)
            nc.tensor.matmul(bank(0)[:, 0:128], ident, ident, start=True, stop=True).then_inc(front_over, 1)
            loop_pe(pe)
            tail_pe(pe)

        @block.scalar
        def _(act):
            step = Steps(act, act_step)
            nc.scalar.preload_act_table_set("natural_log_exp_and_others")

            def read_ring(name, i, dst, **kw):
                u = RING_AT[name] + i
                act.wait_ge(ring_full, u + 1)
                nc.scalar.activation(dst, bank(4 + u % 4, *dst.shape[1:]) if len(dst.shape) > 2 else bank(4 + u % 4),
                                     ACT.Copy, **kw).then_inc(ring_read["act"], 1)

            def read_chunk(n):
                for q in range(4):
                    j, hf = q // 2, q % 2
                    act.wait_ge(proj_full, 4 * n + q + 1)
                    if n == 1 and q == 0:
                        act.wait_ge(ring_full, 4)
                    if n == 2 and q == 0:
                        act.wait_ge(ring_full, RING_AT["turn0"] + 4)
                    if n == 4 and q == 0:
                        act.wait_ge(ring_full, RING_AT["turn1"] + 4)
                    if n == 5 and q == 0:
                        act.wait_ge(ring_full, RING_AT["turn2"] + 4)
                    dst = v if n == 3 else raw[RAW_SLOT[n]]
                    nc.scalar.activation(dst[:, j, hf * 512:hf * 512 + 512], bank(q), ACT.Copy,
                                         scale=col("w_scale", VARIANT[n])).then_inc(proj_read, 1)

            def cross_queries(n):
                for i in range(4):
                    read_ring(f"beta{n}", i, beta[:, 8 * n + 2 * i:8 * n + 2 * i + 2, :])
                for i in range(8):
                    g, c = i // CT, i % CT
                    read_ring(f"A{n}", i, A[:, c, 8 * n + 2 * g:8 * n + 2 * g + 2, :])

            act_rstd(act, step, TT, 0)
            act_rstd(act, step, TT, 1)
            for i in range(4):
                read_ring("center", i, wkc[:, 2 * i:2 * i + 2, :])
            read_chunk(0)
            act_rstd(act, step, NH, 2)
            read_chunk(1)
            cross_queries(0)
            act_rstd(act, step, NH, 3)
            read_chunk(2)
            cross_queries(1)
            act_rstd(act, step, NH, 4)
            read_chunk(3)
            read_chunk(4)
            act_rstd(act, step, NH, 5)
            read_chunk(5)
            for n in range(2):
                act.wait_ge(shifted_core, n + 1)
                nc.scalar.activation(at_p, at_s, ACT.Exp, scale=SCALE).then_inc(exp_core, 1)
                if n == 0:
                    act_rstd(act, step, NH, 6)
            read_ring("core", 0, core)
            nc.scalar.activation(nt[:, 31:32], nt[:, 0:1], ACT.Copy).then_inc(front_over, 1)
            act.wait_ge(ld_idx[0], 16)
            act.wait_ge(front_over, 4)
            nc.scalar.activation(idx[:, 0:2, :], idx_raw, ACT.Copy).then_inc(idx_ready, 1)
            act.wait_ge(ld_idx[1], 16)
            nc.scalar.activation(idx[:, 2, :], idx_raw2, ACT.Copy).then_inc(idx_ready, 1)
            loop_act(act, step)
            tail_act(act, step)

        @block.gpsimd
        def _(pool):
            step = Steps(pool, pool_step)
            nc.gpsimd.memset(nt[:, 30:31], 0.0).then_inc(front_over, 1)
            pool.wait_ge(front_over, 4)
            step(nc.gpsimd.memset(lutw, 0.0))
            loop_pool(pool, step)
            tail_pool(pool, step)

        @block.vector
        def _(dve):
            step = Steps(dve, dve_step)
            dve.wait_ge(ld_const, 32)
            step(nc.vector.reciprocal(inv_scale, vec[:, COL["in_scale"]]))
            step(nc.vector.reciprocal(inv_smooth, vec[:, COL["smooth"]]))
            nc.vector.tensor_copy(bk, col("kxln_b").broadcast_to([128, 128])).then_inc(bk_ready, 1)
            dve.wait_ge(ld_x, 16)
            h0 = raw[0][:, :, 0:C]
            step(token_norm(dve, step, x, h0, 0))
            token_norm(dve, step, h0, h0, 1).then_inc(ln_done, 1)
            dve.wait_ge(ring_full, RING_AT["lnT"] + 4)
            o = bank(4 + RING_AT["lnT"] % 4, CT, T)
            for c in range(CT):
                last = nc.vector.tensor_scalar(lnT[:, c, :], o[:, c, :], col("ln_w", c), col("ln_b", c),
                                               ALU.mult, ALU.add)
            last.then_inc(ring_read["dve"], 4)
            dve.wait_ge(ring_read["dve"], 4)
            for n in range(4):
                yv = y_bf[:, 0:CT * T].rearrange("p (c t) -> p c t", c=CT)
                for c in range(CT):
                    last = nc.vector.tensor_scalar(yv[:, c, :], lnT[:, c, :], inv_scale[:, n * CT + c:n * CT + c + 1],
                                                   FP8_MAX, ALU.mult, ALU.min)
                step(last)
                step(nc.vector.tensor_scalar(y_bf[:, 0:CT * T], y_bf[:, 0:CT * T], -FP8_MAX, None, ALU.max))
                step(round_fp8(step, CT * T, t_fp[:, 0:CT * T]))
                for c in range(CT):
                    last = nc.vector.tensor_scalar(xs[:, n, c, :], t_fp[:, c * T:(c + 1) * T],
                                                   col("in_scale", n * CT + c), None, ALU.mult)
                last.then_inc(xs_ready, 1)
            dve.wait_ge(xs_ready, 4)

            def norm_heads(n):
                dve.wait_ge(proj_read, 4 * n + 4)
                k = ZORDER.index(n)
                r = raw[RAW_SLOT[n]]
                heads = [r[:, j, i * D:(i + 1) * D] for j in range(TT) for i in range(8)]
                stats(dve, step, NH, heads, k + 2)
                for i, hd in enumerate(heads):
                    last = nc.vector.tensor_scalar(hd, hd, mv[:, i, 0:1], rs[:, i:i + 1], ALU.subtract, ALU.mult)
                last.then_inc(z_ready, 1)
                dve.wait_ge(z_ready, k + 1)

            def read_turn(n, dst, w, b):
                u0 = RING_AT[f"turn{n}"]
                for i in range(4):
                    dve.wait_ge(ring_full, u0 + i + 1)
                    nc.vector.tensor_scalar(dst[:, 2 * i:2 * i + 2, :], bank(4 + (u0 + i) % 4, 2, T), col(w), col(b),
                                            ALU.mult, ALU.add).then_inc(ring_read["dve"], 1)

            def read_turn_cross(n):
                u0 = RING_AT[f"turn{n}"]
                if n:
                    dve.wait_ge(ring_full, RING_AT[f"A{n - 1}"] + 8)
                for i in range(4):
                    dve.wait_ge(ring_full, u0 + i + 1)
                    step(nc.vector.tensor_scalar(zlnT[:, 2 * i:2 * i + 2, :], bank(4 + (u0 + i) % 4, 2, T),
                                                 col("qxln_w"), col("qxln_b"), ALU.mult, ALU.add))
                    nc.vector.tensor_scalar(uT[:, 2 * i:2 * i + 2, :], zlnT[:, 2 * i:2 * i + 2, :], col("kxln_w"),
                                            None, ALU.mult).then_inc(ring_read["dve"], 1)

            norm_heads(0)
            read_turn_cross(0)
            norm_heads(1)
            read_turn_cross(1)
            dve.wait_ge(ld_wkT, 16)
            heads = wkT.rearrange("p c (g d) -> p (c g) d", g=G)
            step(nc.vector.tensor_reduce(nt[:, 0:CT * G], heads, AX, ALU.add))
            step(nc.vector.tensor_scalar(nt[:, 0:CT * G], nt[:, 0:CT * G], 1.0 / D, None, ALU.mult))
            nc.vector.tensor_tensor(heads, heads, nt[:, 0:CT * G].unsqueeze(2).broadcast_to([128, CT * G, D]),
                                    ALU.subtract).then_inc(wk_centered, 1)
            norm_heads(2)
            read_turn(2, kT, "kln_w", "kln_b")
            dve.wait_ge(ring_full, RING_AT["A1"] + 8)
            step(nc.vector.memset(pbd, 0.0))
            for n in (4, 5):
                norm_heads(n)
                if n == 4:
                    dve.wait_ge(ring_full, RING_AT["beta1"] + 4)
                else:
                    dve.wait_ge(ring_full, RING_AT["scores4"] + 4)
                read_turn(n, zlnT, "qln_w", "qln_b")
                dve.wait_ge(ring_full, RING_AT[f"scores{n}"] + 4)
                sc = PS[:, 2048:4096].rearrange("p (a q) -> p a q", a=8)
                for b4 in range(4):
                    q0 = 32 * b4
                    src = sc[q0:q0 + 32].rearrange("p a (h q) -> p (a h) q", h=2)[:, :, q0:q0 + 32]
                    last = nc.vector.transpose(at_s[q0:q0 + 32], src)
                last.then_inc(ring_read["dve"], 4)
                dve.wait_ge(ring_read["dve"], RING_OWNER[:RING_AT[f"scores{n}"] + 4].count("dve"))
                step(nc.vector.tensor_reduce(amax[:, 0:16], at_s, AX, ALU.max))
                nc.vector.tensor_tensor(at_s, at_s, amax[:, 0:16].unsqueeze(2).broadcast_to([128, 16, 32]),
                                        ALU.subtract).then_inc(shifted_core, 1)
                dve.wait_ge(exp_core, n - 3)
                step(nc.vector.tensor_reduce(asum[:, 0:16], at_p, AX, ALU.add))
                step(nc.vector.reciprocal(asum[:, 0:16], asum[:, 0:16]))
                step(nc.vector.tensor_tensor(at_p, at_p, asum[:, 0:16].unsqueeze(2).broadcast_to([128, 16, 32]),
                                             ALU.mult))
                if n == 5:
                    dve.wait_ge(ring_full, RING_AT["mix4"] + 4)
                pb = pbd.rearrange("p a h q -> p (a h) q")
                for b4 in range(4):
                    q0 = 32 * b4
                    last = nc.vector.transpose(pb[q0:q0 + 32, :, q0:q0 + 32], at_p[q0:q0 + 32])
                last.then_inc(pbd_ready, 1)
                for i in range(2):
                    dve.wait_ge(ring_full, RING_AT[f"mix{n}"] + 2 * i + 2)
                    h0 = (n - 4) * 8 + 4 * i
                    src = PS[:, 2048 + 1024 * i:3072 + 1024 * i].rearrange("p (a t) -> p a t", a=4)
                    total = RING_OWNER[:RING_AT[f"mix{n}"] + 2 * i + 2].count("dve")
                    quantize(dve, step, src, inv_smooth[:, h0:h0 + 4], 4, T,
                             catc[:, h0:h0 + 4, :].rearrange("p a t -> p (a t)"),
                             (ring_read["dve"], 2, total)).then_inc(catc_ready, 1)
                    dve.wait_ge(catc_ready, 2 * (n - 4) + i + 1)
            nc.vector.memset(nt[:, 29:30], 0.0).then_inc(front_over, 1)
            loop_dve(dve, step)
            tail_dve(dve, step)


def kernel(**inputs):
    import numpy as np
    import concourse.bacc as bacc
    from concourse.bass_utils import run_bass_kernel_spmd

    a = {k: np.asarray(v) for k, v in inputs.items()}
    f32 = np.float32

    def tiles(w):
        return w.reshape(-1, 128, w.shape[-1]).transpose(1, 0, 2)

    def column(v, n):
        return np.asarray(v).reshape(n, 128).T

    X, M = "L0_xattn_", "L0_attn_"
    cols = [column(a[X + "ln_w"], CT), column(a[X + "ln_b"], CT)]
    cols += [column(a[X + n + "_in_scale"], CT) for n in ("qx", "k", "v", "q")]
    cols += [column(a[X + n], 1) for n in ("qln_w", "qln_b", "kln_w", "kln_b", "qxln_w", "qxln_b", "kxln_w", "kxln_b")]
    cols += [column(a[X + "proj_smooth"], 2 * NH)]
    cols += [tiles(a[M + "conv_w"][:, 0, :]).reshape(128, 8), column(a[M + "conv_b"], CT),
             column(a[M + "D"], CT)]
    for n in ("wqx_scale", "wk_scale", "wv_scale", "wq_scale", "proj_w_scale", "proj_in_scale"):
        cols += [np.broadcast_to(a[X + n].reshape(1, 1), (128, 1))]
    cols += [np.broadcast_to(a["L1_ffn_lut"].reshape(1, LUTN), (128, LUTN))]
    cols += [np.concatenate([a[M + "A_log"], np.zeros(64, f32)]).reshape(128, 1)]
    vectors = np.ascontiguousarray(np.concatenate(cols, 1))
    assert vectors.shape == (128, NVEC), vectors.shape

    d = np.arange(128) % 32
    inv = 1.0 / 10000.0 ** (np.arange(0, 8, 2, dtype=f32) / f32(8))
    ang = (np.arange(S, dtype=f32)[None, :] * np.where(d < 8, inv.astype(f32)[np.minimum(d // 2, 3)], 0)[:, None]).astype(f32)
    cos, sin = np.cos(ang), np.sin(ang)
    sin = sin * np.where(d % 2 == 0, -1.0, 1.0)[:, None]
    cos, sin = (np.broadcast_to(t[:, None, :], (128, B, S)).reshape(128, T) for t in (cos, sin))
    consts = np.ascontiguousarray(np.concatenate([
        np.eye(128), np.ones((128, 128)), np.eye(128) - 1.0 / D, cos, sin,
        np.broadcast_to(np.arange(LUTN)[None, :], (128, LUTN))], 1).astype(f32))

    chunks = [a[X + "wqx"][:1024], a[X + "wqx"][1024:], a[X + "wk"], a[X + "wv"], a[X + "wq"][:1024], a[X + "wq"][1024:]]
    wkv = a[X + "w_kv_x"]
    ctx = a["ctx_2048"]
    swap = np.array([1, 0, 3, 2, 5, 4, 7, 6] + list(range(8, 16)))

    def heads(w, n):
        w = w.reshape(C, 4, n, 16).transpose(0, 2, 1, 3)
        return w

    def padded(w):
        z = np.zeros(w.shape[:-1] + (32,), f32)
        z[..., :16] = w
        return z.reshape(C, -1)

    wq, wk, wv = heads(a["L1_attn_Wq"], 4), heads(a["L1_attn_Wk"], 1), heads(a["L1_attn_Wv"], 1)
    wo = np.zeros((4, 4, 32, C), f32)
    wo[:, :, :16] = a["L1_attn_Wo"].reshape(4, 4, 16, C).transpose(1, 0, 2, 3)
    pad = np.full((C, IPAD - INTER), LUTN, np.int32)
    idx = [np.concatenate([a["L1_ffn_gate_idx"].astype(np.int32).T, pad], 1),
           np.concatenate([a["L1_ffn_up_idx"].astype(np.int32).T, pad], 1),
           np.concatenate([a["L1_ffn_down_idx"].astype(np.int32).T, pad.T], 0)]
    idx = np.stack([tiles(t).reshape(128, CT * IPAD) for t in idx], 1)
    wx = a[M + "Wxproj"].T
    wx = np.concatenate([wx[:, :2 * SSM], np.broadcast_to(wx[:, 2 * SSM:], (C, SSM)), a[M + "Winproj"].T], 1)
    mask = a["mask_BxS2_bk0"].view(np.int32)
    arrays = {
        "consts": consts, "vectors": vectors, "x": tiles(a["x"].reshape(T, C)),
        "wk_nat": wkv[:1024].reshape(G, D, C).transpose(1, 0, 2).reshape(128, G * C),
        "chunks": np.stack([tiles(w.T) for w in chunks]),
        "wkT": tiles(wkv[:1024].T), "wvT": tiles(wkv[1024:].T), "wproj": tiles(a[X + "wproj"].T),
        "ctxT": ctx.reshape(B, NK, CT, 128).transpose(0, 3, 2, 1), "ctx": ctx.reshape(B, KT, 128, C).transpose(0, 2, 1, 3),
        "idx": idx, "ssm_in": tiles(wx), "ssm_out": a[M + "Woutproj"].T, "router": tiles(a["L0_ffn_Wr"]),
        "experts": np.stack([a["L0_ffn_" + n].reshape(NE, CT, 128, C).transpose(0, 2, 1, 3)
                             for n in ("Wg", "Wu", "Wd")], 2),
        "mask": mask,
        "wq_rot": np.stack([tiles(padded(wq)), tiles(padded(wq[..., swap]))], 1),
        "wk_rot": np.stack([tiles(padded(wk)), tiles(padded(wk[..., swap]))], 1),
        "wv_rot": tiles(padded(wv)), "wo_rot": wo.reshape(4, 128, C).transpose(1, 0, 2),
    }
    nc = bacc.Bacc("TRN2", target_bir_lowering=False, num_devices=1)
    io, sent = {}, {}
    for name, v in arrays.items():
        v = np.ascontiguousarray(v)
        sent["in_" + name] = v
        io[name] = nc.dram_tensor("in_" + name, v.shape, mybir.dt.from_np(v.dtype), kind="ExternalInput").ap()
    out = nc.dram_tensor("out_x", (128, TT, C), fp32, kind="ExternalOutput").ap()
    build(nc, io, out)
    r = run_bass_kernel_spmd(nc, [sent], core_ids=[0])
    return r.results[0]["out_x"].transpose(1, 0, 2).reshape(B, S, C)
```

```python
from contextlib import ExitStack

import concourse.bass as bass
from concourse import mybir

fp32 = mybir.dt.float32
bf16 = mybir.dt.bfloat16
u16 = mybir.dt.uint16
u8 = mybir.dt.uint8
i32 = mybir.dt.int32
ALU = mybir.AluOpType
ACT = mybir.ActivationFunctionType
AX = mybir.AxisListType.X
DS = bass.DynSlice

B, S, C, NK = 8, 32, 256, 512
T = B * S
TT, CT, KT = T // 128, C // 128, NK // 128
G, HPG, D = 8, 2, 128
NH = G * HPG
NCH = 6
VARIANT = [0, 0, 1, 2, 3, 3]
EPS = 1e-5
SSM = 64
NE = 8
INTER, IPAD = 688, 768
IT = IPAD // 128
LUTN = 16
NLUT = 3 * CT * IPAD
FP8_MAX = 448.0
ROUND = 1.5 * 2.0 ** 20
FP8_MIN_NORMAL = 2.0 ** -6

COL, _n = {}, 0
for _name, _w in [("ln_w", CT), ("ln_b", CT), ("in_scale", 4 * CT), ("qln_w", 1), ("qln_b", 1), ("kln_w", 1),
                  ("kln_b", 1), ("qxln_w", 1), ("qxln_b", 1), ("kxln_w", 1), ("kxln_b", 1), ("smooth", 2 * NH),
                  ("conv_w", 4 * CT), ("conv_b", CT), ("ssm_d", CT), ("w_scale", 4), ("proj_w_scale", 1),
                  ("proj_in_scale", 1), ("lut", LUTN), ("a_log", 1)]:
    COL[_name] = slice(_n, _n + _w)
    _n += _w
NVEC = _n

CONST, _n = {}, 0
for _name, _w in [("ident", 128), ("ones", 128), ("center", 128), ("cos", T), ("sin", T), ("iota", LUTN)]:
    CONST[_name] = slice(_n, _n + _w)
    _n += _w
NCONST = _n

FRONT, LOOP, TAIL, LATE = range(4)
WORDS = [
    ("consts", NCONST, FRONT, LATE), ("vec", NVEC, FRONT, LATE), ("small", 1152, FRONT, LATE),
    ("x", TT * C, FRONT, LATE), ("core", TT * C, FRONT, LATE), ("ctxT_ring", 2 * CT * NK, FRONT, LOOP),
    ("ctx_ring", 2 * KT * C, FRONT, LOOP), ("wkT", CT * G * D, FRONT, LOOP), ("wvT", CT * G * D, FRONT, LOOP),
    ("A", CT * NH * T, FRONT, LOOP), ("beta", NH * T, FRONT, LOOP), ("qtmp", 2560, FRONT, LOOP),
    ("lutw", NLUT, LOOP, LATE), ("wpx", NH * C, LOOP, TAIL), ("catx", NH * T, LOOP, TAIL),
    ("idx", NLUT // 4, LOOP, LOOP), ("luttmp", 2 * CT * IPAD, LOOP, LOOP),
    ("s", 2 * KT * NK, LOOP, LOOP), ("sq", 512, LOOP, LOOP), ("vecs", 6 * NK, LOOP, LOOP),
    ("px", CT * NH * 64, LOOP, LOOP),
    ("wch", 2 * CT * 1024, FRONT, FRONT), ("raw", 2 * TT * 1024, FRONT, FRONT), ("lnT", CT * T, FRONT, FRONT),
    ("xs", 4 * CT * T, FRONT, FRONT), ("zlnT", 8 * T, FRONT, FRONT), ("uT", 8 * T, FRONT, FRONT),
    ("kT", G * T, FRONT, FRONT), ("v", TT * 1024, FRONT, FRONT), ("wkc", G * C, FRONT, FRONT),
    ("attn", 1024, FRONT, FRONT), ("catc", NH * T, FRONT, FRONT),
    ("keysT", CT * B * NK, TAIL, LATE), ("keys", B * KT * C, TAIL, LATE), ("mask", 2 * TT * NK, TAIL, LATE),
    ("h", TT * C, TAIL, LATE), ("hT", CT * T, TAIL, LATE),
    ("ssm", 5200, TAIL, TAIL), ("maskraw", TT * NK // 4, TAIL, TAIL), ("gateup", 2 * 2 * CT * C, TAIL, TAIL),
    ("down", NE * CT * C, TAIL, TAIL), ("ffn", 2 * IT * T, LATE, LATE), ("moe", 2 * 2 * CT * T, TAIL, TAIL),
    ("rot", 2 * 2 * 512 + 2 * 2 * 128 + 2 * 128 + 4 * C, LATE, LATE), ("rotact", 4 * 1024, LATE, LATE),
    ("probs", 2 * TT * NK, LATE, LATE),
]


def place():
    at, done = {}, []
    for name, words, first, last in WORDS:
        words += -words % 8
        near = sorted((p, p + w) for p, w, a, z in done if a <= last and z >= first)
        spot = 0
        for p, q in near:
            if p - spot >= words:
                break
            spot = max(spot, q)
        at[name] = spot
        done.append((spot, words, first, last))
    return at, max(p + w for p, w, _, _ in done)



RING = [("center", 4, "act"), ("lnT", 4, "dve")]
for _n in (0, 1):
    RING += [(f"turn{_n}", 4, "act"), (f"beta{_n}", 4, "act"), (f"A{_n}", 8, "act")]
RING += [("turn2", 4, "act"), ("turn4", 4, "act"), ("scores4", 4, "dve"), ("mix4", 4, "act"), ("core", 1, "act")]
RING_AT, RING_OWNER = {}, []
for _name, _w, _who in RING:
    RING_AT[_name] = len(RING_OWNER)
    RING_OWNER += [_who] * _w


def reads(who, upto):
    return RING_OWNER[:upto].count(who)


ZORDER = [0, 1, 2, 4, 5]


def build(nc, io, out):
    ctx = ExitStack()
    with ctx:
        at, words = place()
        arena = ctx.enter_context(nc.sbuf_tensor("arena", [128, words], fp32))
        PS = ctx.enter_context(nc.psum_tensor("PS", [128, 4096], fp32))

        def sem(name):
            return ctx.enter_context(nc.semaphore(name))

        def buf(name, *dims, skip=0, dtype=fp32):
            n = 1
            for d in dims:
                n *= d
            wide = {fp32: 1, i32: 1, bf16: 2, u8: 4}[dtype]
            v = arena[:, at[name] + skip:at[name] + skip + -(-n // wide)]
            if dtype != fp32:
                v = v.bitcast(dtype)
            if len(dims) == 2:
                return v.rearrange("p (a b) -> p a b", a=dims[0])
            if len(dims) == 3:
                return v.rearrange("p (a b c) -> p a b c", a=dims[0], b=dims[1])
            return v

        def bank(n, *dims):
            v = PS[:, n * 512:(n + 1) * 512]
            if len(dims) == 2:
                return v[:, 0:dims[0] * dims[1]].rearrange("p (a b) -> p a b", a=dims[0])
            if len(dims) == 3:
                return v[:, 0:dims[0] * dims[1] * dims[2]].rearrange("p (a b c) -> p a b c", a=dims[0], b=dims[1])
            return v

        consts, vec = buf("consts", NCONST), buf("vec", NVEC)

        def const(name):
            return consts[:, CONST[name]]

        def col(name, i=0):
            return vec[:, COL[name].start + i:COL[name].start + i + 1]

        ident, ones = const("ident"), const("ones")
        _at = [0]

        def small(*dims):
            n = 1
            for d in dims:
                n *= d
            v = buf("small", *dims, skip=_at[0])
            _at[0] += n
            return v

        st, mv = small(NH, 6), small(NH, 2)
        var, rs0, rs, nt = small(32), small(32), small(32), small(32)
        inv_scale, inv_smooth = small(4 * CT), small(2 * NH)
        amax, asum = small(32), small(32)
        ssq, krs0 = small(2, G), small(2, G)
        kvar, krs, knt, eps = small(G), small(G), small(G), small(1)
        mcol = small(4)
        pscale = small(1)
        negA = small(1)
        nbias = small(NH)
        logit, eq, cand = small(TT, NE), small(TT, NE), small(TT, NE)
        oh = [small(TT, NE), small(TT, NE)]
        top, best, gate2, prob = small(2, TT), small(2, TT), small(2, TT), small(2, TT)
        mixw, mixt = small(TT, NE), small(TT, NE)
        iota8, wide = small(TT, NE), small(128)
        assert _at[0] <= 1152, _at

        x = buf("x", TT, C)
        core = buf("core", TT, C)
        h, hT = buf("h", TT, C), buf("hT", CT, T)

        ld_const, ld_x, ld_wkn, ld_wkT, ld_wvT = (sem(n) for n in ("ld_const", "ld_x", "ld_wkn", "ld_wkT", "ld_wvT"))
        ld_chunk = [sem("ld_chunk0"), sem("ld_chunk1")]
        ld_wpc, ld_wpx = sem("ld_wpc"), sem("ld_wpx")
        ld_idx = [sem("ld_idx0"), sem("ld_idx1"), sem("ld_idx2")]
        dve_step, act_step, pool_step = sem("dve_step"), sem("act_step"), sem("pool_step")
        ln_var, ln_rstd, ln_done = sem("ln_var"), sem("ln_rstd"), sem("ln_done")
        low_full, low_read = sem("low_full"), {"act": sem("low_read_act"), "dve": sem("low_read_dve")}
        u_ready = sem("u_ready")
        pbd_zero, z_act, deviations, y_core = (sem(n) for n in ("pbd_zero", "z_act", "deviations", "y_core"))
        xs_ready, wk_centered, bk_ready = sem("xs_ready"), sem("wk_centered"), sem("bk_ready")
        proj_full, proj_read = sem("proj_full"), sem("proj_read")
        z_ready = sem("z_ready")
        ring_full = sem("ring_full")
        ring_read = {"act": sem("ring_read_act"), "dve": sem("ring_read_dve")}
        shifted_core, exp_core, pbd_ready, catc_ready = (sem(n) for n in ("shifted_core", "exp_core", "pbd_ready",
                                                                          "catc_ready"))
        front_over, loop_over = sem("front_over"), sem("loop_over")
        ld_ctxT, ld_ctx = [sem("ld_ctxT0"), sem("ld_ctxT1")], [sem("ld_ctx0"), sem("ld_ctx1")]
        kx_full, sq_ready, krstd_ready = (sem(n) for n in ("kx_full", "sq_ready", "krstd_ready"))
        st_full, scaled, mx_ready, mxf_ready, tr_full, m_ready, diag_ready, mb_full = (sem(n) for n in (
            "st_full", "scaled", "mx_ready", "mxf_ready", "tr_full", "m_ready", "diag_ready", "mb_full"))
        shifted, p_ready, psum_ready, sum_full, r_ready, pctx, px_ready = (sem(n) for n in (
            "shifted", "p_ready", "psum_ready", "sum_full", "r_ready", "pctx", "px_ready"))
        v_full, v_read, catx_ready, proj_out = (sem(n) for n in ("v_full", "v_read", "catx_ready", "proj_out"))
        idx_ready, lut_term, lut_added = sem("idx_ready"), sem("lut_term"), sem("lut_added")

        class Steps:

            def __init__(self, eng, s):
                self.eng, self.s, self.base, self.k = eng, s, 0, 0

            def __call__(self, ins):
                ins.then_inc(self.s, 1)
                self.k += 1
                self.eng.wait_ge(self.s, self.base + self.k)

            def loop(self, i, first, per):
                self.start, self.per, self.first = self.base + self.k, per, first
                self.base, self.k = (i - first) * per + self.start, 0

            def over(self, turns):
                assert self.k == self.per, self.k
                self.base, self.k = self.start + turns * self.per, 0

        def newton(dve, step, r, r0, v, t):
            step(nc.vector.tensor_tensor(t, r0, r0, ALU.mult))
            step(nc.vector.scalar_tensor_tensor(t, t, -0.5, v, ALU.mult, ALU.mult))
            step(nc.vector.scalar_tensor_tensor(r, t, 1.5, r0, ALU.add, ALU.mult))

        def stats(dve, step, n, srcs, k):
            for i, src in enumerate(srcs):
                last = nc.vector.bn_stats(st[:, i, :], src)
            step(last)
            for i in range(n):
                last = nc.vector.bn_aggr(mv[:, i, :], st[:, i, :])
            step(last)
            nc.vector.tensor_scalar(var[:, 0:n], mv[:, 0:n, 1], EPS, None, ALU.add).then_inc(ln_var, 1)
            dve.wait_ge(ln_rstd, k + 1)
            newton(dve, step, rs[:, 0:n], rs0[:, 0:n], var[:, 0:n], nt[:, 0:n])

        def act_rstd(act, step, n, k):
            act.wait_ge(ln_var, k + 1)
            step(nc.scalar.activation(rs0[:, 0:n], var[:, 0:n], ACT.Ln))
            nc.scalar.activation(rs0[:, 0:n], rs0[:, 0:n], ACT.Exp, scale=-0.5).then_inc(ln_rstd, 1)

        def token_norm(dve, step, src, dst, k):
            stats(dve, step, TT, [src[:, j, :] for j in range(TT)], k)
            for j in range(TT):
                last = nc.vector.tensor_scalar(dst[:, j, :], src[:, j, :], mv[:, j, 0:1], rs[:, j:j + 1],
                                               ALU.subtract, ALU.mult)
            return last

        qt = buf("qtmp", 2560)
        y_bf = buf("qtmp", 1024, dtype=bf16)
        e_bf = buf("qtmp", 1024, skip=512, dtype=bf16)
        m_bf = buf("qtmp", 1024, skip=1024, dtype=bf16)
        t_fp = buf("qtmp", 1024, skip=1536)

        def round_fp8(step, n, dst):
            step(nc.vector.tensor_scalar(e_bf[:, 0:n].bitcast(u16), y_bf[:, 0:n].bitcast(u16), 0x7F80, None,
                                         ALU.bitwise_and))
            step(nc.vector.tensor_scalar(m_bf[:, 0:n], e_bf[:, 0:n], FP8_MIN_NORMAL, ROUND, ALU.max, ALU.mult))
            step(nc.vector.tensor_tensor(t_fp[:, 0:n], y_bf[:, 0:n], m_bf[:, 0:n], ALU.add))
            return nc.vector.tensor_tensor(dst, t_fp[:, 0:n], m_bf[:, 0:n], ALU.subtract)

        wkn = buf("raw", G * C, skip=2048)
        wkc = buf("wkc", G, C)
        wkT, wvT = buf("wkT", CT, G * D), buf("wvT", CT, G * D)
        wch = [buf("wch", CT, 1024), buf("wch", CT, 1024, skip=2048)]
        wpc = buf("wch", NH, C)
        raw = [buf("raw", TT, 1024), buf("raw", TT, 1024, skip=2048)]
        RAW_SLOT = {0: 0, 1: 1, 2: 0, 4: 1, 5: 0}
        lnT, xs = buf("lnT", CT, T), buf("xs", 4, CT, T)
        zlnT, uT, kT, v = buf("zlnT", 8, T), buf("uT", 8, T), buf("kT", G, T), buf("v", TT, 1024)
        zq = [zlnT, buf("xs", 8, T)]
        pbd = [buf("uT", 8, 2, 128), buf("raw", 8, 2, 128)]
        at_s = [buf("attn", 16, 32), buf("raw", 16, 32, skip=2048)]
        at_p = [buf("attn", 16, 32, skip=512), buf("raw", 16, 32, skip=2048 + 512)]
        y_all = [buf("zlnT", 8, T, dtype=bf16), buf("zlnT", 8, T, skip=1024, dtype=bf16)]
        bk = wide
        catc = buf("catc", NH, T)
        A, beta = buf("A", CT, NH, T), buf("beta", NH, T)

        ctxT = [buf("ctxT_ring", CT, NK), buf("ctxT_ring", CT, NK, skip=CT * NK)]
        keysr = [buf("ctx_ring", KT, C), buf("ctx_ring", KT, C, skip=KT * C)]
        sS = [buf("s", KT, NK), buf("s", KT, NK, skip=KT * NK)]
        sq = buf("sq", 1024, dtype=bf16)
        mx, nm, R = buf("vecs", 512), buf("vecs", 512, skip=512), buf("vecs", 512, skip=1536)
        diag = buf("vecs", 4, 128, skip=1024)
        ps2 = buf("vecs", 2, 512, skip=2048)
        px = buf("px", CT, NH, 64)
        catx = buf("catx", NH, T)
        idx = buf("idx", 3, CT * IPAD, dtype=u8)
        lutt = [buf("luttmp", CT * IPAD), buf("luttmp", CT * IPAD, skip=CT * IPAD)]
        idx_raw = buf("luttmp", 2, CT * IPAD, dtype=i32)
        lutw = buf("lutw", 3, CT * IPAD)
        wpx = buf("wpx", NH, C)
        SCALE = D ** -0.5

        def loop_pe(pe):
            def step(b, k, pair=None, prev=True):
                pe.wait_ge(ld_ctxT[k], 8 * (b - k) + 16)
                for t in range(KT):
                    n = 4 * b + t
                    for hf in range(2):
                        if not (prev is False and t == 0):
                            pe.wait_ge(sq_ready, 2 * n + hf - 1)
                        for c in range(CT):
                            last = nc.tensor.matmul(bank(hf), ctxT[k][:, c, t * 128:t * 128 + 128],
                                                    wkT[:, c, hf * 512:hf * 512 + 512],
                                                    start=c == 0, stop=c == CT - 1)
                        last.then_inc(kx_full, 1)
                    if not (prev is False and t < 2):
                        pe.wait_ge(scaled, n - 1)
                    for c in range(CT):
                        last = nc.tensor.matmul(bank(2 + t % 2), ctxT[k][:, c, t * 128:t * 128 + 128],
                                                A[:, c, :, DS(b * S, S)], start=c == 0, stop=c == CT - 1)
                    last.then_inc(st_full, 1)
                    if prev and t == 0:
                        maxima(b - 1)
                        if pair is not None:
                            values(pair, 0)
                    if prev and t == 1:
                        spread(b - 1)
                    if pair is not None and t == 2:
                        values(pair, 1)
                if prev:
                    mix(b - 1, 1 - k)

            def maxima(b):
                pe.wait_ge(mxf_ready, b + 1)
                if not (isinstance(b, int) and b == 0):
                    pe.wait_ge(px_ready, 2 * b)
                for j in range(4):
                    last = nc.tensor.transpose(bank(4, 4, 128)[:, j, :], mx[:, j * 128:j * 128 + 128], ident)
                last.then_inc(tr_full, 1)

            def spread(b):
                pe.wait_ge(diag_ready, b + 1)
                nc.tensor.matmul(bank(4), ones, diag.rearrange("p a q -> p (a q)"), start=True,
                                 stop=True).then_inc(mb_full, 1)

            def mix(b, k):
                pe.wait_ge(p_ready, b + 1)
                pe.wait_ge(ld_ctx[k], 8 * (b - k) + 16)
                for c in range(CT):
                    for t in range(KT):
                        last = nc.tensor.matmul(bank(5 + c), keysr[k][:, t, c * 128:c * 128 + 128], sS[k][:, t, :],
                                                start=t == 0, stop=t == KT - 1)
                    last.then_inc(pctx, 1)
                pe.wait_ge(psum_ready, b + 1)
                nc.tensor.matmul(bank(4), ones, ps2[:, 0, :], start=True, stop=True).then_inc(sum_full, 1)

            def project_out(j, heads, after):
                pe.wait_ge(catx_ready, after)
                for i in heads:
                    last = nc.tensor.matmul(bank(j)[:, 0:C], catx[:, i, j * 128:j * 128 + 128], wpx[:, i, :],
                                            start=i == 0, stop=i == NH - 1)
                if i == NH - 1:
                    last.then_inc(proj_out, 1)

            def values(p, hf):
                if hf == 0:
                    pe.wait_ge(px_ready, 4 * p + 4)
                pe.wait_ge(v_read, 2 * p + hf + 1)
                for g in range(4 * hf, 4 * hf + 4):
                    for c in range(CT):
                        last = nc.tensor.matmul(bank(7)[:, (g % 4) * 128:(g % 4 + 1) * 128],
                                                wvT[:, c, g * D:(g + 1) * D], px[:, c, 2 * g:2 * g + 2, :],
                                                start=c == 0, stop=c == CT - 1)
                last.then_inc(v_full, 1)

            pe.wait_ge(wk_centered, 1)
            pe.wait_ge(ld_wvT, 16)
            step(0, 0, prev=False)
            step(1, 1)
            with pe.Fori(1, 4) as i:
                step(2 * i, 0)
                step(2 * i + 1, 1, pair=i - 1)
            pe.wait_ge(ld_wpx, 16)
            pe.wait_ge(sq_ready, 8 * B)
            project_out(0, range(8), 4)
            maxima(7)
            project_out(0, range(8, 12), 4)
            spread(7)
            project_out(0, range(12, NH), 4)
            mix(7, 1)
            values(3, 0)
            values(3, 1)
            project_out(1, range(8), 7)
            project_out(1, range(8, NH), 8)

        def loop_act(act, self_step):
            def step(b, k, prev=True):
                for t in range(KT):
                    n = 4 * b + t
                    k2 = t % 2
                    if not (prev is False and t < 2):
                        act.wait_ge(scaled, n - 1)
                    for hf in range(2):
                        act.wait_ge(kx_full, 2 * n + hf + 1)
                        if not (prev is False and t == 0):
                            act.wait_ge(sq_ready, 2 * n + hf - 1)
                        for g in range(4):
                            last = nc.scalar.activation(sq[:, (4 * hf + g) * D:(4 * hf + g + 1) * D], bank(hf)[:, g * D:(g + 1) * D], ACT.Square,
                                                        accum_out=ssq[:, k2, 4 * hf + g:4 * hf + g + 1])
                        last.then_inc(sq_ready, 1)
                        if prev and t == 1 and hf == 0:
                            spread_rows(b - 1)
                    act.wait_ge(sq_ready, 2 * n + 2)
                    self_step(nc.scalar.activation(krs0[:, k2, :], ssq[:, k2, :], ACT.Ln, scale=1.0 / D, bias=eps))
                    nc.scalar.activation(krs0[:, k2, :], krs0[:, k2, :], ACT.Exp, scale=-0.5)\
                        .then_inc(krstd_ready, 1)
                    if prev and t == 2:
                        exponentials(b - 1, 1 - k)
                if prev:
                    inverse(b - 1)

            def spread_rows(b):
                act.wait_ge(m_ready, b + 1)
                for j in range(4):
                    last = nc.scalar.activation(diag[:, j, :], ident, ACT.Copy, scale=mcol[:, j:j + 1])
                last.then_inc(diag_ready, 1)

            def exponentials(b, k):
                act.wait_ge(shifted, b + 1)
                nc.scalar.activation(sS[k], sS[k], ACT.Exp, scale=SCALE).then_inc(p_ready, 1)

            def inverse(b):
                act.wait_ge(sum_full, b + 1)
                self_step(nc.scalar.activation(R, bank(4), ACT.Ln))
                nc.scalar.activation(R, R, ACT.Exp, scale=-1.0).then_inc(r_ready, 1)

            step(0, 0, prev=False)
            step(1, 1)
            with act.Fori(1, 4) as i:
                self_step.loop(i, 1, 10)
                step(2 * i, 0)
                step(2 * i + 1, 1)
                self_step.over(3)
            spread_rows(7)
            exponentials(7, 1)
            inverse(7)
            nc.scalar.activation(nt[:, 31:32], nt[:, 0:1], ACT.Copy).then_inc(loop_over, 1)

        LUT_STEP = 6

        def loop_pool(pool, self_step):
            for m in range(3):
                pool.wait_ge(ld_idx[m], 16)
                nc.gpsimd.tensor_copy(idx[:, m, :], idx_raw[:, m % 2, :]).then_inc(idx_ready, 1)
            nc.gpsimd.memset(lutw, 0.0).then_inc(lut_added, 1)

            def add(b, which):
                for q in which:
                    n = LUT_STEP * (b - 1) + q
                    pool.wait_ge(lut_term, n + 1)
                    if not (isinstance(b, int) and n == 0) and q < 3:
                        pool.wait_ge(lut_added, n - 1)
                    nc.gpsimd.tensor_tensor(lutw[:, q % 3, :], lutw[:, q % 3, :], lutt[q % 2], ALU.add)\
                        .then_inc(lut_added, 1)

            def sums(b, k):
                pool.wait_ge(p_ready, b + 1)
                if not (isinstance(b, int) and b == 0):
                    pool.wait_ge(sum_full, b)
                self_step(nc.gpsimd.tensor_tensor(ps2, sS[k][:, 0:2, :], sS[k][:, 2:4, :], ALU.add))
                nc.gpsimd.tensor_tensor(ps2[:, 0, :], ps2[:, 0, :], ps2[:, 1, :], ALU.add).then_inc(psum_ready, 1)

            def step(b, k):
                add(b, range(0, 3))
                sums(b - 1, 1 - k)
                add(b, range(3, LUT_STEP))

            pool.wait_ge(lut_added, 1)
            step(1, 1)
            with pool.Fori(1, 4) as i:
                self_step.loop(i, 1, 2)
                step(2 * i, 0)
                step(2 * i + 1, 1)
                self_step.over(3)
            add(8, range(0, 2))
            sums(7, 1)
            add(8, range(2, LUT_STEP))
            self_step(nc.gpsimd.memset(nt[:, 30:31], 0.0))
            nc.gpsimd.memset(nt[:, 30:31], 0.0).then_inc(loop_over, 1)

        def loop_dve(dve, self_step):
            def step(b, k, pair=None, prev=True):
                for t in range(KT):
                    n = 4 * b + t
                    dve.wait_ge(sq_ready, 2 * n + 2)
                    self_step(nc.vector.tensor_scalar(kvar, ssq[:, t % 2, :], 1.0 / D, EPS, ALU.mult, ALU.add))
                    dve.wait_ge(krstd_ready, n + 1)
                    newton(dve, self_step, krs, krs0[:, t % 2, :], kvar, knt)
                    dve.wait_ge(st_full, n + 1)
                    if t == 0 and prev and not (isinstance(b, int) and b < 2):
                        dve.wait_ge(pctx, 2 * b - 2)
                    nc.vector.tensor_tensor(sS[k][:, t, :].rearrange("p (g q) -> p g q", g=G), bank(2 + t % 2, G, 64),
                                            krs.unsqueeze(2).broadcast_to([128, G, 64]), ALU.mult)\
                        .then_inc(scaled, 1)
                    if prev and t == 0:
                        maxima(b - 1)
                    if prev and t == 1:
                        shift(b - 1, 1 - k)
                    if pair is not None and t == 1:
                        quantize_values(pair, 0)
                    if pair is not None and t == 3:
                        quantize_values(pair, 1)
                    if prev:
                        terms(b, range(t, t + 1))
                dve.wait_ge(scaled, 4 * b + 4)
                if prev:
                    dve.wait_ge(tr_full, b)
                nc.vector.tensor_reduce(mx, sS[k].rearrange("p t q -> p q t"), AX, ALU.max).then_inc(mx_ready, 1)
                dve.wait_ge(mx_ready, b + 1)
                nc.vector.tensor_tensor(mx, mx, beta[:, :, DS(b * S, S)], ALU.add).then_inc(mxf_ready, 1)
                if prev:
                    terms(b, range(4, 5))
                if prev:
                    normalise(b - 1, 1 - k)
                if prev:
                    terms(b, range(5, LUT_STEP))

            def terms(b, which):
                for q in which:
                    n = LUT_STEP * (b - 1) + q
                    if isinstance(b, int) and n < 2:
                        dve.wait_ge(lut_added, 1)
                    else:
                        dve.wait_ge(lut_added, n)
                    jc, jl = (CONST["iota"].start + q // 3 - 2), (COL["lut"].start + q // 3 - 2)
                    nc.vector.tensor_scalar(lutt[q % 2], idx[:, q % 3, :], consts[:, DS(2 * b + jc, 1)],
                                            vec[:, DS(2 * b + jl, 1)], ALU.is_equal, ALU.mult).then_inc(lut_term, 1)

            def maxima(b):
                dve.wait_ge(tr_full, b + 1)
                nc.vector.tensor_reduce(mcol, bank(4, 4, 128), AX, ALU.max).then_inc(m_ready, 1)

            def shift(b, k):
                dve.wait_ge(mb_full, b + 1)
                self_step(nc.vector.tensor_tensor(nm.rearrange("p (a q) -> p a q", a=NH), bank(4, NH, S),
                                                  beta[:, :, DS(b * S, S)], ALU.subtract))
                nc.vector.tensor_tensor(sS[k], sS[k], nm.unsqueeze(1).broadcast_to([128, KT, 512]), ALU.subtract)\
                    .then_inc(shifted, 1)

            def normalise(b, k):
                dve.wait_ge(r_ready, b + 1)
                self_step(nc.vector.scalar_tensor_tensor(nm, bank(4), -1.0, R, ALU.mult, ALU.mult))
                self_step(nc.vector.scalar_tensor_tensor(R, nm, 2.0, R, ALU.add, ALU.mult))
                dve.wait_ge(pctx, 2 * b + 2)
                if k == 0 and not (isinstance(b, int) and b == 0):
                    dve.wait_ge(v_full, b)
                for c in range(CT):
                    nc.vector.tensor_tensor(px[:, c, :, k * S:(k + 1) * S], bank(5 + c, NH, S),
                                            R.rearrange("p (a q) -> p a q", a=NH), ALU.mult).then_inc(px_ready, 1)

            def quantize_values(p, hf):
                dve.wait_ge(v_full, 2 * p + hf + 1)
                src = bank(7, 8, 64)
                heads = slice(8 * hf, 8 * hf + 8)
                y = y_bf[:, 0:512].rearrange("p (a q) -> p a q", a=8)
                nc.vector.tensor_tensor(y, src, inv_smooth[:, NH + 8 * hf:NH + 8 * hf + 8].unsqueeze(2)
                                        .broadcast_to([128, 8, 64]), ALU.mult).then_inc(v_read, 1)
                dve.wait_ge(v_read, 2 * p + hf + 2)
                self_step(nc.vector.tensor_scalar(y_bf[:, 0:512], y_bf[:, 0:512], FP8_MAX, -FP8_MAX, ALU.min, ALU.max))
                dst = catx[:, heads, DS(2 * S * p, 2 * S)]
                self_step(nc.vector.tensor_scalar(e_bf[:, 0:512].bitcast(u16), y_bf[:, 0:512].bitcast(u16), 0x7F80,
                                                  None, ALU.bitwise_and))
                self_step(nc.vector.tensor_scalar(m_bf[:, 0:512], e_bf[:, 0:512], FP8_MIN_NORMAL, ROUND, ALU.max,
                                                  ALU.mult))
                self_step(nc.vector.tensor_tensor(t_fp[:, 0:512], y_bf[:, 0:512], m_bf[:, 0:512], ALU.add))
                nc.vector.tensor_tensor(dst, t_fp[:, 0:512].rearrange("p (a q) -> p a q", a=8),
                                        m_bf[:, 0:512].rearrange("p (a q) -> p a q", a=8), ALU.subtract)\
                    .then_inc(catx_ready, 1)

            dve.wait_ge(front_over, 4)
            nc.vector.memset(nt[:, 29:30], 0.0).then_inc(v_read, 1)
            step(0, 0, prev=False)
            step(1, 1)
            with dve.Fori(1, 4) as i:
                self_step.loop(i, 1, 2 * (16 + 3) + 8)
                step(2 * i, 0)
                step(2 * i + 1, 1, pair=i - 1)
                self_step.over(3)
            self_step(nc.vector.tensor_tensor(pscale, col("proj_w_scale"), col("proj_in_scale"), ALU.mult))
            self_step(nc.vector.scalar_tensor_tensor(x, core, pscale, x, ALU.mult, ALU.add))
            maxima(7)
            terms(8, range(0, 2))
            shift(7, 1)
            terms(8, range(2, LUT_STEP))
            dve.wait_ge(proj_out, 1)
            nc.vector.scalar_tensor_tensor(x[:, 0, :], bank(0)[:, 0:C], pscale, x[:, 0, :], ALU.mult, ALU.add)
            normalise(7, 1)
            quantize_values(3, 0)
            quantize_values(3, 1)
            dve.wait_ge(catx_ready, 8)
            nc.vector.memset(nt[:, 29:30], 0.0).then_inc(loop_over, 1)

        keysT_all, keys_all = buf("keysT", CT, B, NK), buf("keys", B, KT, C)
        o_ = [0]

        def ssm(*dims):
            n = 1
            for d in dims:
                n *= d
            view = buf("ssm", *dims, skip=o_[0])
            o_[0] += n
            return view

        w_ssm, w_ssmo = ssm(CT, 4 * SSM), ssm(C)[0:SSM, :]
        hpad, xc, diagD = ssm(CT, B, S + 3), ssm(CT, T), ssm(CT, 128)
        sx, sy, sz, su, sa = (ssm(T)[0:SSM, :] for _ in range(5))
        wr = ssm(CT, NE)
        assert o_[0] <= 5200, o_
        wgu = [buf("gateup", 2, CT * C, skip=2 * k * CT * C) for k in range(2)]
        wdn = buf("down", NE, CT * C)
        sg = [buf("moe", CT * T, skip=2 * k * CT * T) for k in range(2)]
        am = [buf("moe", CT, T, skip=(2 * k + 1) * CT * T) for k in range(2)]
        mask = buf("mask", TT, NK)
        negm = buf("mask", TT, NK, skip=TT * NK)
        mask_u8 = buf("maskraw", TT, NK, dtype=u8)
        mask_raw = buf("maskraw", TT, NK // 4, dtype=i32)
        pr = buf("probs", TT, NK)
        pT = buf("probs", TT, KT * 128, skip=TT * NK)
        r_ = [0]

        def rot(*dims):
            n = 1
            for d in dims:
                n *= d
            view = buf("rot", *dims, skip=r_[0])
            r_[0] += n
            return view

        wq_r, wk_r, wv_r, wo_r = rot(2 * CT, 512), rot(2 * CT, 128), rot(CT, 128), rot(4, C)
        qr, qt2 = buf("rotact", 4, T), buf("rotact", 4, T, skip=1024)
        kr, kt2 = buf("rotact", T, skip=2048), buf("rotact", T, skip=2304)
        vr = buf("rotact", TT, 128, skip=2560)
        rs_ = buf("probs", 32, 32)
        rp_ = buf("rotact", 32, 32, skip=3072)
        oT = buf("probs", 4, T, skip=1024)
        sgf, hm = buf("ffn", IT, T), buf("ffn", IT, T, skip=IT * T)
        ld_w = {n: sem("ld_" + n) for n in ("ssm", "keysT", "keys", "mask", "rot")}
        ld_e, ld_down = [sem("ld_experts0"), sem("ld_experts1")], sem("ld_down")
        x_ready, turned, hT_ready, diag_d, hpad_zero = (sem(n) for n in (
            "x_ready", "turned", "hT_ready", "diag_d", "hpad_zero"))
        ssm_p, conv_ready, ssm_x, soft_in, soft_out, decay, hm_ready, ssm_out_full = (sem(n) for n in (
            "ssm_p", "conv_ready", "ssm_x", "soft_in", "soft_out", "decay", "hm_ready", "ssm_out_full"))
        route_full, gap_ready, gap_exp, gu_full, silu_ready, act_ready, down_full, moe_added = (sem(n) for n in (
            "route_full", "gap_ready", "gap_exp", "gu_full", "silu_ready", "act_ready", "down_full", "moe_added"))
        mask_ready, sc_full, sc_shift, sc_exp, pt_full, pt_ready, read_full = (sem(n) for n in (
            "mask_ready", "sc_full", "sc_shift", "sc_exp", "pt_full", "pt_ready", "read_full"))
        qkv_full, rot_ready, v_ready, rsc_full, rsc_shift, rsc_exp, rp_ready, rmix_full, oT_ready, wo_full = (
            sem(n) for n in ("qkv_full", "rot_ready", "v_ready", "rsc_full", "rsc_shift", "rsc_exp", "rp_ready",
                             "rmix_full", "oT_ready", "wo_full"))
        ffn_full, ffn_silu, ffn_ready, ffn_out, stored = (sem(n) for n in (
            "ffn_full", "ffn_silu", "ffn_ready", "ffn_out", "stored"))
        XC = {"proj": 1, "ssm": 2, "moe": 3, "read": 4, "rot": 5, "ffn": 6}

        def tail_sync(sp):
            sp.wait_ge(loop_over, 3)
            sp.dma_start(w_ssm, io["ssm_in"]).then_inc(ld_w["ssm"], 16)
            sp.dma_start(w_ssmo, io["ssm_out"]).then_inc(ld_w["ssm"], 16)
            sp.dma_start(wr, io["router"]).then_inc(ld_w["ssm"], 16)
            for k in range(2):
                sp.dma_start(wgu[k], io["gate_up"][k]).then_inc(ld_e[k], 16)
            for j in range(TT):
                for b4 in range(4):
                    sp.dma_start(mask_raw[32 * b4:32 * b4 + 32, j, :],
                                 io["mask"][4 * j + b4:4 * j + b4 + 1, :].broadcast_to([32, NK // 4])).then_inc(ld_w["mask"], 16)
            sp.dma_start(wdn, io["down"]).then_inc(ld_down, 16)
            for b in range(B):
                sp.dma_start(keysT_all[:, :, b, :], io["ctxT"][b]).then_inc(ld_w["keysT"], 16)
            for b in range(B):
                sp.dma_start(keys_all[:, b, :, :], io["ctx"][b]).then_inc(ld_w["keys"], 16)

            def load_expert(e, k):
                sp.wait_ge(gu_full, 2 * e - 2)
                sp.dma_start(wgu[k], io["gate_up"][DS(e, 1)].rearrange("o p a n -> (o p) a n"))\
                    .then_inc(ld_e[k], 16)

            with sp.Fori(1, 4) as i:
                load_expert(2 * i, 0)
                load_expert(2 * i + 1, 1)
            sp.wait_ge(x_ready, XC["moe"])
            sp.dma_start(wq_r.rearrange("p (a c) n -> p a c n", a=2), io["wq_rot"]).then_inc(ld_w["rot"], 16)
            sp.dma_start(wk_r.rearrange("p (a c) n -> p a c n", a=2), io["wk_rot"]).then_inc(ld_w["rot"], 16)
            sp.dma_start(wv_r, io["wv_rot"]).then_inc(ld_w["rot"], 16)
            sp.dma_start(wo_r, io["wo_rot"]).then_inc(ld_w["rot"], 16)
            sp.wait_ge(x_ready, XC["ffn"])
            sp.dma_start(out, x).then_inc(stored, 16)
            sp.wait_ge(stored, 16)

        def tail_pe(pe):
            def turn_norm(k, nb):
                pe.wait_ge(ln_done, k + 1)
                o = bank(nb, CT, T)
                for i in range(4):
                    j, c = i // CT, i % CT
                    last = nc.tensor.transpose(o[:, c, j * 128:j * 128 + 128], h[:, j, c * 128:c * 128 + 128], ident)
                last.then_inc(turned, 1)

            turn_norm(1, 1)
            pe.wait_ge(ld_w["ssm"], 48)
            pe.wait_ge(hT_ready, 1)
            for i in range(3):
                o = bank(2 + i // 2)[0:SSM, (i % 2) * T:(i % 2) * T + T]
                for c in range(CT):
                    last = nc.tensor.matmul(o, w_ssm[:, c, i * SSM:(i + 1) * SSM], hpad[:, c, :, 3:S + 3],
                                            start=c == 0, stop=c == CT - 1)
            last.then_inc(ssm_p, 1)
            pe.wait_ge(conv_ready, 1)
            for c in range(CT):
                last = nc.tensor.matmul(bank(4)[0:SSM, 0:T], w_ssm[:, c, 3 * SSM:4 * SSM], xc[:, c, :],
                                        start=c == 0, stop=c == CT - 1)
            last.then_inc(ssm_x, 1)
            pe.wait_ge(diag_d, 1)
            pe.wait_ge(hm_ready, 1)
            o = bank(5, TT, C)
            for j in range(TT):
                nc.tensor.matmul(o[:, j, :], sz[:, j * 128:j * 128 + 128], w_ssmo, start=True, stop=False,
                                 skip_group_check=True)
                for c in range(CT):
                    last = nc.tensor.matmul(o[:, j, c * 128:c * 128 + 128], xc[:, c, j * 128:j * 128 + 128],
                                            diagD[:, c, :], start=False, stop=c == CT - 1, skip_group_check=True)
            last.then_inc(ssm_out_full, 1)
            turn_norm(2, 6)
            pe.wait_ge(hT_ready, 2)
            o = bank(7, TT, NE)
            for j in range(TT):
                for c in range(CT):
                    last = nc.tensor.matmul(o[:, j, :], hT[:, c, j * 128:j * 128 + 128], wr[:, c, :],
                                            start=c == 0, stop=c == CT - 1)
            last.then_inc(route_full, 1)

            def gate_up(e, k):
                pe.wait_ge(ld_e[k], 8 * (e - k) + 16)
                if not (isinstance(e, int) and e < 2):
                    pe.wait_ge(act_ready, e - 1)
                for i in range(2):
                    o = bank(2 * k + i, CT, T)
                    for m in range(CT):
                        for c in range(CT):
                            w0 = c * C + m * 128
                            last = nc.tensor.matmul(o[:, m, :], wgu[k][:, i, w0:w0 + 128], hT[:, c, :],
                                                    start=c == 0, stop=c == CT - 1)
                    last.then_inc(gu_full, 1)

            def down(e, k):
                pe.wait_ge(act_ready, e + 1)
                if not (isinstance(e, int) and e == 0):
                    pe.wait_ge(moe_added, e)
                o = bank(4 + k, TT, C)
                for j in range(TT):
                    for m in range(CT):
                        last = nc.tensor.matmul(o[:, j, :], am[k][:, m, j * 128:j * 128 + 128],
                                                wdn[:, DS(e, 1), m * C:(m + 1) * C] if not isinstance(e, int) else
                                                wdn[:, e, m * C:(m + 1) * C],
                                                start=m == 0, stop=m == CT - 1)
                last.then_inc(down_full, 1)

            gate_up(0, 0)
            gate_up(1, 1)
            pe.wait_ge(ld_down, 16)
            down(0, 0)
            with pe.Fori(1, 4) as i:
                gate_up(2 * i, 0)
                down(2 * i - 1, 1)
                gate_up(2 * i + 1, 1)
                down(2 * i, 0)
            down(7, 1)
            turn_norm(3, 6)
            pe.wait_ge(hT_ready, 3)
            pe.wait_ge(ld_w["keysT"], 16 * B)
            for b in range(B):
                q0 = 32 * (b % 4)
                for c in range(CT):
                    last = nc.tensor.matmul(bank(b // 4)[q0:q0 + 32, :], hT[:, c, b * S:b * S + S], keysT_all[:, c, b, :],
                                            start=c == 0, stop=c == CT - 1)
                if b % 4 == 3:
                    last.then_inc(sc_full, 1)
            pe.wait_ge(ld_w["keys"], 16 * B)
            for b in range(B):
                j, q0 = b // 4, 32 * (b % 4)
                if q0 == 0:
                    pe.wait_ge(sc_exp, j + 1)
                    for t in range(KT):
                        last = nc.tensor.transpose(bank(2 + j, KT, 128)[:, t, :], pr[:, j, t * 128:t * 128 + 128],
                                                   ident)
                    last.then_inc(pt_full, 1)
                    pe.wait_ge(pt_ready, j + 1)
                for t in range(KT):
                    last = nc.tensor.matmul(bank(4 + j)[q0:q0 + 32, 0:C], pT[:, j, t * 128 + q0:t * 128 + q0 + 32],
                                            keys_all[:, b, t, :], start=t == 0, stop=t == KT - 1)
            last.then_inc(read_full, 1)
            turn_norm(4, 6)
            pe.wait_ge(hT_ready, 4)
            pe.wait_ge(ld_w["rot"], 64)
            for i in range(5):
                o = bank(i, 2, T)
                for sw in range(2):
                    for c in range(CT):
                        w = wq_r[:, sw * CT + c, i * 128:i * 128 + 128] if i < 4 else wk_r[:, sw * CT + c, :]
                        last = nc.tensor.matmul(o[:, sw, :], w, hT[:, c, :], start=c == 0, stop=c == CT - 1)
                last.then_inc(qkv_full, 1)
            o = bank(5, TT, 128)
            for j in range(TT):
                for c in range(CT):
                    last = nc.tensor.matmul(o[:, j, :], hT[:, c, j * 128:j * 128 + 128], wv_r[:, c, :],
                                            start=c == 0, stop=c == CT - 1)
            last.then_inc(qkv_full, 1)
            pe.wait_ge(rot_ready, 1)
            for g in range(4):
                for b in range(B):
                    q0 = 32 * (b % 4)
                    last = nc.tensor.matmul(bank(g)[q0:q0 + 32, (b // 4) * 128:(b // 4) * 128 + 128],
                                            kr[32 * g:32 * g + 32, b * S:b * S + S],
                                            qr[32 * g:32 * g + 32, :, b * S:b * S + S], start=True, stop=True)
            last.then_inc(rsc_full, 1)
            pe.wait_ge(rp_ready, 1)
            pe.wait_ge(v_ready, 1)
            rpv = rs_.rearrange("p (g j a) q -> p g j (a q)", g=4, j=TT)
            for b4 in range(4):
                q0 = 32 * b4
                for j in range(TT):
                    for g in range(4):
                        last = nc.tensor.matmul(bank(4 + b4)[32 * g:32 * g + 32, j * 128:j * 128 + 128],
                                                vr[q0:q0 + 32, j, 32 * g:32 * g + 32], rpv[q0:q0 + 32, g, j, :],
                                                start=True, stop=True)
            last.then_inc(rmix_full, 1)
            pe.wait_ge(oT_ready, 1)
            o = bank(0, TT, C)
            for j in range(TT):
                for a in range(4):
                    last = nc.tensor.matmul(o[:, j, :], oT[:, a, j * 128:j * 128 + 128], wo_r[:, a, :],
                                            start=a == 0, stop=a == 3)
            last.then_inc(wo_full, 1)
            turn_norm(5, 6)
            pe.wait_ge(hT_ready, 5)
            for i in range(IT // 2):
                for m in range(2):
                    o = bank(2 * i + m, 2, T)
                    for a in range(2):
                        for c in range(CT):
                            w0 = c * IPAD + (2 * i + a) * 128
                            last = nc.tensor.matmul(o[:, a, :], lutw[:, m, w0:w0 + 128], hT[:, c, :],
                                                    start=c == 0, stop=c == CT - 1)
                    last.then_inc(ffn_full, 1)
            for j in range(TT):
                o = bank(7, TT, C)
                for i in range(IT):
                    if j == 0 and i % 2 == 0:
                        pe.wait_ge(ffn_ready, i // 2 + 1)
                    last = nc.tensor.matmul(o[:, j, :], hm[:, i, j * 128:j * 128 + 128],
                                            lutw[:, 2, i * C:(i + 1) * C], start=i == 0, stop=i == IT - 1)
            last.then_inc(ffn_out, 1)

        def tail_act(act, step):
            act.wait_ge(loop_over, 3)
            act_rstd(act, step, TT, 7)
            act.wait_ge(ssm_p, 1)
            nc.scalar.activation(sx, bank(3)[0:SSM, 0:T], ACT.Copy).then_inc(soft_in, 1)
            step(nc.scalar.activation(negA[0:SSM, :], col("a_log")[0:SSM, :], ACT.Exp))
            act.wait_ge(soft_in, 2)
            step(nc.scalar.activation(sy, sy, ACT.Exp))
            step(nc.scalar.activation(sy, sy, ACT.Ln, bias=ones[0:SSM, 0:1]))
            nc.scalar.activation(sa, sx, ACT.Copy).then_inc(soft_out, 1)
            act.wait_ge(soft_in, 3)
            nc.scalar.activation(sa, sx, ACT.Exp, scale=negA[0:SSM, :]).then_inc(decay, 1)
            act_rstd(act, step, TT, 8)
            act.wait_ge(gap_ready, 1)
            nc.scalar.activation(gate2[:, 0, :], gate2[:, 1, :], ACT.Exp).then_inc(gap_exp, 1)

            def silu(e, k):
                act.wait_ge(gu_full, 2 * e + 1)
                if not (isinstance(e, int) and e < 2):
                    act.wait_ge(act_ready, e - 1)
                nc.scalar.activation(sg[k], bank(2 * k), ACT.Silu).then_inc(silu_ready, 1)

            nc.scalar.preload_act_table(ACT.Silu)
            silu(0, 0)
            silu(1, 1)
            with act.Fori(1, 4) as i:
                silu(2 * i, 0)
                silu(2 * i + 1, 1)
            nc.scalar.preload_act_table_set("natural_log_exp_and_others")
            act_rstd(act, step, TT, 9)
            for j in range(TT):
                act.wait_ge(sc_shift, j + 1)
                nc.scalar.activation(pr[:, j, :], pr[:, j, :], ACT.Exp, bias=amax[:, j:j + 1],
                                     accum_out=asum[:, j:j + 1]).then_inc(sc_exp, 1)
            act_rstd(act, step, TT, 10)
            act.wait_ge(qkv_full, 6)
            nc.scalar.activation(vr, bank(5, TT, 128), ACT.Copy).then_inc(v_ready, 1)
            act.wait_ge(rsc_shift, 1)
            nc.scalar.activation(rs_, rs_, ACT.Exp, scale=0.25).then_inc(rsc_exp, 1)
            act_rstd(act, step, TT, 11)
            nc.scalar.preload_act_table(ACT.Silu)
            for i in range(IT // 2):
                act.wait_ge(ffn_full, 2 * i + 1)
                nc.scalar.activation(sgf[:, 2 * i:2 * i + 2, :], bank(2 * i, 2, T), ACT.Silu).then_inc(ffn_silu, 1)

        def tail_pool(pool, step):
            pool.wait_ge(loop_over, 3)
            nc.gpsimd.memset(hpad[:, :, :, 0:3], 0.0).then_inc(hpad_zero, 1)
            for c in range(CT):
                last = nc.gpsimd.tensor_tensor(diagD[:, c, :], ident, col("ssm_d", c).broadcast_to([128, 128]), ALU.mult)
            last.then_inc(diag_d, 1)
            pool.wait_ge(ld_w["mask"], 16 * B)
            step(nc.gpsimd.tensor_copy(mask, mask_u8))
            nc.gpsimd.tensor_scalar(negm, mask, -1.0, 1e30, ALU.add, ALU.mult).then_inc(mask_ready, 1)

        def tail_dve(dve, step):
            def norm(k):
                dve.wait_ge(x_ready, k)
                token_norm(dve, step, x, h, 6 + k).then_inc(ln_done, 1)
                dve.wait_ge(turned, k)

            dve.wait_ge(loop_over, 3)
            dve.wait_ge(proj_out, 2)
            nc.vector.scalar_tensor_tensor(x[:, 1, :], bank(1)[:, 0:C], pscale, x[:, 1, :], ALU.mult, ALU.add)\
                .then_inc(x_ready, 1)
            norm(1)
            dve.wait_ge(hpad_zero, 1)
            o = bank(1, CT, T)
            for c in range(CT):
                last = nc.vector.tensor_copy(hpad[:, c, :, 3:S + 3], o[:, c, :].rearrange("p (b s) -> p b s", b=B))
            last.then_inc(hT_ready, 1)
            dve.wait_ge(hT_ready, 1)
            xcv = xc.rearrange("p c (b s) -> p c b s", b=B)
            for c in range(CT):
                last = nc.vector.tensor_scalar(xcv[:, c], hpad[:, c, :, 0:S], col("conv_w", 4 * c), col("conv_b", c),
                                               ALU.mult, ALU.add)
            step(last)
            for k in range(1, 4):
                for c in range(CT):
                    last = nc.vector.scalar_tensor_tensor(xcv[:, c], hpad[:, c, :, k:S + k], col("conv_w", 4 * c + k),
                                                          xcv[:, c], ALU.mult, ALU.add)
                if k < 3:
                    step(last)
            last.then_inc(conv_ready, 1)
            dve.wait_ge(soft_in, 1)
            nc.vector.scalar_tensor_tensor(sy, sx, -1.0, sx, ALU.mult, ALU.min).then_inc(soft_in, 1)
            dve.wait_ge(soft_out, 1)
            step(nc.vector.tensor_scalar(negA[0:SSM, :], negA[0:SSM, :], -1.0, None, ALU.mult))
            nc.vector.scalar_tensor_tensor(sx, sx, 0.0, sy, ALU.max, ALU.add).then_inc(soft_in, 1)
            dve.wait_ge(soft_in, 3)
            step(nc.vector.tensor_tensor(su, sx, bank(2)[0:SSM, 0:T], ALU.mult))
            dve.wait_ge(ssm_x, 1)
            step(nc.vector.tensor_tensor(su, su, bank(4)[0:SSM, 0:T], ALU.mult))
            dve.wait_ge(decay, 1)
            step(nc.vector.memset(sa.rearrange("p (b s) -> p b s", b=B)[:, :, 0:1], 0.0))
            step(nc.vector.tensor_tensor_scan(sy, sa, su, 0.0, ALU.mult, ALU.add))
            nc.vector.tensor_tensor(sz, sy, bank(2)[0:SSM, T:2 * T], ALU.mult).then_inc(hm_ready, 1)
            dve.wait_ge(ssm_out_full, 1)
            nc.vector.tensor_tensor(x, x, bank(5, TT, C), ALU.add).then_inc(x_ready, 1)
            norm(2)
            nc.vector.tensor_copy(hT, bank(6, CT, T)).then_inc(hT_ready, 1)
            dve.wait_ge(route_full, 1)
            iota = const("iota")[:, 0:NE].unsqueeze(1).broadcast_to([128, TT, NE])
            step(nc.vector.tensor_scalar(iota8, iota, float(NE), None, ALU.add))
            step(nc.vector.tensor_copy(logit, bank(7, TT, NE)))

            def over(a):
                return a.unsqueeze(2).broadcast_to([128, TT, NE])

            for k in range(2):
                step(nc.vector.tensor_reduce(top[:, k, :], logit, AX, ALU.max))
                step(nc.vector.tensor_tensor(eq, logit, over(top[:, k, :]), ALU.is_equal))
                step(nc.vector.scalar_tensor_tensor(cand, eq, -float(NE), iota8, ALU.mult, ALU.add))
                step(nc.vector.tensor_reduce(best[:, k, :], cand, AX, ALU.min))
                step(nc.vector.tensor_tensor(oh[k], cand, over(best[:, k, :]), ALU.is_equal))
                if k == 0:
                    step(nc.vector.scalar_tensor_tensor(logit, oh[k], -3.0e38, logit, ALU.mult, ALU.add))
            nc.vector.tensor_tensor(gate2[:, 1, :], top[:, 1, :], top[:, 0, :], ALU.subtract).then_inc(gap_ready, 1)
            dve.wait_ge(gap_exp, 1)
            step(nc.vector.tensor_scalar(gate2[:, 1, :], gate2[:, 0, :], 1.0, None, ALU.add))
            step(nc.vector.reciprocal(prob[:, 0, :], gate2[:, 1, :]))
            step(nc.vector.tensor_tensor(prob[:, 1, :], prob[:, 0, :], gate2[:, 0, :], ALU.mult))
            step(nc.vector.tensor_tensor(mixw, oh[0], over(prob[:, 0, :]), ALU.mult))
            step(nc.vector.tensor_tensor(mixt, oh[1], over(prob[:, 1, :]), ALU.mult))
            nc.vector.tensor_tensor(mixw, mixw, mixt, ALU.add).then_inc(moe_added, 1)

            def activate(e, k):
                dve.wait_ge(silu_ready, e + 1)
                step(nc.vector.tensor_scalar(sg[k], sg[k], 7.0, -7.0, ALU.min, ALU.max))
                dve.wait_ge(gu_full, 2 * e + 2)
                if not (isinstance(e, int) and e < 2):
                    dve.wait_ge(down_full, e - 1)
                nc.vector.tensor_tensor(am[k], sg[k].rearrange("p (m t) -> p m t", m=CT), bank(2 * k + 1, CT, T),
                                        ALU.mult).then_inc(act_ready, 1)

            def add_expert(e, k):
                dve.wait_ge(down_full, e + 1)
                dve.wait_ge(moe_added, e + 1)
                o = bank(4 + k, TT, C)
                for j in range(TT):
                    last = nc.vector.scalar_tensor_tensor(x[:, j, :], o[:, j, :],
                                                          mixw.rearrange("p j e -> p (j e)")[:, DS(e + j * NE, 1)],
                                                          x[:, j, :], ALU.mult, ALU.add)
                last.then_inc(moe_added, 1)

            activate(0, 0)
            activate(1, 1)
            add_expert(0, 0)
            with dve.Fori(1, 4) as i:
                step.loop(i, 1, 2)
                activate(2 * i, 0)
                add_expert(2 * i - 1, 1)
                activate(2 * i + 1, 1)
                add_expert(2 * i, 0)
                step.over(3)
            add_expert(7, 1)
            dve.wait_ge(moe_added, 9)
            nc.vector.memset(nt[:, 29:30], 0.0).then_inc(x_ready, 1)
            norm(3)
            nc.vector.tensor_copy(hT, bank(6, CT, T)).then_inc(hT_ready, 1)
            dve.wait_ge(mask_ready, 1)
            step(nc.vector.tensor_reduce(top[:, 0, :], mask, AX, ALU.max))
            for j in range(TT):
                dve.wait_ge(sc_full, j + 1)
                step(nc.vector.scalar_tensor_tensor(pr[:, j, :], bank(j), C ** -0.5, mask[:, j, :], ALU.mult, ALU.mult))
                step(nc.vector.tensor_tensor(pr[:, j, :], pr[:, j, :], negm[:, j, :], ALU.add))
                nc.vector.tensor_reduce(amax[:, j:j + 1], pr[:, j, :], AX, ALU.max, negate=True).then_inc(sc_shift, 1)
            dve.wait_ge(sc_exp, 2)
            step(nc.vector.reciprocal(asum[:, 0:TT], asum[:, 0:TT]))
            step(nc.vector.tensor_tensor(asum[:, 0:TT], asum[:, 0:TT], top[:, 0, :], ALU.mult))
            for j in range(TT):
                dve.wait_ge(pt_full, j + 1)
                nc.vector.tensor_copy(pT[:, j, :], bank(2 + j)).then_inc(pt_ready, 1)
            dve.wait_ge(read_full, 1)
            for j in range(TT):
                last = nc.vector.scalar_tensor_tensor(x[:, j, :], bank(4 + j)[:, 0:C], asum[:, j:j + 1], x[:, j, :],
                                                      ALU.mult, ALU.add)
            last.then_inc(x_ready, 1)
            norm(4)
            nc.vector.tensor_copy(hT, bank(6, CT, T)).then_inc(hT_ready, 1)
            cos, sin = const("cos"), const("sin")
            for i in range(5):
                dve.wait_ge(qkv_full, i + 1)
                o = bank(i, 2, T)
                q1, q2 = (qr[:, i, :], qt2[:, i, :]) if i < 4 else (kr, kt2)
                nc.vector.tensor_tensor(q1, o[:, 0, :], cos, ALU.mult)
                last = nc.vector.tensor_tensor(q2, o[:, 1, :], sin, ALU.mult)
            step(last)
            nc.vector.tensor_tensor(kr, kr, kt2, ALU.add)
            nc.vector.tensor_tensor(qr, qr, qt2, ALU.add).then_inc(rot_ready, 1)
            dve.wait_ge(rsc_full, 1)
            src = PS[:, 0:2048].rearrange("p (g q) -> p g q", g=4)[:, :, 0:256]
            step(nc.vector.transpose(rs_.rearrange("p (g a) q -> p g (a q)", g=4), src))
            step(nc.vector.tensor_reduce(amax, rs_, AX, ALU.max))
            nc.vector.tensor_tensor(rs_, rs_, amax.unsqueeze(2).broadcast_to([128, 32, 32]), ALU.subtract)\
                .then_inc(rsc_shift, 1)
            dve.wait_ge(rsc_exp, 1)
            step(nc.vector.tensor_reduce(asum, rs_, AX, ALU.add))
            step(nc.vector.reciprocal(asum, asum))
            step(nc.vector.tensor_tensor(rp_, rs_, asum.unsqueeze(2).broadcast_to([128, 32, 32]), ALU.mult))
            nc.vector.transpose(rs_, rp_).then_inc(rp_ready, 1)
            dve.wait_ge(rmix_full, 1)
            for b4 in range(4):
                src = bank(4 + b4, TT, 4, S)
                dst = oT.rearrange("p a (j q) -> p j a q", j=TT)[:, :, :, 32 * b4:32 * b4 + 32]
                for j in range(TT):
                    last = nc.vector.tensor_copy(dst[:, j], src[:, j])
            last.then_inc(oT_ready, 1)
            dve.wait_ge(wo_full, 1)
            nc.vector.tensor_tensor(x, x, bank(0, TT, C), ALU.add).then_inc(x_ready, 1)
            norm(5)
            nc.vector.tensor_copy(hT, bank(6, CT, T)).then_inc(hT_ready, 1)
            for i in range(IT // 2):
                dve.wait_ge(ffn_silu, i + 1)
                dve.wait_ge(ffn_full, 2 * i + 2)
                nc.vector.tensor_tensor(hm[:, 2 * i:2 * i + 2, :], sgf[:, 2 * i:2 * i + 2, :], bank(2 * i + 1, 2, T),
                                        ALU.mult).then_inc(ffn_ready, 1)
            dve.wait_ge(ffn_out, 1)
            nc.vector.tensor_tensor(x, x, bank(7, TT, C), ALU.add).then_inc(x_ready, 1)

        block = ctx.enter_context(nc.Block())

        @block.sync
        def _(sp):
            sp.dma_start(consts, io["consts"]).then_inc(ld_const, 16)
            sp.dma_start(vec, io["vectors"]).then_inc(ld_const, 16)
            sp.dma_start(x, io["x"]).then_inc(ld_x, 16)
            sp.dma_start(wkn, io["wk_nat"]).then_inc(ld_wkn, 16)
            for n in range(2):
                sp.dma_start(wch[n], io["chunks"][n]).then_inc(ld_chunk[n], 16)
            sp.dma_start(wkT, io["wkT"]).then_inc(ld_wkT, 16)
            for n in range(2, NCH):
                sp.wait_ge(proj_full, 4 * (n - 1))
                sp.dma_start(wch[n % 2], io["chunks"][n]).then_inc(ld_chunk[n % 2], 16)
                if n == 3:
                    for b in range(2):
                        sp.dma_start(ctxT[b], io["ctxT"][b]).then_inc(ld_ctxT[b], 16)
                        sp.dma_start(keysr[b], io["ctx"][b]).then_inc(ld_ctx[b], 16)
                    sp.dma_start(wvT, io["wvT"]).then_inc(ld_wvT, 16)
            sp.wait_ge(proj_full, 4 * NCH)
            sp.dma_start(wpc, io["wproj"][:, 0:NH, :]).then_inc(ld_wpc, 16)
            sp.wait_ge(front_over, 4)
            for m in range(2):
                sp.dma_start(idx_raw[:, m, :], io["idx"][:, m, :]).then_inc(ld_idx[m], 16)
            sp.wait_ge(idx_ready, 1)
            sp.dma_start(idx_raw[:, 0, :], io["idx"][:, 2, :]).then_inc(ld_idx[2], 16)
            sp.dma_start(wpx, io["wproj"][:, NH:2 * NH, :]).then_inc(ld_wpx, 16)

            def load_ctxT(b, k):
                sp.wait_ge(st_full, 4 * b - 4)
                sp.dma_start(ctxT[k], io["ctxT"][DS(b, 1)].rearrange("o p c n -> (o p) c n")).then_inc(ld_ctxT[k], 16)

            def load_ctx(b, k):
                sp.wait_ge(pctx, 2 * b - 2)
                sp.dma_start(keysr[k], io["ctx"][DS(b, 1)].rearrange("o p c n -> (o p) c n")).then_inc(ld_ctx[k], 16)

            load_ctxT(2, 0)
            with sp.Fori(1, 3) as i:
                load_ctxT(2 * i + 1, 1)
                load_ctx(2 * i, 0)
                load_ctxT(2 * i + 2, 0)
                load_ctx(2 * i + 1, 1)
            load_ctxT(7, 1)
            load_ctx(6, 0)
            load_ctx(7, 1)
            tail_sync(sp)

        @block.tensor
        def _(pe):
            def ring(name, i=0):
                u = RING_AT[name] + i
                if u >= 4:
                    who = RING_OWNER[u - 4]
                    pe.wait_ge(ring_read[who], reads(who, u - 3))
                return 4 + u % 4

            pe.wait_ge(ld_const, 32)
            pe.wait_ge(ld_wkn, 16)
            for i in range(4):
                nc.tensor.matmul(bank(ring("center", i)), const("center"), wkn[:, i * 512:(i + 1) * 512],
                                 start=True, stop=True).then_inc(ring_full, 1)
            pe.wait_ge(ln_done, 1)
            o = bank(ring("lnT"), CT, T)
            for i in range(4):
                j, c = i // CT, i % CT
                last = nc.tensor.transpose(o[:, c, j * 128:j * 128 + 128], raw[0][:, j, c * 128:c * 128 + 128], ident)
            last.then_inc(ring_full, 4)

            def project(n):
                pe.wait_ge(xs_ready, VARIANT[n] + 1)
                pe.wait_ge(ld_chunk[n % 2], 16 * (n // 2 + 1))
                for q in range(4):
                    j, hf = q // 2, q % 2
                    if n:
                        pe.wait_ge(proj_read, 4 * n - 3 + q)
                    for c in range(CT):
                        last = nc.tensor.matmul(bank(q), xs[:, VARIANT[n], c, j * 128:j * 128 + 128],
                                                wch[n % 2][:, c, hf * 512:hf * 512 + 512],
                                                start=c == 0, stop=c == CT - 1)
                    last.then_inc(proj_full, 1)

            def turn(n):
                pe.wait_ge(z_ready, ZORDER.index(n) + 1)
                pe.wait_ge(z_act, ZORDER.index(n) + 1)
                for i in range(4):
                    if n == 5:
                        pe.wait_ge(proj_read, 20 + i + 1)
                        o = bank(i, 2, T)
                    else:
                        o = bank(ring(f"turn{n}", i), 2, T)
                    for k in range(4):
                        hd, j = k // 2, k % 2
                        c0 = (2 * i + hd) * 128
                        last = nc.tensor.transpose(o[:, hd, j * 128:j * 128 + 128],
                                                   raw[RAW_SLOT[n]][:, j, c0:c0 + 128], ident)
                    last.then_inc(low_full if n == 5 else ring_full, 1)

            def cross_queries(n):
                pe.wait_ge(ring_read["act"], reads("act", RING_AT[f"turn{n}"] + 4))
                pe.wait_ge(bk_ready, 1)
                for i in range(4):
                    nc.tensor.matmul(bank(ring(f"beta{n}", i)), bk, zlnT[:, 2 * i:2 * i + 2, :],
                                     start=True, stop=True).then_inc(ring_full, 1)
                pe.wait_ge(u_ready, n + 1)
                for i in range(8):
                    g, c = i // CT, i % CT
                    nc.tensor.matmul(bank(ring(f"A{n}", i)), wkc[:, 4 * n + g, c * 128:c * 128 + 128],
                                     uT[:, 2 * g:2 * g + 2, :], start=True, stop=True).then_inc(ring_full, 1)

            def scores(n):
                low = n == 5
                if low:
                    pe.wait_ge(low_read["act"], 4)
                else:
                    pe.wait_ge(ring_read["act"], reads("act", RING_AT["turn4"] + 4))
                for i in range(4):
                    o = bank(i if low else ring("scores4", i), TT, 256)
                    for j in range(TT):
                        last = nc.tensor.matmul(o[:, j, :], kT[:, 4 * low + i, j * 128:j * 128 + 128],
                                                zq[low][:, 2 * i:2 * i + 2, j * 128:j * 128 + 128],
                                                start=True, stop=True)
                    last.then_inc(low_full if low else ring_full, 1)

            def mix(n):
                low = n == 5
                pe.wait_ge(pbd_ready, n - 3)
                pe.wait_ge(proj_read, 16)
                for i in range(4):
                    g = 4 * low + i
                    o = bank(i if low else ring("mix4", i), HPG, T)
                    for j in range(TT):
                        last = nc.tensor.matmul(o[:, :, j * 128:j * 128 + 128], v[:, j, g * D:(g + 1) * D],
                                                pbd[low][:, 2 * i + j, :, :], start=True, stop=True)
                    last.then_inc(low_full if low else ring_full, 1)

            project(0)
            project(1)
            turn(0)
            cross_queries(0)
            project(2)
            turn(1)
            cross_queries(1)
            project(3)
            turn(2)
            project(4)
            project(5)
            turn(4)
            scores(4)
            turn(5)
            scores(5)
            mix(4)
            mix(5)
            pe.wait_ge(ld_wpc, 16)
            o = bank(ring("core"), TT, C)
            for j in range(TT):
                for i in range(NH):
                    if j == 0 and i % 4 == 0:
                        pe.wait_ge(catc_ready, i // 4 + 1)
                    last = nc.tensor.matmul(o[:, j, :], catc[:, i, j * 128:j * 128 + 128], wpc[:, i, :],
                                            start=i == 0, stop=i == NH - 1)
            last.then_inc(ring_full, 1)
            nc.tensor.matmul(bank(0)[:, 0:128], ident, ident, start=True, stop=True).then_inc(front_over, 1)
            loop_pe(pe)
            tail_pe(pe)

        @block.scalar
        def _(act):
            step = Steps(act, act_step)
            nc.scalar.preload_act_table_set("natural_log_exp_and_others")

            def read_ring(name, i, dst, **kw):
                u = RING_AT[name] + i
                act.wait_ge(ring_full, u + 1)
                nc.scalar.activation(dst, bank(4 + u % 4, *dst.shape[1:]) if len(dst.shape) > 2 else bank(4 + u % 4),
                                     ACT.Copy, **kw).then_inc(ring_read["act"], 1)

            def read_chunk(n):
                for q in range(4):
                    j, hf = q // 2, q % 2
                    act.wait_ge(proj_full, 4 * n + q + 1)
                    if n == 1 and q == 0:
                        act.wait_ge(ring_full, 4)
                    if n == 2 and q == 0:
                        act.wait_ge(ring_full, RING_AT["turn0"] + 4)
                    if n == 4 and q == 0:
                        act.wait_ge(ring_full, RING_AT["turn1"] + 4)
                    if n == 5 and q == 0:
                        act.wait_ge(ring_full, RING_AT["turn2"] + 4)
                    dst = v if n == 3 else raw[RAW_SLOT[n]]
                    nc.scalar.activation(dst[:, j, hf * 512:hf * 512 + 512], bank(q), ACT.Copy,
                                         scale=col("w_scale", VARIANT[n])).then_inc(proj_read, 1)

            def cross_queries(n):
                for i in range(4):
                    read_ring(f"beta{n}", i, beta[:, 8 * n + 2 * i:8 * n + 2 * i + 2, :])
                for i in range(8):
                    g, c = i // CT, i % CT
                    read_ring(f"A{n}", i, A[:, c, 8 * n + 2 * g:8 * n + 2 * g + 2, :])

            def normalise(n):
                k = ZORDER.index(n)
                act_rstd(act, step, NH, k + 2)
                act.wait_ge(deviations, k + 1)
                for i in range(8):
                    hd = raw[RAW_SLOT[n]][:, 1, i * D:(i + 1) * D]
                    last = nc.scalar.activation(hd, hd, ACT.Identity, scale=rs[:, 8 + i:9 + i], bias=nbias[:, 8 + i:9 + i])
                last.then_inc(z_act, 1)

            def read_turn(n, dst, w, b):
                for i in range(4):
                    if n == 5:
                        act.wait_ge(low_full, i + 1)
                        src = bank(i, 2, T)
                    else:
                        act.wait_ge(ring_full, RING_AT[f"turn{n}"] + i + 1)
                        src = bank(4 + (RING_AT[f"turn{n}"] + i) % 4, 2, T)
                    nc.scalar.activation(dst[:, 2 * i:2 * i + 2, :], src, ACT.Identity, scale=col(w), bias=col(b))\
                        .then_inc(low_read["act"] if n == 5 else ring_read["act"], 1)

            act_rstd(act, step, TT, 0)
            act_rstd(act, step, TT, 1)
            for i in range(4):
                read_ring("center", i, wkc[:, 2 * i:2 * i + 2, :])
            read_chunk(0)
            normalise(0)
            read_chunk(1)
            read_turn(0, zlnT, "qxln_w", "qxln_b")
            cross_queries(0)
            normalise(1)
            read_chunk(2)
            read_turn(1, zlnT, "qxln_w", "qxln_b")
            cross_queries(1)
            normalise(2)
            read_chunk(3)
            read_turn(2, kT, "kln_w", "kln_b")
            read_chunk(4)
            normalise(4)
            read_chunk(5)
            read_turn(4, zlnT, "qln_w", "qln_b")
            normalise(5)
            read_turn(5, zq[1], "qln_w", "qln_b")
            for n in range(2):
                act.wait_ge(shifted_core, n + 1)
                nc.scalar.activation(at_p[n], at_s[n], ACT.Exp, scale=SCALE).then_inc(exp_core, 1)
            for n in range(2):
                for i in range(4):
                    if n:
                        act.wait_ge(low_full, 8 + i + 1)
                        src = bank(i, HPG, T)
                    else:
                        act.wait_ge(ring_full, RING_AT["mix4"] + i + 1)
                        src = bank(4 + (RING_AT["mix4"] + i) % 4, HPG, T)
                    for a in range(HPG):
                        hd = 8 * n + 2 * i + a
                        last = nc.scalar.activation(y_all[n][:, 2 * i + a, :], src[:, a, :], ACT.Copy,
                                                    scale=inv_smooth[:, hd:hd + 1])
                    last.then_inc(y_core if n else ring_read["act"], 1)
            read_ring("core", 0, core)
            nc.scalar.activation(nt[:, 31:32], nt[:, 0:1], ACT.Copy).then_inc(front_over, 1)
            loop_act(act, step)
            tail_act(act, step)

        @block.gpsimd
        def _(pool):
            step = Steps(pool, pool_step)
            nc.gpsimd.memset(eps, EPS).then_inc(front_over, 1)
            pool.wait_ge(ring_full, RING_AT["A1"] + 8)
            nc.gpsimd.memset(pbd[0], 0.0).then_inc(pbd_zero, 1)
            pool.wait_ge(low_full, 4)
            nc.gpsimd.memset(pbd[1], 0.0).then_inc(pbd_zero, 1)
            pool.wait_ge(front_over, 4)
            loop_pool(pool, step)
            tail_pool(pool, step)

        @block.vector
        def _(dve):
            step = Steps(dve, dve_step)
            dve.wait_ge(ld_const, 32)
            step(nc.vector.reciprocal(inv_scale, vec[:, COL["in_scale"]]))
            step(nc.vector.reciprocal(inv_smooth, vec[:, COL["smooth"]]))
            nc.vector.tensor_copy(bk, col("kxln_b").broadcast_to([128, 128])).then_inc(bk_ready, 1)
            dve.wait_ge(ld_x, 16)
            h0 = raw[0][:, :, 0:C]
            step(token_norm(dve, step, x, h0, 0))
            token_norm(dve, step, h0, h0, 1).then_inc(ln_done, 1)
            dve.wait_ge(ring_full, RING_AT["lnT"] + 4)
            o = bank(4 + RING_AT["lnT"] % 4, CT, T)
            for c in range(CT):
                last = nc.vector.tensor_scalar(lnT[:, c, :], o[:, c, :], col("ln_w", c), col("ln_b", c),
                                               ALU.mult, ALU.add)
            last.then_inc(ring_read["dve"], 4)
            dve.wait_ge(ring_read["dve"], 4)
            for n in range(4):
                yv = y_bf[:, 0:CT * T].rearrange("p (c t) -> p c t", c=CT)
                for c in range(CT):
                    last = nc.vector.tensor_scalar(yv[:, c, :], lnT[:, c, :], inv_scale[:, n * CT + c:n * CT + c + 1],
                                                   FP8_MAX, ALU.mult, ALU.min)
                step(last)
                step(nc.vector.tensor_scalar(y_bf[:, 0:CT * T], y_bf[:, 0:CT * T], -FP8_MAX, None, ALU.max))
                step(round_fp8(step, CT * T, t_fp[:, 0:CT * T]))
                for c in range(CT):
                    last = nc.vector.tensor_scalar(xs[:, n, c, :], t_fp[:, c * T:(c + 1) * T],
                                                   col("in_scale", n * CT + c), None, ALU.mult)
                last.then_inc(xs_ready, 1)
            dve.wait_ge(xs_ready, 4)

            def norm_heads(n):
                k = ZORDER.index(n)
                r = raw[RAW_SLOT[n]]
                for j in range(TT):
                    dve.wait_ge(proj_read, 4 * n + 2 * j + 2)
                    for i in range(8):
                        last = nc.vector.bn_stats(st[:, 8 * j + i, :], r[:, j, i * D:(i + 1) * D])
                step(last)
                step(nc.vector.tensor_tensor(mv[:, :, 0], st[:, :, 1], st[:, :, 4], ALU.add))
                step(nc.vector.tensor_tensor(mv[:, :, 1], st[:, :, 1], st[:, :, 4], ALU.subtract))
                step(nc.vector.tensor_tensor(nt[:, 0:NH], st[:, :, 2], st[:, :, 5], ALU.add))
                step(nc.vector.scalar_tensor_tensor(mv[:, :, 1], mv[:, :, 1], D / 4.0, mv[:, :, 1], ALU.mult, ALU.mult))
                step(nc.vector.tensor_tensor(nt[:, 0:NH], nt[:, 0:NH], mv[:, :, 1], ALU.add))
                nc.vector.tensor_scalar(var[:, 0:NH], nt[:, 0:NH], 1.0 / D, EPS, ALU.mult, ALU.add).then_inc(ln_var, 1)
                dve.wait_ge(ln_rstd, k + 3)
                dve.wait_ge(ln_var, k + 3)
                newton(dve, step, rs[:, 0:NH], rs0[:, 0:NH], var[:, 0:NH], nt[:, 0:NH])
                nc.vector.scalar_tensor_tensor(nbias, mv[:, :, 0], -0.5, rs[:, 0:NH], ALU.mult, ALU.mult)\
                    .then_inc(deviations, 1)
                dve.wait_ge(deviations, k + 1)
                for i in range(8):
                    hd = r[:, 0, i * D:(i + 1) * D]
                    last = nc.vector.tensor_scalar(hd, hd, rs[:, i:i + 1], nbias[:, i:i + 1], ALU.mult, ALU.add)
                last.then_inc(z_ready, 1)
                dve.wait_ge(z_ready, k + 1)
                dve.wait_ge(z_act, k + 1)

            def read_turn_cross(n):
                u0 = RING_AT[f"turn{n}"]
                if n:
                    dve.wait_ge(ring_full, RING_AT[f"A{n - 1}"] + 8)
                for i in range(4):
                    dve.wait_ge(ring_read["act"], reads("act", u0 + i + 1))
                    last = nc.vector.tensor_scalar(uT[:, 2 * i:2 * i + 2, :], zlnT[:, 2 * i:2 * i + 2, :],
                                                   col("kxln_w"), None, ALU.mult)
                last.then_inc(u_ready, 1)

            norm_heads(0)
            read_turn_cross(0)
            norm_heads(1)
            read_turn_cross(1)
            dve.wait_ge(ld_wkT, 16)
            heads = wkT.rearrange("p c (g d) -> p (c g) d", g=G)
            step(nc.vector.tensor_reduce(nt[:, 0:CT * G], heads, AX, ALU.add))
            step(nc.vector.tensor_scalar(nt[:, 0:CT * G], nt[:, 0:CT * G], 1.0 / D, None, ALU.mult))
            nc.vector.tensor_tensor(heads, heads, nt[:, 0:CT * G].unsqueeze(2).broadcast_to([128, CT * G, D]),
                                    ALU.subtract).then_inc(wk_centered, 1)
            norm_heads(2)
            norm_heads(4)
            norm_heads(5)

            def core_scores(low):
                if low:
                    dve.wait_ge(low_full, 8)
                else:
                    dve.wait_ge(ring_full, RING_AT["scores4"] + 4)
                sc = PS[:, 2048 * (1 - low):2048 * (2 - low)].rearrange("p (a q) -> p a q", a=8)
                for b4 in range(4):
                    q0 = 32 * b4
                    src = sc[q0:q0 + 32].rearrange("p a (h q) -> p (a h) q", h=2)[:, :, q0:q0 + 32]
                    last = nc.vector.transpose(at_s[low][q0:q0 + 32], src)
                if low:
                    step(last)
                else:
                    last.then_inc(ring_read["dve"], 4)
                    dve.wait_ge(ring_read["dve"], reads("dve", RING_AT["scores4"] + 4))
                step(nc.vector.tensor_reduce(amax[:, 0:16], at_s[low], AX, ALU.max))
                nc.vector.tensor_tensor(at_s[low], at_s[low], amax[:, 0:16].unsqueeze(2).broadcast_to([128, 16, 32]),
                                        ALU.subtract).then_inc(shifted_core, 1)

            def core_weights(low):
                dve.wait_ge(exp_core, low + 1)
                step(nc.vector.tensor_reduce(asum[:, 0:16], at_p[low], AX, ALU.add))
                step(nc.vector.reciprocal(asum[:, 0:16], asum[:, 0:16]))
                step(nc.vector.tensor_tensor(at_p[low], at_p[low], asum[:, 0:16].unsqueeze(2)
                                             .broadcast_to([128, 16, 32]), ALU.mult))
                dve.wait_ge(pbd_zero, low + 1)
                pb = pbd[low].rearrange("p a h q -> p (a h) q")
                for b4 in range(4):
                    q0 = 32 * b4
                    last = nc.vector.transpose(pb[q0:q0 + 32, :, q0:q0 + 32], at_p[low][q0:q0 + 32])
                last.then_inc(pbd_ready, 1)

            core_scores(0)
            core_scores(1)
            core_weights(0)
            core_weights(1)
            for n in range(4):
                if n < 2:
                    dve.wait_ge(ring_read["act"], reads("act", RING_AT["mix4"] + 2 * n + 2))
                else:
                    dve.wait_ge(y_core, 2 * n - 2)
                y4 = y_all[n // 2][:, 4 * (n % 2):4 * (n % 2) + 4, :].rearrange("p a t -> p (a t)")
                step(nc.vector.tensor_scalar(y_bf, y4, FP8_MAX, -FP8_MAX, ALU.min, ALU.max))
                round_fp8(step, 4 * T, catc[:, 4 * n:4 * n + 4, :].rearrange("p a t -> p (a t)")).then_inc(catc_ready, 1)
                dve.wait_ge(catc_ready, n + 1)
            nc.vector.memset(nt[:, 29:30], 0.0).then_inc(front_over, 1)
            loop_dve(dve, step)
            tail_dve(dve, step)


def kernel(**inputs):
    import numpy as np
    import concourse.bacc as bacc
    from concourse.bass_utils import run_bass_kernel_spmd

    a = {k: np.asarray(v) for k, v in inputs.items()}
    f32 = np.float32

    def tiles(w):
        return w.reshape(-1, 128, w.shape[-1]).transpose(1, 0, 2)

    def column(v, n):
        return np.asarray(v).reshape(n, 128).T

    X, M = "L0_xattn_", "L0_attn_"
    cols = [column(a[X + "ln_w"], CT), column(a[X + "ln_b"], CT)]
    cols += [column(a[X + n + "_in_scale"], CT) for n in ("qx", "k", "v", "q")]
    cols += [column(a[X + n], 1) for n in ("qln_w", "qln_b", "kln_w", "kln_b", "qxln_w", "qxln_b", "kxln_w", "kxln_b")]
    cols += [column(a[X + "proj_smooth"], 2 * NH)]
    cols += [tiles(a[M + "conv_w"][:, 0, :]).reshape(128, 8), column(a[M + "conv_b"], CT),
             column(a[M + "D"], CT)]
    for n in ("wqx_scale", "wk_scale", "wv_scale", "wq_scale", "proj_w_scale", "proj_in_scale"):
        cols += [np.broadcast_to(a[X + n].reshape(1, 1), (128, 1))]
    cols += [np.broadcast_to(a["L1_ffn_lut"].reshape(1, LUTN), (128, LUTN))]
    cols += [np.concatenate([a[M + "A_log"], np.zeros(64, f32)]).reshape(128, 1)]
    vectors = np.ascontiguousarray(np.concatenate(cols, 1))
    assert vectors.shape == (128, NVEC), vectors.shape

    d = np.arange(128) % 32
    inv = 1.0 / 10000.0 ** (np.arange(0, 8, 2, dtype=f32) / f32(8))
    ang = (np.arange(S, dtype=f32)[None, :] * np.where(d < 8, inv.astype(f32)[np.minimum(d // 2, 3)], 0)[:, None]).astype(f32)
    cos, sin = np.cos(ang), np.sin(ang)
    sin = sin * np.where(d % 2 == 0, -1.0, 1.0)[:, None]
    cos, sin = (np.broadcast_to(t[:, None, :], (128, B, S)).reshape(128, T) for t in (cos, sin))
    consts = np.ascontiguousarray(np.concatenate([
        np.eye(128), np.ones((128, 128)), np.eye(128) - 1.0 / D, cos, sin,
        np.broadcast_to(np.arange(LUTN)[None, :], (128, LUTN))], 1).astype(f32))

    chunks = [a[X + "wqx"][:1024], a[X + "wqx"][1024:], a[X + "wk"], a[X + "wv"], a[X + "wq"][:1024], a[X + "wq"][1024:]]
    wkv = a[X + "w_kv_x"]
    ctx = a["ctx_2048"]
    swap = np.array([1, 0, 3, 2, 5, 4, 7, 6] + list(range(8, 16)))

    def heads(w, n):
        w = w.reshape(C, 4, n, 16).transpose(0, 2, 1, 3)
        return w

    def padded(w):
        z = np.zeros(w.shape[:-1] + (32,), f32)
        z[..., :16] = w
        return z.reshape(C, -1)

    wq, wk, wv = heads(a["L1_attn_Wq"], 4), heads(a["L1_attn_Wk"], 1), heads(a["L1_attn_Wv"], 1)
    wo = np.zeros((4, 4, 32, C), f32)
    wo[:, :, :16] = a["L1_attn_Wo"].reshape(4, 4, 16, C).transpose(1, 0, 2, 3)
    pad = np.full((C, IPAD - INTER), LUTN, np.int32)
    idx = [np.concatenate([a["L1_ffn_gate_idx"].astype(np.int32).T, pad], 1),
           np.concatenate([a["L1_ffn_up_idx"].astype(np.int32).T, pad], 1),
           np.concatenate([a["L1_ffn_down_idx"].astype(np.int32).T, pad.T], 0)]
    idx = np.stack([tiles(t).reshape(128, CT * IPAD) for t in idx], 1)
    wx = a[M + "Wxproj"].T
    wx = np.concatenate([wx[:, :2 * SSM], np.broadcast_to(wx[:, 2 * SSM:], (C, SSM)), a[M + "Winproj"].T], 1)
    mask = a["mask_BxS2_bk0"].view(np.int32)
    arrays = {
        "consts": consts, "vectors": vectors, "x": tiles(a["x"].reshape(T, C)),
        "wk_nat": wkv[:1024].reshape(G, D, C).transpose(1, 0, 2).reshape(128, G * C),
        "chunks": np.stack([tiles(w.T) for w in chunks]),
        "wkT": tiles(wkv[:1024].T), "wvT": tiles(wkv[1024:].T), "wproj": tiles(a[X + "wproj"].T),
        "ctxT": ctx.reshape(B, NK, CT, 128).transpose(0, 3, 2, 1), "ctx": ctx.reshape(B, KT, 128, C).transpose(0, 2, 1, 3),
        "idx": idx, "ssm_in": tiles(wx), "ssm_out": a[M + "Woutproj"].T, "router": tiles(a["L0_ffn_Wr"]),
        "gate_up": np.stack([a["L0_ffn_" + n].reshape(NE, CT, 128, C).transpose(0, 2, 1, 3).reshape(NE, 128, CT * C)
                             for n in ("Wg", "Wu")], 2),
        "down": a["L0_ffn_Wd"].reshape(NE, CT, 128, C).transpose(2, 0, 1, 3).reshape(128, NE, CT * C),
        "mask": mask,
        "wq_rot": np.stack([tiles(padded(wq)), tiles(padded(wq[..., swap]))], 1),
        "wk_rot": np.stack([tiles(padded(wk)), tiles(padded(wk[..., swap]))], 1),
        "wv_rot": tiles(padded(wv)), "wo_rot": wo.reshape(4, 128, C).transpose(1, 0, 2),
    }
    nc = bacc.Bacc("TRN2", target_bir_lowering=False, num_devices=1)
    io, sent = {}, {}
    for name, v in arrays.items():
        v = np.ascontiguousarray(v)
        sent["in_" + name] = v
        io[name] = nc.dram_tensor("in_" + name, v.shape, mybir.dt.from_np(v.dtype), kind="ExternalInput").ap()
    out = nc.dram_tensor("out_x", (128, TT, C), fp32, kind="ExternalOutput").ap()
    build(nc, io, out)
    r = run_bass_kernel_spmd(nc, [sent], core_ids=[0])
    return r.results[0]["out_x"].transpose(1, 0, 2).reshape(B, S, C)
```

```python
from contextlib import ExitStack

import concourse.bass as bass
from concourse import mybir

fp32 = mybir.dt.float32
fp32r = mybir.dt.float32r
bf16 = mybir.dt.bfloat16
u16 = mybir.dt.uint16
u8 = mybir.dt.uint8
i32 = mybir.dt.int32
ALU = mybir.AluOpType
ACT = mybir.ActivationFunctionType
AX = mybir.AxisListType.X
DS = bass.DynSlice

B, S, C, NK = 8, 32, 256, 512
T = B * S
TT, CT, KT = T // 128, C // 128, NK // 128
G, HPG, D = 8, 2, 128
NH = G * HPG
NCH = 6
VARIANT = [0, 0, 1, 3, 3, 2]
SCALED = [0, 1, 3, 2]
EPS = 1e-5
SSM = 64
NE = 8
INTER, IPAD = 688, 768
IT = IPAD // 128
LUTN = 16
NLUT = 3 * CT * IPAD
FP8_MAX = 448.0
ROUND = 1.5 * 2.0 ** 20
FP8_MIN_NORMAL = 2.0 ** -6

COL, _n = {}, 0
for _name, _w in [("ln_w", CT), ("ln_b", CT), ("in_scale", 4 * CT), ("qln_w", 1), ("qln_b", 1), ("kln_w", 1),
                  ("kln_b", 1), ("qxln_w", 1), ("qxln_b", 1), ("kxln_w", 1), ("kxln_b", 1), ("smooth", 2 * NH),
                  ("conv_w", 4 * CT), ("conv_b", CT), ("ssm_d", CT), ("w_scale", 4), ("proj_w_scale", 1),
                  ("proj_in_scale", 1), ("lut", LUTN), ("a_log", 1)]:
    COL[_name] = slice(_n, _n + _w)
    _n += _w
NVEC = _n

CONST, _n = {}, 0
for _name, _w in [("ident", 128), ("ones", 128), ("center", 128), ("cos", T), ("sin", T), ("iota", LUTN)]:
    CONST[_name] = slice(_n, _n + _w)
    _n += _w
NCONST = _n

FRONT, LOOP, TAIL, LATE = range(4)
WORDS = [
    ("consts", NCONST, FRONT, LATE), ("vec", NVEC, FRONT, LATE), ("small", 1008, FRONT, LATE),
    ("x", TT * C, FRONT, LATE), ("core", TT * C, FRONT, LATE), ("A_first", NH * C, FRONT, TAIL),
    ("A_last", NH * C, FRONT, LOOP), ("ctxT_ring", 2 * CT * NK, FRONT, LOOP), ("ctx_ring", 2 * KT * C, FRONT, LOOP),
    ("wkT", CT * G * D, FRONT, LOOP), ("wvT", CT * G * D, FRONT, LOOP), ("wkc", G * C, FRONT, LOOP),
    ("ctx_hi0", CT * NK, FRONT, LOOP), ("beta", NH * T, FRONT, LOOP), ("qtmp", 2560, FRONT, LOOP),
    ("wch", 2 * CT * 1024, FRONT, FRONT), ("raw", 2 * TT * 1024, FRONT, FRONT), ("lnT", CT * T, FRONT, FRONT),
    ("xs", 4 * CT * T, FRONT, FRONT), ("zlnT", 8 * T, FRONT, FRONT), ("uT", 8 * T, FRONT, FRONT),
    ("kT", G * T, FRONT, FRONT), ("v", TT * 1024, FRONT, FRONT), ("attn", 1024, FRONT, FRONT),
    ("catc", NH * T, FRONT, FRONT),
    ("s", 2 * KT * NK, LOOP, LOOP), ("sq", 512, LOOP, LOOP), ("vecs", 6 * NK, LOOP, LOOP),
    ("px", CT * NH * 64, LOOP, LOOP), ("ctx_hi1", CT * NK, LOOP, LOOP), ("catx", NH * T, LOOP, TAIL),
    ("luttmp", 2 * CT * IPAD, LOOP, LATE), ("lutw", NLUT, LOOP, LATE), ("idx", NLUT // 4, LOOP, LATE),
    ("keysT", CT * B * NK, TAIL, LATE), ("keys", B * KT * C, TAIL, LATE), ("mask", 2 * TT * NK, TAIL, LATE),
    ("h", TT * C, TAIL, LATE), ("hT", CT * T, TAIL, LATE), ("maskraw", TT * NK // 4, TAIL, TAIL),
    ("ssm", 3400, TAIL, TAIL), ("gateup", 2 * 2 * CT * C, TAIL, TAIL), ("down", NE * CT * C, TAIL, TAIL),
    ("moe", 2 * 2 * CT * T, TAIL, TAIL),
    ("ffn", 2 * IT * T, LATE, LATE), ("rot", 2 * 2 * 512 + 2 * 2 * 128 + 2 * 128 + 4 * C, LATE, LATE),
    ("rotact", 4 * 1024, LATE, LATE), ("probs", 2 * TT * NK, LATE, LATE),
]


def place():
    at, done = {}, []
    for name, words, first, last in WORDS:
        words += -words % 8
        near = sorted((p, p + w) for p, w, a, z in done if a <= last and z >= first)
        spot = 0
        for p, q in near:
            if p - spot >= words:
                break
            spot = max(spot, q)
        at[name] = spot
        done.append((spot, words, first, last))
    return at, max(p + w for p, w, _, _ in done)



RING = [("lnT", 4, "dve"), ("center", 4, "act")]
for _n in (0, 1):
    RING += [(f"turn{_n}", 4, "act"), (f"beta{_n}", 4, "act"), (f"A{_n}", 8, "act")]
RING += [("turn2", 4, "act"), ("turn3", 4, "act"), ("scores3", 4, "dve"), ("mix3", 4, "act"), ("core", 1, "act")]
RING_AT, RING_OWNER = {}, []
for _name, _w, _who in RING:
    RING_AT[_name] = len(RING_OWNER)
    RING_OWNER += [_who] * _w


def reads(who, upto):
    return RING_OWNER[:upto].count(who)


ZORDER = [0, 1, 2, 3, 4]


def build(nc, io, out):
    ctx = ExitStack()
    with ctx:
        at, words = place()
        size = {name: w for name, w, _, _ in WORDS}
        size["A"], at["A"] = size["A_first"] + size["A_last"], at["A_first"]

        def tensor(name, dtype):
            with ExitStack() as stack:
                if at[name]:
                    stack.enter_context(nc.sbuf_tensor(f"below_{name}_{dtype}", [128, at[name]], fp32))
                return stack.enter_context(nc.sbuf_tensor(f"{name}_{dtype}", [128, size[name]], dtype))

        tensors = {(name, fp32): tensor(name, fp32) for name in size}
        for name in ("wkc", "wkT", "ctx_hi0", "ctx_hi1", "ctxT_ring", "qtmp", "kT", "xs", "wch", "catc", "A", "catx", "A_first"):
            tensors[name, fp32r] = tensor(name, fp32r)
        PS = ctx.enter_context(nc.psum_tensor("PS", [128, 4096], fp32))

        def sem(name):
            return ctx.enter_context(nc.semaphore(name))

        def buf(name, *dims, skip=0, dtype=fp32):
            n = 1
            for d in dims:
                n *= d
            per_word = {fp32: 1, fp32r: 1, i32: 1, bf16: 2, u8: 4}[dtype]
            v = tensors[name, dtype if dtype == fp32r else fp32][:, skip:skip + -(-n // per_word)]
            if dtype not in (fp32, fp32r):
                v = v.bitcast(dtype)
            if len(dims) == 2:
                return v.rearrange("p (a b) -> p a b", a=dims[0])
            if len(dims) == 3:
                return v.rearrange("p (a b c) -> p a b c", a=dims[0], b=dims[1])
            return v

        def bank(n, *dims):
            v = PS[:, n * 512:(n + 1) * 512]
            if len(dims) == 2:
                return v[:, 0:dims[0] * dims[1]].rearrange("p (a b) -> p a b", a=dims[0])
            if len(dims) == 3:
                return v[:, 0:dims[0] * dims[1] * dims[2]].rearrange("p (a b c) -> p a b c", a=dims[0], b=dims[1])
            return v

        consts, vec = buf("consts", NCONST), buf("vec", NVEC)

        def const(name):
            return consts[:, CONST[name]]

        def col(name, i=0):
            return vec[:, COL[name].start + i:COL[name].start + i + 1]

        ident, ones = const("ident"), const("ones")
        _at = [0]

        def small(*dims):
            n = 1
            for d in dims:
                n *= d
            v = buf("small", *dims, skip=_at[0])
            _at[0] += n
            return v

        st, mv = small(NH, 6), small(NH, 2)
        var, rs0, rs, nt = small(32), small(32), small(32), small(32)
        inv_scale, inv_smooth = small(4 * CT), small(2 * NH)
        amax, asum = small(32), small(32)
        ssq, krs0 = small(2, G), small(2, G)
        kvar, krs, knt, eps = small(G), small(G), small(G), small(1)
        mcol = small(4)
        pscale = small(1)
        negA = small(1)
        nbias = small(NH)
        logit, eq, cand = small(TT, NE), small(TT, NE), small(TT, NE)
        oh = [small(TT, NE), small(TT, NE)]
        top, best, gate2, prob = small(2, TT), small(2, TT), small(2, TT), small(2, TT)
        mixw, mixt = small(TT, NE), small(TT, NE)
        iota8, bk = small(TT, NE), small(128)
        attends = small(TT)
        assert _at[0] <= 1008, _at

        x = buf("x", TT, C)
        core = buf("core", TT, C)
        h, hT = buf("h", TT, C), buf("hT", CT, T)

        ld_const, ld_x, ld_wkn, ld_wkT, ld_wvT = (sem(n) for n in ("ld_const", "ld_x", "ld_wkn", "ld_wkT", "ld_wvT"))
        ld_chunk = [sem("ld_chunk0"), sem("ld_chunk1")]
        ld_wpc, ld_wpx = sem("ld_wpc"), sem("ld_wpx")
        ld_idx = [sem("ld_idx0"), sem("ld_idx1"), sem("ld_idx2")]
        dve_step, act_step, pool_step = sem("dve_step"), sem("act_step"), sem("pool_step")
        ln_var, ln_rstd, ln_done = sem("ln_var"), sem("ln_rstd"), sem("ln_done")
        low_full, low_read = sem("low_full"), {"act": sem("low_read_act"), "dve": sem("low_read_dve")}
        u_ready = sem("u_ready")
        rounded, catc_odd = sem("rounded"), sem("catc_odd")
        lut_zero, wpx_hi_ready, wpx_split = sem("lut_zero"), sem("wpx_hi_ready"), sem("wpx_split")
        wk_hi_ready, wk_split, wpc_hi_ready, wpc_split = (sem(n) for n in ("wk_hi_ready", "wk_split", "wpc_hi_ready",
                                                                           "wpc_split"))
        ctx_hi_ready, ctx_split, A_hi_ready, A_split = (sem(n) for n in ("ctx_hi_ready", "ctx_split", "A_hi_ready",
                                                                         "A_split"))
        pbd_zero, z_act, deviations, y_core = (sem(n) for n in ("pbd_zero", "z_act", "deviations", "y_core"))
        xs_ready, wk_centered, bk_ready = sem("xs_ready"), sem("wk_centered"), sem("bk_ready")
        proj_full, proj_read = sem("proj_full"), sem("proj_read")
        z_ready = sem("z_ready")
        ring_full = sem("ring_full")
        ring_read = {"act": sem("ring_read_act"), "dve": sem("ring_read_dve")}
        shifted_core, exp_core, pbd_ready, catc_even = (sem(n) for n in ("shifted_core", "exp_core", "pbd_ready",
                                                                         "catc_even"))
        front_over, loop_over = sem("front_over"), sem("loop_over")
        ld_ctxT, ld_ctx = [sem("ld_ctxT0"), sem("ld_ctxT1")], [sem("ld_ctx0"), sem("ld_ctx1")]
        kx_full, sq_ready, krstd_ready = (sem(n) for n in ("kx_full", "sq_ready", "krstd_ready"))
        st_full, scaled, mx_ready, mxf_ready, tr_full, m_ready, diag_ready, mb_full = (sem(n) for n in (
            "st_full", "scaled", "mx_ready", "mxf_ready", "tr_full", "m_ready", "diag_ready", "mb_full"))
        shifted, p_ready, psum_ready, sum_full, r_ready, pctx, px_ready = (sem(n) for n in (
            "shifted", "p_ready", "psum_ready", "sum_full", "r_ready", "pctx", "px_ready"))
        v_full, v_read, catx_ready, proj_out = (sem(n) for n in ("v_full", "v_read", "catx_ready", "proj_out"))
        idx_ready, lut_term, lut_added = sem("idx_ready"), sem("lut_term"), sem("lut_added")

        class Steps:

            def __init__(self, eng, s):
                self.eng, self.s, self.base, self.k = eng, s, 0, 0

            def __call__(self, ins):
                ins.then_inc(self.s, 1)
                self.k += 1
                self.eng.wait_ge(self.s, self.base + self.k)

            def loop(self, i, first, per):
                self.start, self.per, self.first = self.base + self.k, per, first
                self.base, self.k = (i - first) * per + self.start, 0

            def over(self, turns):
                assert self.k == self.per, self.k
                self.base, self.k = self.start + turns * self.per, 0

        def newton(dve, step, r, r0, v, t):
            step(nc.vector.tensor_tensor(t, r0, r0, ALU.mult))
            step(nc.vector.scalar_tensor_tensor(t, t, -0.5, v, ALU.mult, ALU.mult))
            step(nc.vector.scalar_tensor_tensor(r, t, 1.5, r0, ALU.add, ALU.mult))

        def stats(dve, step, n, srcs, k):
            for i, src in enumerate(srcs):
                last = nc.vector.bn_stats(st[:, i, :], src)
            step(last)
            for i in range(n):
                last = nc.vector.bn_aggr(mv[:, i, :], st[:, i, :])
            last.then_inc(ln_var, 1)
            dve.wait_ge(ln_var, k + 1)
            step(nc.vector.tensor_scalar(var[:, 0:n], mv[:, 0:n, 1], EPS, None, ALU.add))
            dve.wait_ge(ln_rstd, k + 1)
            newton(dve, step, rs[:, 0:n], rs0[:, 0:n], var[:, 0:n], nt[:, 0:n])

        def act_rstd(act, step, n, k, src=None, scale=1.0):
            act.wait_ge(ln_var, k + 1)
            step(nc.scalar.activation(rs0[:, 0:n], mv[:, 0:n, 1] if src is None else src, ACT.Ln, scale=scale, bias=eps))
            nc.scalar.activation(rs0[:, 0:n], rs0[:, 0:n], ACT.Exp, scale=-0.5).then_inc(ln_rstd, 1)

        def token_norm(dve, step, src, dst, k):
            stats(dve, step, TT, [src[:, j, :] for j in range(TT)], k)
            for j in range(TT):
                last = nc.vector.tensor_scalar(dst[:, j, :], src[:, j, :], mv[:, j, 0:1], rs[:, j:j + 1],
                                               ALU.subtract, ALU.mult)
            return last

        y_bf = buf("qtmp", 1024, dtype=bf16)
        e_bf = buf("qtmp", 1024, skip=512, dtype=bf16)
        m_bf = buf("qtmp", 1024, skip=1024, dtype=bf16)
        t_fp = buf("qtmp", 1024, skip=1536)

        rounding = [(m_bf, t_fp), (buf("raw", 1024, skip=3072, dtype=bf16), buf("raw", 1024, skip=2048))]
        catc_flat = [buf("catc", 4 * T, skip=4 * T * n, dtype=fp32r) for n in range(4)]
        y_q, e_q, m_q = (buf("qtmp", 512, skip=256 * i, dtype=bf16) for i in range(3))
        t_q = buf("qtmp", 512, skip=768)

        def round_fp8(step, n, dst):
            step(nc.vector.tensor_scalar(e_bf[:, 0:n].bitcast(u16), y_bf[:, 0:n].bitcast(u16), 0x7F80, None,
                                         ALU.bitwise_and))
            step(nc.vector.tensor_scalar(m_bf[:, 0:n], e_bf[:, 0:n], FP8_MIN_NORMAL, ROUND, ALU.max, ALU.mult))
            step(nc.vector.tensor_tensor(t_fp[:, 0:n], y_bf[:, 0:n], m_bf[:, 0:n], ALU.add))
            return nc.vector.tensor_tensor(dst, t_fp[:, 0:n], m_bf[:, 0:n], ALU.subtract)

        wkn = buf("raw", G * C, skip=2048)
        wkc = buf("wkc", G, C)
        wkT, wvT = buf("wkT", CT, G * D), buf("wvT", CT, G * D)
        wch = [buf("wch", CT, 1024), buf("wch", CT, 1024, skip=2048)]
        wpc = buf("wch", NH, C)
        raw = [buf("raw", TT, 1024), buf("raw", TT, 1024, skip=2048)]
        RAW_SLOT = {0: 0, 1: 1, 2: 0, 3: 1, 4: 0}
        lnT, xs = buf("lnT", CT, T), buf("xs", 4, CT, T)
        zlnT, uT, kT, v = buf("zlnT", 8, T), buf("uT", 8, T), buf("kT", G, T), buf("v", TT, 1024)
        zq = [zlnT, buf("xs", 8, T)]
        pbd = [buf("uT", 8, 2, 128), buf("raw", 8, 2, 128)]
        at_s = [buf("attn", 16, 32), buf("raw", 16, 32, skip=2048)]
        at_p = [buf("attn", 16, 32, skip=512), buf("raw", 16, 32, skip=2048 + 512)]
        y_all = [buf("zlnT", 8, T, dtype=bf16), buf("zlnT", 8, T, skip=1024, dtype=bf16)]
        catc = buf("catc", NH, T)
        assert at["A_last"] == at["A_first"] + NH * C
        A = buf("A", B, CT, NH * S)
        beta = buf("beta", NH, T)

        ctxT = [buf("ctxT_ring", CT, NK), buf("ctxT_ring", CT, NK, skip=CT * NK)]
        keysr = [buf("ctx_ring", KT, C), buf("ctx_ring", KT, C, skip=KT * C)]
        sS = [buf("s", KT, NK), buf("s", KT, NK, skip=KT * NK)]
        sq = buf("sq", 1024, dtype=bf16)
        mx, nm, R = buf("vecs", 512), buf("vecs", 512, skip=512), buf("vecs", 512, skip=1536)
        diag = buf("vecs", 4, 128, skip=1024)
        ps2 = buf("vecs", 2, 512, skip=2048)
        px = buf("px", CT, NH, 64)
        catx = buf("catx", NH, T, dtype=fp32r)
        idx = buf("idx", 3, CT * IPAD, dtype=u8)
        lutt = [buf("luttmp", CT * IPAD), buf("luttmp", CT * IPAD, skip=CT * IPAD)]
        idx_raw = buf("luttmp", 2, CT * IPAD, dtype=i32)
        lutw = buf("lutw", 3, CT * IPAD)
        wpx = buf("A_first", NH, C)
        wpx_lo, wpx_hi = buf("A_first", NH, C, dtype=fp32r), buf("A", NH, C, skip=NH * C, dtype=fp32r)
        wk_hi, wk_lo = buf("wkc", CT, G * D, dtype=fp32r), buf("wkT", CT, G * D, dtype=fp32r)
        ctx_hi = [buf("ctx_hi0", CT, NK, dtype=fp32r), buf("ctx_hi1", CT, NK, dtype=fp32r)]
        ctx_lo = [buf("ctxT_ring", CT, NK, skip=k * CT * NK, dtype=fp32r) for k in range(2)]
        A_hi = buf("qtmp", CT, NK, skip=1280, dtype=fp32r)
        A_lo = buf("A", B, CT, NH * S, dtype=fp32r)
        wpc_hi = [buf("kT", 8, C, dtype=fp32r), buf("xs", 8, C, dtype=fp32r)]
        wpc_lo, catc_r = buf("wch", NH, C, dtype=fp32r), buf("catc", NH, T, dtype=fp32r)
        SCALE = D ** -0.5

        def loop_pe(pe):
            def step(b, k, pair=None, prev=True):
                pe.wait_ge(ctx_split, b + 1)
                for t in range(KT):
                    n = 4 * b + t
                    for hf in range(2):
                        if not (prev is False and t == 0):
                            pe.wait_ge(sq_ready, 2 * n + hf - 1)
                        last = product(bank(hf), k, t, wk_hi[:, :, hf * 512:hf * 512 + 512],
                                       wk_lo[:, :, hf * 512:hf * 512 + 512])
                        last.then_inc(kx_full, 1)
                    if not (prev is False and t < 2):
                        pe.wait_ge(scaled, n - 1)
                    if t == 0:
                        pe.wait_ge(A_split, b + 1)
                    lo = A_lo[:, b, :, :] if isinstance(b, int) else A_lo[:, DS(b, 1), :, :].rearrange(
                        "p o c m -> p (o c) m")
                    product(bank(2 + t % 2), k, t, A_hi, lo).then_inc(st_full, 1)
                    if prev and t == 0:
                        maxima(b - 1)
                        if pair is not None:
                            values(pair, 0)
                    if prev and t == 1:
                        spread(b - 1)
                    if pair is not None and t == 2:
                        values(pair, 1)
                if prev:
                    mix(b - 1, 1 - k)

            def product(o, k, t, hi, lo):
                for c in range(CT):
                    x_hi, x_lo = (v[k][:, c, t * 128:t * 128 + 128] for v in (ctx_hi, ctx_lo))
                    nc.tensor.matmul(o, x_hi, hi[:, c, :], start=c == 0, stop=False)
                    nc.tensor.matmul(o, x_hi, lo[:, c, :], start=False, stop=False)
                    last = nc.tensor.matmul(o, x_lo, hi[:, c, :], start=False, stop=c == CT - 1)
                return last

            def maxima(b):
                pe.wait_ge(mxf_ready, b + 1)
                if not (isinstance(b, int) and b == 0):
                    pe.wait_ge(px_ready, 2 * b)
                for j in range(4):
                    last = nc.tensor.transpose(bank(4, 4, 128)[:, j, :], mx[:, j * 128:j * 128 + 128], ident)
                last.then_inc(tr_full, 1)

            def spread(b):
                pe.wait_ge(diag_ready, b + 1)
                nc.tensor.matmul(bank(4), ones, diag.rearrange("p a q -> p (a q)"), start=True,
                                 stop=True).then_inc(mb_full, 1)

            def mix(b, k):
                pe.wait_ge(p_ready, b + 1)
                pe.wait_ge(ld_ctx[k], 8 * (b - k) + 16)
                for c in range(CT):
                    for t in range(KT):
                        last = nc.tensor.matmul(bank(5 + c), keysr[k][:, t, c * 128:c * 128 + 128], sS[k][:, t, :],
                                                start=t == 0, stop=t == KT - 1)
                    last.then_inc(pctx, 1)
                pe.wait_ge(psum_ready, b + 1)
                nc.tensor.matmul(bank(4), ones, ps2[:, 0, :], start=True, stop=True).then_inc(sum_full, 1)

            def project_out(j, heads, after):
                pe.wait_ge(catx_ready, after)
                for i in heads:
                    if j == 0 and i % 4 == 0:
                        pe.wait_ge(wpx_split, i // 4 + 1)
                    cat = catx[:, i, j * 128:j * 128 + 128]
                    nc.tensor.matmul(bank(j)[:, 0:C], cat, wpx_hi[:, i, :], start=i == 0, stop=False)
                    last = nc.tensor.matmul(bank(j)[:, 0:C], cat, wpx_lo[:, i, :], start=False, stop=i == NH - 1)
                if i == NH - 1:
                    last.then_inc(proj_out, 1)

            def values(p, hf):
                if isinstance(p, int):
                    pe.wait_ge(px_ready, 4 * p + 3 + hf)
                elif hf == 0:
                    pe.wait_ge(px_ready, 4 * p + 4)
                pe.wait_ge(v_read, 2 * p + hf + 1)
                for g in range(4 * hf, 4 * hf + 4):
                    for c in range(CT):
                        last = nc.tensor.matmul(bank(7)[:, (g % 4) * 128:(g % 4 + 1) * 128],
                                                wvT[:, c, g * D:(g + 1) * D], px[:, c, 2 * g:2 * g + 2, :],
                                                start=c == 0, stop=c == CT - 1)
                last.then_inc(v_full, 1)

            pe.wait_ge(wk_split, 1)
            pe.wait_ge(ld_wvT, 16)
            step(0, 0, prev=False)
            step(1, 1)
            with pe.Fori(1, 4) as i:
                step(2 * i, 0)
                step(2 * i + 1, 1, pair=i - 1)
            maxima(7)
            spread(7)
            mix(7, 1)
            project_out(0, range(NH), 4)
            values(3, 0)
            values(3, 1)
            project_out(1, range(8), 7)
            project_out(1, range(8, NH), 8)

        def loop_act(act, self_step):
            def split_A(b):
                if not (isinstance(b, int) and b == 0):
                    act.wait_ge(st_full, 4 * b)
                if isinstance(b, int):
                    part = A[:, b, :, :]
                else:
                    part = A[:, DS(b, 1), :, :].rearrange("p o c m -> p (o c) m")
                    nc.scalar.activation(nt[:, 27:28], ones[:, 0:1], ACT.Copy)
                nc.scalar.activation(A_hi, part, ACT.Copy).then_inc(A_hi_ready, 1)

            def split_context(b, k):
                act.wait_ge(ld_ctxT[k], 8 * (b - k) + 16)
                nc.scalar.activation(ctx_hi[k], ctxT[k], ACT.Copy).then_inc(ctx_hi_ready, 1)

            def step(b, k, prev=True, more=True):
                for t in range(KT):
                    n = 4 * b + t
                    k2 = t % 2
                    if not (prev is False and t < 2):
                        act.wait_ge(scaled, n - 1)
                    for hf in range(2):
                        act.wait_ge(kx_full, 2 * n + hf + 1)
                        if not (prev is False and t == 0):
                            act.wait_ge(sq_ready, 2 * n + hf - 1)
                        for g in range(4):
                            last = nc.scalar.activation(sq[:, (4 * hf + g) * D:(4 * hf + g + 1) * D], bank(hf)[:, g * D:(g + 1) * D], ACT.Square,
                                                        accum_out=ssq[:, k2, 4 * hf + g:4 * hf + g + 1])
                        last.then_inc(sq_ready, 1)
                        if prev and t == 1 and hf == 0:
                            spread_rows(b - 1)
                    act.wait_ge(sq_ready, 2 * n + 2)
                    self_step(nc.scalar.activation(krs0[:, k2, :], ssq[:, k2, :], ACT.Ln, scale=1.0 / D, bias=eps))
                    nc.scalar.activation(krs0[:, k2, :], krs0[:, k2, :], ACT.Exp, scale=-0.5)\
                        .then_inc(krstd_ready, 1)
                    if prev and t == 2:
                        exponentials(b - 1, 1 - k)
                    if more and t == 1:
                        split_context(b + 1, 1 - k)
                if more:
                    split_A(b + 1)
                if prev:
                    inverse(b - 1)

            def spread_rows(b):
                act.wait_ge(m_ready, b + 1)
                for j in range(4):
                    last = nc.scalar.activation(diag[:, j, :], ident, ACT.Copy, scale=mcol[:, j:j + 1])
                last.then_inc(diag_ready, 1)

            def exponentials(b, k):
                act.wait_ge(shifted, b + 1)
                nc.scalar.activation(sS[k], sS[k], ACT.Exp, scale=SCALE).then_inc(p_ready, 1)

            def inverse(b):
                act.wait_ge(sum_full, b + 1)
                self_step(nc.scalar.activation(R, bank(4), ACT.Ln))
                nc.scalar.activation(R, R, ACT.Exp, scale=-1.0).then_inc(r_ready, 1)

            split_A(0)
            step(0, 0, prev=False)
            step(1, 1)
            with act.Fori(1, 3) as i:
                self_step.loop(i, 1, 10)
                step(2 * i, 0)
                step(2 * i + 1, 1)
                self_step.over(2)
            step(6, 0)
            step(7, 1, more=False)
            act.wait_ge(ld_wpx, 16)
            act.wait_ge(st_full, 4 * B)
            for i in range(4):
                nc.scalar.activation(wpx_hi[:, 4 * i:4 * i + 4, :], wpx[:, 4 * i:4 * i + 4, :], ACT.Copy)\
                    .then_inc(wpx_hi_ready, 1)
            spread_rows(7)
            exponentials(7, 1)
            inverse(7)
            nc.scalar.activation(nt[:, 31:32], nt[:, 0:1], ACT.Copy).then_inc(loop_over, 1)

        def terms(e0, which):
            for q in which:
                n = 3 * e0 + q
                nc.vector.wait_ge(lut_added, n if q else n + 1)
                jc, jl = CONST["iota"].start + q // 3, COL["lut"].start + q // 3
                nc.vector.tensor_scalar(lutt[q % 2], idx[:, q % 3, :], consts[:, DS(e0 + jc, 1)],
                                        vec[:, DS(e0 + jl, 1)], ALU.is_equal, ALU.mult).then_inc(lut_term, 1)

        def add(e0, which):
            for q in which:
                n = 3 * e0 + q
                nc.gpsimd.wait_ge(lut_term, n + 1)
                if not (isinstance(e0, int) and n < 3) and q < 3:
                    nc.gpsimd.wait_ge(lut_added, n - 1)
                nc.gpsimd.tensor_tensor(lutw[:, q % 3, :], lutw[:, q % 3, :], lutt[q % 2], ALU.add)\
                    .then_inc(lut_added, 1)

        def loop_pool(pool, self_step):
            def lo_of_A(b):
                pool.wait_ge(A_hi_ready, b + 1)
                if isinstance(b, int):
                    part, lo = A[:, b, :, :], A_lo[:, b, :, :]
                else:
                    part, lo = (v[:, DS(b, 1), :, :].rearrange("p o c m -> p (o c) m") for v in (A, A_lo))
                    nc.gpsimd.tensor_tensor(nt[:, 28:29], ones[:, 0:1], ones[:, 0:1], ALU.mult)
                nc.gpsimd.tensor_tensor(lo, part, A_hi, ALU.subtract).then_inc(A_split, 1)

            def lo_of_context(b, k):
                pool.wait_ge(ctx_hi_ready, b + 1)
                nc.gpsimd.tensor_tensor(ctx_lo[k], ctxT[k], ctx_hi[k], ALU.subtract).then_inc(ctx_split, 1)

            def pack(m):
                pool.wait_ge(ld_idx[m], 16)
                nc.gpsimd.tensor_copy(idx[:, m, :], idx_raw[:, m % 2, :]).then_inc(idx_ready, 1)

            lo_of_A(0)
            pack(0)
            lo_of_context(1, 1)
            pack(1)
            lo_of_A(1)
            pack(2)
            pool.wait_ge(idx_ready, 3)
            nc.gpsimd.memset(nt[:, 30:31], 0.0).then_inc(lut_added, 1)

            def sums(b, k):
                pool.wait_ge(p_ready, b + 1)
                if not (isinstance(b, int) and b == 0):
                    pool.wait_ge(sum_full, b)
                self_step(nc.gpsimd.tensor_tensor(ps2, sS[k][:, 0:2, :], sS[k][:, 2:4, :], ALU.add))
                nc.gpsimd.tensor_tensor(ps2[:, 0, :], ps2[:, 0, :], ps2[:, 1, :], ALU.add).then_inc(psum_ready, 1)

            def step(b, k, e0, more=True):
                add(e0, range(4 * k, 4 * k + 1))
                if more:
                    lo_of_context(b + 1, 1 - k)
                sums(b - 1, 1 - k)
                add(e0, range(4 * k + 1, 4 * k + 2))
                if more:
                    lo_of_A(b + 1)
                add(e0, range(4 * k + 2, 9 if k else 4))

            lo_of_context(2, 0)
            sums(0, 0)
            pool.wait_ge(lut_zero, 1)
            lo_of_A(2)
            add(0, range(3))
            with pool.Fori(1, 3) as i:
                self_step.loop(i, 1, 2)
                step(2 * i, 0, 3 * i - 2)
                step(2 * i + 1, 1, 3 * i - 2)
                self_step.over(2)
            step(6, 0, 7)
            step(7, 1, 7, more=False)
            add(10, range(0, 2))
            sums(7, 1)
            add(10, range(2, 6))
            self_step(nc.gpsimd.memset(nt[:, 30:31], 0.0))
            nc.gpsimd.memset(nt[:, 30:31], 0.0).then_inc(loop_over, 1)

        def loop_dve(dve, self_step):
            def step(b, k, pair=None, prev=True):
                for t in range(KT):
                    n = 4 * b + t
                    dve.wait_ge(sq_ready, 2 * n + 2)
                    self_step(nc.vector.tensor_scalar(kvar, ssq[:, t % 2, :], 1.0 / D, EPS, ALU.mult, ALU.add))
                    dve.wait_ge(krstd_ready, n + 1)
                    newton(dve, self_step, krs, krs0[:, t % 2, :], kvar, knt)
                    dve.wait_ge(st_full, n + 1)
                    if t == 0 and prev and not (isinstance(b, int) and b < 2):
                        dve.wait_ge(pctx, 2 * b - 2)
                    nc.vector.tensor_tensor(sS[k][:, t, :].rearrange("p (g q) -> p g q", g=G), bank(2 + t % 2, G, 64),
                                            krs.unsqueeze(2).broadcast_to([128, G, 64]), ALU.mult)\
                        .then_inc(scaled, 1)
                    if prev and t == 0:
                        maxima(b - 1)
                    if pair is not None and t == 1:
                        read_values(pair, 0)
                    if prev and t == 1:
                        shift(b - 1, 1 - k)
                    if pair is not None and t == 3:
                        read_values(pair, 1)
                    if pair is not None and t in (1, 3):
                        quantize_values(pair, t // 2)
                    if prev:
                        table_terms(b, k, t)
                dve.wait_ge(scaled, 4 * b + 4)
                if prev:
                    dve.wait_ge(tr_full, b)
                nc.vector.tensor_reduce(mx, sS[k].rearrange("p t q -> p q t"), AX, ALU.max).then_inc(mx_ready, 1)
                dve.wait_ge(mx_ready, b + 1)
                nc.vector.tensor_tensor(mx, mx, beta[:, :, DS(b * S, S)], ALU.add).then_inc(mxf_ready, 1)
                if prev:
                    table_terms(b, k, 4)
                if prev:
                    normalise(b - 1, 1 - k)
                if prev:
                    table_terms(b, k, 5)

            def table_terms(b, k, at):
                if isinstance(b, int):
                    if at > 2:
                        terms(0, range(at - 3, at - 2))
                elif k == 0:
                    if at in (0, 2, 3, 4):
                        terms(turn_entry, range(max(at - 1, 0), max(at, 1)))
                elif at != 1:
                    terms(turn_entry, range(4 + max(at - 1, 0), 5 + max(at - 1, 0)))

            def maxima(b):
                dve.wait_ge(tr_full, b + 1)
                nc.vector.tensor_reduce(mcol, bank(4, 4, 128), AX, ALU.max).then_inc(m_ready, 1)

            def shift(b, k):
                dve.wait_ge(mb_full, b + 1)
                self_step(nc.vector.tensor_tensor(nm.rearrange("p (a q) -> p a q", a=NH), bank(4, NH, S),
                                                  beta[:, :, DS(b * S, S)], ALU.subtract))
                nc.vector.tensor_tensor(sS[k], sS[k], nm.unsqueeze(1).broadcast_to([128, KT, 512]), ALU.subtract)\
                    .then_inc(shifted, 1)

            def normalise(b, k):
                dve.wait_ge(r_ready, b + 1)
                self_step(nc.vector.scalar_tensor_tensor(nm, bank(4), -1.0, R, ALU.mult, ALU.mult))
                self_step(nc.vector.scalar_tensor_tensor(R, nm, 2.0, R, ALU.add, ALU.mult))
                dve.wait_ge(pctx, 2 * b + 2)
                if k == 0 and not (isinstance(b, int) and b == 0):
                    dve.wait_ge(v_full, b)
                for c in range(CT):
                    nc.vector.tensor_tensor(px[:, c, :, k * S:(k + 1) * S], bank(5 + c, NH, S),
                                            R.rearrange("p (a q) -> p a q", a=NH), ALU.mult).then_inc(px_ready, 1)

            def read_values(p, hf):
                dve.wait_ge(v_full, 2 * p + hf + 1)
                src = bank(7, 8, 64)
                y = y_q.rearrange("p (a q) -> p a q", a=8)
                nc.vector.tensor_tensor(y, src, inv_smooth[:, NH + 8 * hf:NH + 8 * hf + 8].unsqueeze(2)
                                        .broadcast_to([128, 8, 64]), ALU.mult).then_inc(v_read, 1)

            def quantize_values(p, hf):
                heads = slice(8 * hf, 8 * hf + 8)
                dve.wait_ge(v_read, 2 * p + hf + 2)
                self_step(nc.vector.tensor_scalar(y_q, y_q, FP8_MAX, -FP8_MAX, ALU.min, ALU.max))
                dst = catx[:, heads, DS(2 * S * p, 2 * S)]
                self_step(nc.vector.tensor_scalar(e_q.bitcast(u16), y_q.bitcast(u16), 0x7F80,
                                                  None, ALU.bitwise_and))
                self_step(nc.vector.tensor_scalar(m_q, e_q, FP8_MIN_NORMAL, ROUND, ALU.max,
                                                  ALU.mult))
                self_step(nc.vector.tensor_tensor(t_q, y_q, m_q, ALU.add))
                nc.vector.tensor_tensor(dst, t_q.rearrange("p (a q) -> p a q", a=8),
                                        m_q.rearrange("p (a q) -> p a q", a=8), ALU.subtract)\
                    .then_inc(catx_ready, 1)

            dve.wait_ge(front_over, 4)
            nc.vector.memset(nt[:, 29:30], 0.0).then_inc(v_read, 1)
            nc.vector.memset(lutw, 0.0).then_inc(lut_zero, 1)
            step(0, 0, prev=False)
            step(1, 1)
            with dve.Fori(1, 4) as i:
                self_step.loop(i, 1, 2 * (16 + 3) + 8)
                turn_entry = 3 * i - 2
                step(2 * i, 0)
                step(2 * i + 1, 1, pair=i - 1)
                self_step.over(3)
            self_step(nc.vector.tensor_tensor(pscale, col("proj_w_scale"), col("proj_in_scale"), ALU.mult))
            self_step(nc.vector.scalar_tensor_tensor(x, core, pscale, x, ALU.mult, ALU.add))
            maxima(7)
            terms(10, range(0, 2))
            shift(7, 1)
            for i in range(4):
                dve.wait_ge(wpx_hi_ready, i + 1)
                nc.vector.tensor_tensor(wpx_lo[:, 4 * i:4 * i + 4, :], wpx[:, 4 * i:4 * i + 4, :],
                                        wpx_hi[:, 4 * i:4 * i + 4, :], ALU.subtract).then_inc(wpx_split, 1)
            terms(10, range(2, 4))
            dve.wait_ge(r_ready, 8)
            dve.wait_ge(pctx, 16)
            dve.wait_ge(v_full, 6)
            for hf in range(2):
                m = slice(256 * hf, 256 * hf + 256)
                self_step(nc.vector.scalar_tensor_tensor(nm[:, m], bank(4)[:, m], -1.0, R[:, m], ALU.mult, ALU.mult))
                self_step(nc.vector.scalar_tensor_tensor(R[:, m], nm[:, m], 2.0, R[:, m], ALU.add, ALU.mult))
                for c in range(CT):
                    last = nc.vector.tensor_tensor(px[:, c, 8 * hf:8 * hf + 8, S:2 * S],
                                                   bank(5 + c, NH, S)[:, 8 * hf:8 * hf + 8, :],
                                                   R[:, m].rearrange("p (a q) -> p a q", a=8), ALU.mult)
                last.then_inc(px_ready, 1)
            for hf in range(2):
                read_values(3, hf)
                quantize_values(3, hf)
                if hf == 0:
                    terms(10, range(4, 5))
                    dve.wait_ge(proj_out, 1)
                    nc.vector.scalar_tensor_tensor(x[:, 0, :], bank(0)[:, 0:C], pscale, x[:, 0, :], ALU.mult, ALU.add)
            terms(10, range(5, 6))
            dve.wait_ge(catx_ready, 8)
            nc.vector.memset(nt[:, 29:30], 0.0).then_inc(loop_over, 1)

        keysT_all, keys_all = buf("keysT", CT, B, NK), buf("keys", B, KT, C)
        o_ = [0]

        def ssm(*dims):
            n = 1
            for d in dims:
                n *= d
            view = buf("ssm", *dims, skip=o_[0])
            o_[0] += n
            return view

        w_ssm, w_ssmo = ssm(CT, 4 * SSM), ssm(C)[0:SSM, :]
        hpad, xc, diagD = ssm(CT, B, S + 3), ssm(CT, T), ssm(CT, 128)
        sx, sy, sz, su, sa = (ssm(T)[0:SSM, :] for _ in range(5))
        wr = ssm(CT, NE)
        assert o_[0] <= 5200, o_
        wgu = [buf("gateup", 2, CT * C, skip=2 * k * CT * C) for k in range(2)]
        wdn = buf("down", NE, CT * C)
        sg = [buf("moe", CT * T, skip=2 * k * CT * T) for k in range(2)]
        am = [buf("moe", CT, T, skip=(2 * k + 1) * CT * T) for k in range(2)]
        mask = buf("mask", TT, NK)
        negm = buf("mask", TT, NK, skip=TT * NK)
        mask_u8 = buf("maskraw", TT, NK, dtype=u8)
        mask_raw = buf("maskraw", TT, NK // 4, dtype=i32)
        pr = buf("probs", TT, NK)
        pT = buf("probs", TT, KT * 128, skip=TT * NK)
        r_ = [0]

        def rot(*dims):
            n = 1
            for d in dims:
                n *= d
            view = buf("rot", *dims, skip=r_[0])
            r_[0] += n
            return view

        wq_r, wk_r, wv_r, wo_r = rot(2 * CT, 512), rot(2 * CT, 128), rot(CT, 128), rot(4, C)
        qr, qt2 = buf("rotact", 4, T), buf("rotact", 4, T, skip=1024)
        kr, kt2 = buf("rotact", T, skip=2048), buf("rotact", T, skip=2304)
        vr = buf("rotact", TT, 128, skip=2560)
        rs_ = buf("probs", 32, 32)
        rp_ = buf("rotact", 32, 32, skip=3072)
        oT = buf("probs", 4, T, skip=1024)
        sgf, hm = buf("ffn", IT, T), buf("ffn", IT, T, skip=IT * T)
        ld_w = {n: sem("ld_" + n) for n in ("ssm", "keysT", "keys", "mask", "rot")}
        ld_e, ld_down = [sem("ld_experts0"), sem("ld_experts1")], sem("ld_down")
        x_ready, turned, hT_ready, diag_d, hpad_zero = (sem(n) for n in (
            "x_ready", "turned", "hT_ready", "diag_d", "hpad_zero"))
        ssm_p, conv_ready, ssm_x, soft_in, soft_out, decay, hm_ready, ssm_out_full = (sem(n) for n in (
            "ssm_p", "conv_ready", "ssm_x", "soft_in", "soft_out", "decay", "hm_ready", "ssm_out_full"))
        route_full, gap_ready, gap_exp, gu_full, silu_ready, act_ready, down_full, moe_added = (sem(n) for n in (
            "route_full", "gap_ready", "gap_exp", "gu_full", "silu_ready", "act_ready", "down_full", "moe_added"))
        mask_ready, sc_full, sc_shift, sc_exp, pt_full, pt_ready, read_full = (sem(n) for n in (
            "mask_ready", "sc_full", "sc_shift", "sc_exp", "pt_full", "pt_ready", "read_full"))
        qkv_full, rot_ready, v_ready, rsc_full, rsc_shift, rsc_exp, rp_ready, rmix_full, oT_ready, wo_full = (
            sem(n) for n in ("qkv_full", "rot_ready", "v_ready", "rsc_full", "rsc_shift", "rsc_exp", "rp_ready",
                             "rmix_full", "oT_ready", "wo_full"))
        ffn_full, ffn_silu, ffn_ready, ffn_out, stored = (sem(n) for n in (
            "ffn_full", "ffn_silu", "ffn_ready", "ffn_out", "stored"))
        oT_ready_act = sem("oT_ready_act")
        XC = {"proj": 1, "ssm": 2, "moe": 3, "read": 4, "rot": 5, "ffn": 6}

        def tail_sync(sp):
            sp.wait_ge(loop_over, 3)
            sp.dma_start(w_ssm, io["ssm_in"]).then_inc(ld_w["ssm"], 16)
            sp.dma_start(w_ssmo, io["ssm_out"]).then_inc(ld_w["ssm"], 16)
            sp.dma_start(wr, io["router"]).then_inc(ld_w["ssm"], 16)
            for k in range(2):
                sp.dma_start(wgu[k], io["gate_up"][k]).then_inc(ld_e[k], 16)
            for j in range(TT):
                for b4 in range(4):
                    sp.dma_start(mask_raw[32 * b4:32 * b4 + 32, j, :],
                                 io["mask"][4 * j + b4:4 * j + b4 + 1, :].broadcast_to([32, NK // 4])).then_inc(ld_w["mask"], 16)
            sp.dma_start(wdn, io["down"]).then_inc(ld_down, 16)
            sp.wait_ge(proj_out, 2)
            for b in range(B):
                sp.dma_start(keysT_all[:, :, b, :], io["ctxT"][b]).then_inc(ld_w["keysT"], 16)
            for b in range(2):
                sp.dma_start(keys_all[:, b, :, :], io["ctx"][b]).then_inc(ld_w["keys"], 16)

            def load_expert(e, k):
                sp.wait_ge(gu_full, 2 * e - 2)
                sp.dma_start(wgu[k], io["gate_up"][DS(e, 1)].rearrange("o p a n -> (o p) a n"))\
                    .then_inc(ld_e[k], 16)

            with sp.Fori(1, 4) as i:
                for k in range(2):
                    load_expert(2 * i + k, k)
                    sp.dma_start(keys_all[:, DS(2 * i + k, 1), :, :].rearrange("p o t c -> p (o t) c"),
                                 io["ctx"][DS(2 * i + k, 1)].rearrange("o p t c -> (o p) t c")).then_inc(ld_w["keys"], 16)
            sp.wait_ge(x_ready, XC["moe"])
            sp.dma_start(wq_r.rearrange("p (a c) n -> p a c n", a=2), io["wq_rot"]).then_inc(ld_w["rot"], 16)
            sp.dma_start(wk_r.rearrange("p (a c) n -> p a c n", a=2), io["wk_rot"]).then_inc(ld_w["rot"], 16)
            sp.dma_start(wv_r, io["wv_rot"]).then_inc(ld_w["rot"], 16)
            sp.dma_start(wo_r, io["wo_rot"]).then_inc(ld_w["rot"], 16)
            for j in range(TT):
                sp.wait_ge(x_ready, XC["ffn"] + j)
                sp.dma_start(out[:, j, :], x[:, j, :]).then_inc(stored, 16)
            sp.wait_ge(stored, 16 * TT)

        def tail_pe(pe):
            def turn_norm(k, nb):
                pe.wait_ge(ln_done, k + 1)
                o = bank(nb, CT, T)
                for i in range(4):
                    j, c = i // CT, i % CT
                    last = nc.tensor.transpose(o[:, c, j * 128:j * 128 + 128], h[:, j, c * 128:c * 128 + 128], ident)
                last.then_inc(turned, 1)

            turn_norm(1, 1)
            pe.wait_ge(ld_w["ssm"], 48)
            pe.wait_ge(hT_ready, 1)
            for i in (2, 0, 1):
                o = bank(2 + i // 2)[0:SSM, (i % 2) * T:(i % 2) * T + T]
                for c in range(CT):
                    last = nc.tensor.matmul(o, w_ssm[:, c, i * SSM:(i + 1) * SSM], hpad[:, c, :, 3:S + 3],
                                            start=c == 0, stop=c == CT - 1)
                if i != 0:
                    last.then_inc(ssm_p, 1)
            pe.wait_ge(conv_ready, 1)
            for c in range(CT):
                last = nc.tensor.matmul(bank(4)[0:SSM, 0:T], w_ssm[:, c, 3 * SSM:4 * SSM], xc[:, c, :],
                                        start=c == 0, stop=c == CT - 1)
            last.then_inc(ssm_x, 1)
            pe.wait_ge(diag_d, 1)
            pe.wait_ge(hm_ready, 1)
            o = bank(5, TT, C)
            for j in range(TT):
                nc.tensor.matmul(o[:, j, :], sz[:, j * 128:j * 128 + 128], w_ssmo, start=True, stop=False,
                                 skip_group_check=True)
                for c in range(CT):
                    last = nc.tensor.matmul(o[:, j, c * 128:c * 128 + 128], xc[:, c, j * 128:j * 128 + 128],
                                            diagD[:, c, :], start=False, stop=c == CT - 1, skip_group_check=True)
            last.then_inc(ssm_out_full, 1)
            turn_norm(2, 6)
            pe.wait_ge(hT_ready, 2)
            o = bank(7, TT, NE)
            for j in range(TT):
                for c in range(CT):
                    last = nc.tensor.matmul(o[:, j, :], hT[:, c, j * 128:j * 128 + 128], wr[:, c, :],
                                            start=c == 0, stop=c == CT - 1)
            last.then_inc(route_full, 1)

            def gate_up(e, k):
                pe.wait_ge(ld_e[k], 8 * (e - k) + 16)
                if not (isinstance(e, int) and e < 2):
                    pe.wait_ge(act_ready, e - 1)
                for i in range(2):
                    o = bank(2 * k + i, CT, T)
                    for m in range(CT):
                        for c in range(CT):
                            w0 = c * C + m * 128
                            last = nc.tensor.matmul(o[:, m, :], wgu[k][:, i, w0:w0 + 128], hT[:, c, :],
                                                    start=c == 0, stop=c == CT - 1)
                    last.then_inc(gu_full, 1)

            def down(e, k):
                pe.wait_ge(act_ready, e + 1)
                if not (isinstance(e, int) and e == 0):
                    pe.wait_ge(moe_added, e)
                o = bank(4 + k, TT, C)
                for j in range(TT):
                    for m in range(CT):
                        last = nc.tensor.matmul(o[:, j, :], am[k][:, m, j * 128:j * 128 + 128],
                                                wdn[:, DS(e, 1), m * C:(m + 1) * C] if not isinstance(e, int) else
                                                wdn[:, e, m * C:(m + 1) * C],
                                                start=m == 0, stop=m == CT - 1)
                last.then_inc(down_full, 1)

            gate_up(0, 0)
            gate_up(1, 1)
            pe.wait_ge(ld_down, 16)
            down(0, 0)
            with pe.Fori(1, 4) as i:
                gate_up(2 * i, 0)
                down(2 * i - 1, 1)
                gate_up(2 * i + 1, 1)
                down(2 * i, 0)
            down(7, 1)
            turn_norm(3, 6)
            pe.wait_ge(hT_ready, 3)
            pe.wait_ge(ld_w["keysT"], 16 * B)
            for b in range(B):
                q0 = 32 * (b % 4)
                for c in range(CT):
                    last = nc.tensor.matmul(bank(b // 4)[q0:q0 + 32, :], hT[:, c, b * S:b * S + S], keysT_all[:, c, b, :],
                                            start=c == 0, stop=c == CT - 1)
                if b % 4 == 3:
                    last.then_inc(sc_full, 1)
            pe.wait_ge(ld_w["keys"], 16 * B)
            for b in range(B):
                j, q0 = b // 4, 32 * (b % 4)
                if q0 == 0:
                    pe.wait_ge(sc_exp, j + 1)
                    for t in range(KT):
                        last = nc.tensor.transpose(bank(2 + j, KT, 128)[:, t, :], pr[:, j, t * 128:t * 128 + 128],
                                                   ident)
                    last.then_inc(pt_full, 1)
                    pe.wait_ge(pt_ready, j + 1)
                for t in range(KT):
                    last = nc.tensor.matmul(bank(4 + j)[q0:q0 + 32, 0:C], pT[:, j, t * 128 + q0:t * 128 + q0 + 32],
                                            keys_all[:, b, t, :], start=t == 0, stop=t == KT - 1)
            last.then_inc(read_full, 1)
            turn_norm(4, 6)
            pe.wait_ge(hT_ready, 4)
            pe.wait_ge(ld_w["rot"], 64)
            for i in range(5):
                o = bank(i, 2, T)
                for sw in range(2):
                    for c in range(CT):
                        w = wq_r[:, sw * CT + c, i * 128:i * 128 + 128] if i < 4 else wk_r[:, sw * CT + c, :]
                        last = nc.tensor.matmul(o[:, sw, :], w, hT[:, c, :], start=c == 0, stop=c == CT - 1)
                last.then_inc(qkv_full, 1)
            o = bank(5, TT, 128)
            for j in range(TT):
                for c in range(CT):
                    last = nc.tensor.matmul(o[:, j, :], hT[:, c, j * 128:j * 128 + 128], wv_r[:, c, :],
                                            start=c == 0, stop=c == CT - 1)
            last.then_inc(qkv_full, 1)
            pe.wait_ge(rot_ready, 1)
            for g in range(4):
                for b in range(B):
                    q0 = 32 * (b % 4)
                    last = nc.tensor.matmul(bank(g)[q0:q0 + 32, (b // 4) * 128:(b // 4) * 128 + 128],
                                            kr[32 * g:32 * g + 32, b * S:b * S + S],
                                            qr[32 * g:32 * g + 32, :, b * S:b * S + S], start=True, stop=True)
                if g % 2:
                    last.then_inc(rsc_full, 1)
            pe.wait_ge(v_ready, 1)
            rpv = rs_.rearrange("p (g j a) q -> p g j (a q)", g=4, j=TT)
            for half in range(2):
                pe.wait_ge(rp_ready, half + 1)
                for b4 in range(4):
                    q0 = 32 * b4
                    for j in range(TT):
                        for g in (2 * half, 2 * half + 1):
                            last = nc.tensor.matmul(bank(4 + b4)[32 * g:32 * g + 32, j * 128:j * 128 + 128],
                                                    vr[q0:q0 + 32, j, 32 * g:32 * g + 32], rpv[q0:q0 + 32, g, j, :],
                                                    start=True, stop=True)
            last.then_inc(rmix_full, 1)
            pe.wait_ge(oT_ready, 1)
            pe.wait_ge(oT_ready_act, 1)
            o = bank(0, TT, C)
            for j in range(TT):
                for a in range(4):
                    last = nc.tensor.matmul(o[:, j, :], oT[:, a, j * 128:j * 128 + 128], wo_r[:, a, :],
                                            start=a == 0, stop=a == 3)
            last.then_inc(wo_full, 1)
            turn_norm(5, 6)
            pe.wait_ge(hT_ready, 5)
            pe.wait_ge(lut_added, 3 * LUTN + 1)
            for i in range(IT // 2):
                for m in range(2):
                    o = bank(2 * i + m, 2, T)
                    for a in range(2):
                        for c in range(CT):
                            w0 = c * IPAD + (2 * i + a) * 128
                            last = nc.tensor.matmul(o[:, a, :], lutw[:, m, w0:w0 + 128], hT[:, c, :],
                                                    start=c == 0, stop=c == CT - 1)
                    last.then_inc(ffn_full, 1)
            for j in range(TT):
                o = bank(6 + j, TT, C)
                for i in range(IT):
                    if j == 0 and i % 2 == 0:
                        pe.wait_ge(ffn_ready, i // 2 + 1)
                    last = nc.tensor.matmul(o[:, j, :], hm[:, i, j * 128:j * 128 + 128],
                                            lutw[:, 2, i * C:(i + 1) * C], start=i == 0, stop=i == IT - 1)
                last.then_inc(ffn_out, 1)

        def turn_heads(copy, quadrants, done):
            for b4 in quadrants:
                src = bank(4 + b4, TT, 4, S)
                dst = oT.rearrange("p a (j q) -> p j a q", j=TT)[:, :, :, 32 * b4:32 * b4 + 32]
                for j in range(TT):
                    last = copy(dst[:, j], src[:, j])
            last.then_inc(done, 1)

        def tail_act(act, step):
            act.wait_ge(loop_over, 3)
            act_rstd(act, step, TT, 7)
            step(nc.scalar.activation(negA[0:SSM, :], col("a_log")[0:SSM, :], ACT.Exp))
            step(nc.scalar.activation(negA[0:SSM, :], negA[0:SSM, :], ACT.Copy, scale=-1.0))
            act.wait_ge(ssm_p, 1)
            nc.scalar.activation(sx, bank(3)[0:SSM, 0:T], ACT.Copy).then_inc(soft_in, 1)
            act.wait_ge(soft_in, 2)
            step(nc.scalar.activation(sy, sy, ACT.Exp))
            step(nc.scalar.activation(sy, sy, ACT.Ln, bias=ones[0:SSM, 0:1]))
            nc.scalar.activation(sa, sx, ACT.Copy).then_inc(soft_out, 1)
            act.wait_ge(soft_in, 3)
            nc.scalar.activation(sa, sx, ACT.Exp, scale=negA[0:SSM, :]).then_inc(decay, 1)
            act_rstd(act, step, TT, 8)
            act.wait_ge(gap_ready, 1)
            nc.scalar.activation(gate2[:, 0, :], gate2[:, 1, :], ACT.Exp).then_inc(gap_exp, 1)

            def silu(e, k):
                act.wait_ge(gu_full, 2 * e + 1)
                if not (isinstance(e, int) and e < 2):
                    act.wait_ge(act_ready, e - 1)
                nc.scalar.activation(sg[k], bank(2 * k), ACT.Silu).then_inc(silu_ready, 1)

            nc.scalar.preload_act_table(ACT.Silu)
            silu(0, 0)
            silu(1, 1)
            with act.Fori(1, 4) as i:
                silu(2 * i, 0)
                silu(2 * i + 1, 1)
            nc.scalar.preload_act_table_set("natural_log_exp_and_others")
            act_rstd(act, step, TT, 9)
            for j in range(TT):
                act.wait_ge(sc_shift, j + 1)
                nc.scalar.activation(pr[:, j, :], pr[:, j, :], ACT.Exp, bias=amax[:, j:j + 1],
                                     accum_out=asum[:, j:j + 1]).then_inc(sc_exp, 1)
                act.wait_ge(pt_full, j + 1)
                nc.scalar.activation(pT[:, j, :], bank(2 + j), ACT.Copy).then_inc(pt_ready, 1)
            act_rstd(act, step, TT, 10)
            act.wait_ge(qkv_full, 6)
            nc.scalar.activation(vr, bank(5, TT, 128), ACT.Copy).then_inc(v_ready, 1)
            for half in range(2):
                act.wait_ge(rsc_shift, half + 1)
                r = rs_[:, 16 * half:16 * half + 16, :]
                nc.scalar.activation(r, r, ACT.Exp, scale=0.25).then_inc(rsc_exp, 1)
            act.wait_ge(rmix_full, 1)
            turn_heads(nc.scalar.copy, (2, 3), oT_ready_act)
            act_rstd(act, step, TT, 11)
            nc.scalar.preload_act_table(ACT.Silu)
            for i in range(IT // 2):
                act.wait_ge(ffn_full, 2 * i + 1)
                nc.scalar.activation(sgf[:, 2 * i:2 * i + 2, :], bank(2 * i, 2, T), ACT.Silu).then_inc(ffn_silu, 1)

        def tail_pool(pool, step):
            pool.wait_ge(loop_over, 3)
            nc.gpsimd.memset(hpad[:, :, :, 0:3], 0.0).then_inc(hpad_zero, 1)
            for c in range(CT):
                last = nc.gpsimd.tensor_tensor(diagD[:, c, :], ident, col("ssm_d", c).broadcast_to([128, 128]), ALU.mult)
            last.then_inc(diag_d, 1)
            pool.wait_ge(ld_w["mask"], 16 * B)
            step(nc.gpsimd.tensor_copy(mask, mask_u8))
            nc.gpsimd.tensor_scalar(negm, mask, -1.0, 1e30, ALU.add, ALU.mult).then_inc(mask_ready, 1)
            with pool.Fori(1, 4) as i:
                add(i + 11, range(3))
            add(15, range(3))

        def tail_dve(dve, step):
            def norm(k):
                dve.wait_ge(x_ready, k)
                token_norm(dve, step, x, h, 6 + k).then_inc(ln_done, 1)
                dve.wait_ge(turned, k)

            dve.wait_ge(proj_out, 2)
            nc.vector.scalar_tensor_tensor(x[:, 1, :], bank(1)[:, 0:C], pscale, x[:, 1, :], ALU.mult, ALU.add)\
                .then_inc(x_ready, 1)
            norm(1)
            dve.wait_ge(loop_over, 3)
            dve.wait_ge(hpad_zero, 1)
            o = bank(1, CT, T)
            for c in range(CT):
                last = nc.vector.tensor_copy(hpad[:, c, :, 3:S + 3], o[:, c, :].rearrange("p (b s) -> p b s", b=B))
            last.then_inc(hT_ready, 1)
            dve.wait_ge(hT_ready, 1)
            xcv = xc.rearrange("p c (b s) -> p c b s", b=B)
            for c in range(CT):
                last = nc.vector.tensor_scalar(xcv[:, c], hpad[:, c, :, 0:S], col("conv_w", 4 * c), col("conv_b", c),
                                               ALU.mult, ALU.add)
            step(last)
            for k in range(1, 4):
                for c in range(CT):
                    last = nc.vector.scalar_tensor_tensor(xcv[:, c], hpad[:, c, :, k:S + k], col("conv_w", 4 * c + k),
                                                          xcv[:, c], ALU.mult, ALU.add)
                if k < 3:
                    step(last)
                if k == 1:
                    dve.wait_ge(soft_in, 1)
                    nc.vector.scalar_tensor_tensor(sy, sx, -1.0, sx, ALU.mult, ALU.min).then_inc(soft_in, 1)
            last.then_inc(conv_ready, 1)
            dve.wait_ge(soft_out, 1)
            nc.vector.scalar_tensor_tensor(sx, sx, 0.0, sy, ALU.max, ALU.add).then_inc(soft_in, 1)
            dve.wait_ge(soft_in, 3)
            dve.wait_ge(ssm_p, 2)
            step(nc.vector.tensor_tensor(su, sx, bank(2)[0:SSM, 0:T], ALU.mult))
            dve.wait_ge(ssm_x, 1)
            step(nc.vector.tensor_tensor(su, su, bank(4)[0:SSM, 0:T], ALU.mult))
            dve.wait_ge(decay, 1)
            step(nc.vector.memset(sa.rearrange("p (b s) -> p b s", b=B)[:, :, 0:1], 0.0))
            step(nc.vector.tensor_tensor_scan(sy, sa, su, 0.0, ALU.mult, ALU.add))
            nc.vector.tensor_tensor(sz, sy, bank(2)[0:SSM, T:2 * T], ALU.mult).then_inc(hm_ready, 1)
            dve.wait_ge(ssm_out_full, 1)
            nc.vector.tensor_tensor(x, x, bank(5, TT, C), ALU.add).then_inc(x_ready, 1)
            norm(2)
            nc.vector.tensor_copy(hT, bank(6, CT, T)).then_inc(hT_ready, 1)
            dve.wait_ge(route_full, 1)
            iota = const("iota")[:, 0:NE].unsqueeze(1).broadcast_to([128, TT, NE])
            step(nc.vector.tensor_scalar(iota8, iota, float(NE), None, ALU.add))
            step(nc.vector.tensor_copy(logit, bank(7, TT, NE)))

            def over(a):
                return a.unsqueeze(2).broadcast_to([128, TT, NE])

            for k in range(2):
                step(nc.vector.tensor_reduce(top[:, k, :], logit, AX, ALU.max))
                step(nc.vector.tensor_tensor(eq, logit, over(top[:, k, :]), ALU.is_equal))
                step(nc.vector.scalar_tensor_tensor(cand, eq, -float(NE), iota8, ALU.mult, ALU.add))
                step(nc.vector.tensor_reduce(best[:, k, :], cand, AX, ALU.min))
                step(nc.vector.tensor_tensor(oh[k], cand, over(best[:, k, :]), ALU.is_equal))
                if k == 0:
                    step(nc.vector.scalar_tensor_tensor(logit, oh[k], -3.0e38, logit, ALU.mult, ALU.add))
            nc.vector.tensor_tensor(gate2[:, 1, :], top[:, 1, :], top[:, 0, :], ALU.subtract).then_inc(gap_ready, 1)
            dve.wait_ge(gap_exp, 1)
            step(nc.vector.tensor_scalar(gate2[:, 1, :], gate2[:, 0, :], 1.0, None, ALU.add))
            step(nc.vector.reciprocal(prob[:, 0, :], gate2[:, 1, :]))
            step(nc.vector.tensor_tensor(prob[:, 1, :], prob[:, 0, :], gate2[:, 0, :], ALU.mult))
            step(nc.vector.tensor_tensor(mixw, oh[0], over(prob[:, 0, :]), ALU.mult))
            step(nc.vector.tensor_tensor(mixt, oh[1], over(prob[:, 1, :]), ALU.mult))
            nc.vector.tensor_tensor(mixw, mixw, mixt, ALU.add).then_inc(moe_added, 1)

            def activate(e, k):
                dve.wait_ge(silu_ready, e + 1)
                step(nc.vector.tensor_scalar(sg[k], sg[k], 7.0, -7.0, ALU.min, ALU.max))
                dve.wait_ge(gu_full, 2 * e + 2)
                if not (isinstance(e, int) and e < 2):
                    dve.wait_ge(down_full, e - 1)
                nc.vector.tensor_tensor(am[k], sg[k].rearrange("p (m t) -> p m t", m=CT), bank(2 * k + 1, CT, T),
                                        ALU.mult).then_inc(act_ready, 1)

            def add_expert(e, k):
                dve.wait_ge(down_full, e + 1)
                dve.wait_ge(moe_added, e + 1)
                o = bank(4 + k, TT, C)
                for j in range(TT):
                    last = nc.vector.scalar_tensor_tensor(x[:, j, :], o[:, j, :],
                                                          mixw.rearrange("p j e -> p (j e)")[:, DS(e + j * NE, 1)],
                                                          x[:, j, :], ALU.mult, ALU.add)
                last.then_inc(moe_added, 1)

            activate(0, 0)
            activate(1, 1)
            dve.wait_ge(mask_ready, 1)
            step(nc.vector.tensor_reduce(attends, mask, AX, ALU.max))
            add_expert(0, 0)
            with dve.Fori(1, 4) as i:
                step.loop(i, 1, 2)
                activate(2 * i, 0)
                terms(i + 11, range(0, 1))
                add_expert(2 * i - 1, 1)
                terms(i + 11, range(1, 2))
                activate(2 * i + 1, 1)
                terms(i + 11, range(2, 3))
                add_expert(2 * i, 0)
                step.over(3)
            add_expert(7, 1)
            dve.wait_ge(moe_added, 9)
            nc.vector.memset(nt[:, 29:30], 0.0).then_inc(x_ready, 1)
            norm(3)
            nc.vector.tensor_copy(hT, bank(6, CT, T)).then_inc(hT_ready, 1)
            terms(15, range(0, 2))
            for j in range(TT):
                dve.wait_ge(sc_full, j + 1)
                step(nc.vector.scalar_tensor_tensor(pr[:, j, :], bank(j), C ** -0.5, negm[:, j, :], ALU.mult, ALU.add))
                nc.vector.tensor_reduce(amax[:, j:j + 1], pr[:, j, :], AX, ALU.max, negate=True).then_inc(sc_shift, 1)
            terms(15, range(2, 3))
            dve.wait_ge(sc_exp, 2)
            step(nc.vector.reciprocal(asum[:, 0:TT], asum[:, 0:TT]))
            step(nc.vector.tensor_tensor(asum[:, 0:TT], asum[:, 0:TT], attends, ALU.mult))
            dve.wait_ge(read_full, 1)
            for j in range(TT):
                last = nc.vector.scalar_tensor_tensor(x[:, j, :], bank(4 + j)[:, 0:C], asum[:, j:j + 1], x[:, j, :],
                                                      ALU.mult, ALU.add)
            last.then_inc(x_ready, 1)
            norm(4)
            nc.vector.tensor_copy(hT, bank(6, CT, T)).then_inc(hT_ready, 1)
            cos, sin = const("cos"), const("sin")
            for i in range(5):
                dve.wait_ge(qkv_full, i + 1)
                o = bank(i, 2, T)
                q1, q2 = (qr[:, i, :], qt2[:, i, :]) if i < 4 else (kr, kt2)
                nc.vector.tensor_tensor(q1, o[:, 0, :], cos, ALU.mult)
                step(nc.vector.tensor_tensor(q2, o[:, 1, :], sin, ALU.mult))
                last = nc.vector.tensor_tensor(q1, q1, q2, ALU.add)
            last.then_inc(rot_ready, 1)
            for half in range(2):
                dve.wait_ge(rsc_full, half + 1)
                m = slice(16 * half, 16 * half + 16)
                src = PS[:, 1024 * half:1024 * half + 1024].rearrange("p (g q) -> p g q", g=2)[:, :, 0:256]
                step(nc.vector.transpose(rs_[:, m, :].rearrange("p (g a) q -> p g (a q)", g=2), src))
                step(nc.vector.tensor_reduce(amax[:, m], rs_[:, m, :], AX, ALU.max))
                nc.vector.tensor_tensor(rs_[:, m, :], rs_[:, m, :], amax[:, m].unsqueeze(2).broadcast_to([128, 16, 32]),
                                        ALU.subtract).then_inc(rsc_shift, 1)
            for half in range(2):
                m = slice(16 * half, 16 * half + 16)
                dve.wait_ge(rsc_exp, half + 1)
                step(nc.vector.tensor_reduce(asum[:, m], rs_[:, m, :], AX, ALU.add))
                step(nc.vector.reciprocal(asum[:, m], asum[:, m]))
                step(nc.vector.tensor_tensor(rp_[:, m, :], rs_[:, m, :], asum[:, m].unsqueeze(2)
                                             .broadcast_to([128, 16, 32]), ALU.mult))
                nc.vector.transpose(rs_[:, m, :], rp_[:, m, :]).then_inc(rp_ready, 1)
            dve.wait_ge(rmix_full, 1)
            turn_heads(nc.vector.tensor_copy, (0, 1), oT_ready)
            dve.wait_ge(wo_full, 1)
            nc.vector.tensor_tensor(x, x, bank(0, TT, C), ALU.add).then_inc(x_ready, 1)
            norm(5)
            nc.vector.tensor_copy(hT, bank(6, CT, T)).then_inc(hT_ready, 1)
            for i in range(IT // 2):
                dve.wait_ge(ffn_silu, i + 1)
                dve.wait_ge(ffn_full, 2 * i + 2)
                nc.vector.tensor_tensor(hm[:, 2 * i:2 * i + 2, :], sgf[:, 2 * i:2 * i + 2, :], bank(2 * i + 1, 2, T),
                                        ALU.mult).then_inc(ffn_ready, 1)
            for j in range(TT):
                dve.wait_ge(ffn_out, j + 1)
                nc.vector.tensor_tensor(x[:, j, :], x[:, j, :], bank(6 + j, TT, C)[:, j, :], ALU.add).then_inc(x_ready, 1)

        block = ctx.enter_context(nc.Block())

        @block.sync
        def _(sp):
            sp.dma_start(x, io["x"]).then_inc(ld_x, 16)
            sp.dma_start(vec, io["vectors"]).then_inc(ld_const, 16)
            sp.dma_start(consts, io["consts"]).then_inc(ld_const, 16)
            sp.dma_start(wch[0], io["chunks"][0]).then_inc(ld_chunk[0], 16)
            sp.dma_start(wkn, io["wk_nat"]).then_inc(ld_wkn, 16)
            sp.dma_start(wch[1], io["chunks"][1]).then_inc(ld_chunk[1], 16)
            sp.dma_start(wkT, io["wkT"]).then_inc(ld_wkT, 16)
            for n in range(2, NCH):
                sp.wait_ge(proj_full, 4 * (n - 1))
                sp.dma_start(wch[n % 2], io["chunks"][n]).then_inc(ld_chunk[n % 2], 16)
                if n == 3:
                    for b in range(2):
                        sp.dma_start(ctxT[b], io["ctxT"][b]).then_inc(ld_ctxT[b], 16)
                        sp.dma_start(keysr[b], io["ctx"][b]).then_inc(ld_ctx[b], 16)
                    sp.dma_start(wvT, io["wvT"]).then_inc(ld_wvT, 16)
            sp.wait_ge(proj_full, 4 * NCH)
            sp.dma_start(wpc, io["wproj"][:, 0:NH, :]).then_inc(ld_wpc, 16)
            sp.wait_ge(front_over, 4)
            for m in range(2):
                sp.dma_start(idx_raw[:, m, :], io["idx"][:, m, :]).then_inc(ld_idx[m], 16)
            sp.wait_ge(idx_ready, 1)
            sp.dma_start(idx_raw[:, 0, :], io["idx"][:, 2, :]).then_inc(ld_idx[2], 16)

            def load_ctxT(b, k):
                sp.wait_ge(st_full, 4 * b - 4)
                sp.dma_start(ctxT[k], io["ctxT"][DS(b, 1)].rearrange("o p c n -> (o p) c n")).then_inc(ld_ctxT[k], 16)

            def load_ctx(b, k):
                sp.wait_ge(pctx, 2 * b - 2)
                sp.dma_start(keysr[k], io["ctx"][DS(b, 1)].rearrange("o p c n -> (o p) c n")).then_inc(ld_ctx[k], 16)

            load_ctxT(2, 0)
            with sp.Fori(1, 3) as i:
                load_ctxT(2 * i + 1, 1)
                load_ctx(2 * i, 0)
                load_ctxT(2 * i + 2, 0)
                load_ctx(2 * i + 1, 1)
            load_ctxT(7, 1)
            sp.dma_start(wpx, io["wproj"][:, NH:2 * NH, :]).then_inc(ld_wpx, 16)
            load_ctx(6, 0)
            load_ctx(7, 1)
            tail_sync(sp)

        @block.tensor
        def _(pe):
            def ring(name, i=0):
                u = RING_AT[name] + i
                if u >= 4:
                    who = RING_OWNER[u - 4]
                    pe.wait_ge(ring_read[who], reads(who, u - 3))
                return 4 + u % 4

            pe.wait_ge(ld_const, 32)
            pe.wait_ge(ln_done, 1)
            o = bank(ring("lnT"), CT, T)
            for i in range(4):
                j, c = i // CT, i % CT
                last = nc.tensor.transpose(o[:, c, j * 128:j * 128 + 128], raw[0][:, j, c * 128:c * 128 + 128], ident)
            last.then_inc(ring_full, 4)

            def project(n):
                pe.wait_ge(xs_ready, SCALED.index(VARIANT[n]) + 1)
                pe.wait_ge(ld_chunk[n % 2], 16 * (n // 2 + 1))
                for q in range(4):
                    j, hf = q // 2, q % 2
                    if n:
                        pe.wait_ge(proj_read, 4 * n - 3 + q)
                    for c in range(CT):
                        last = nc.tensor.matmul(bank(q), xs[:, VARIANT[n], c, j * 128:j * 128 + 128],
                                                wch[n % 2][:, c, hf * 512:hf * 512 + 512],
                                                start=c == 0, stop=c == CT - 1)
                    last.then_inc(proj_full, 1)

            def turn(n):
                pe.wait_ge(z_ready, ZORDER.index(n) + 1)
                pe.wait_ge(z_act, ZORDER.index(n) + 1)
                for i in range(4):
                    if n == 4:
                        pe.wait_ge(proj_read, 20 + i + 1)
                        o = bank(i, 2, T)
                    else:
                        o = bank(ring(f"turn{n}", i), 2, T)
                    for k in range(4):
                        hd, j = k // 2, k % 2
                        c0 = (2 * i + hd) * 128
                        last = nc.tensor.transpose(o[:, hd, j * 128:j * 128 + 128],
                                                   raw[RAW_SLOT[n]][:, j, c0:c0 + 128], ident)
                    last.then_inc(low_full if n == 4 else ring_full, 1)

            def cross_queries(n):
                pe.wait_ge(ring_read["act"], reads("act", RING_AT[f"turn{n}"] + 4))
                pe.wait_ge(bk_ready, 1)
                for i in range(4):
                    nc.tensor.matmul(bank(ring(f"beta{n}", i)), bk, zlnT[:, 2 * i:2 * i + 2, :],
                                     start=True, stop=True).then_inc(ring_full, 1)
                pe.wait_ge(u_ready, n + 1)
                for i in range(8):
                    g, c = i // CT, i % CT
                    nc.tensor.matmul(bank(ring(f"A{n}", i)), wkc[:, 4 * n + g, c * 128:c * 128 + 128],
                                     uT[:, 2 * g:2 * g + 2, :], start=True, stop=True).then_inc(ring_full, 1)

            def scores(n):
                low = n == 4
                if low:
                    pe.wait_ge(low_read["act"], 4)
                else:
                    pe.wait_ge(ring_read["act"], reads("act", RING_AT["turn3"] + 4))
                for i in range(4):
                    o = bank(i if low else ring("scores3", i), TT, 256)
                    for j in range(TT):
                        last = nc.tensor.matmul(o[:, j, :], kT[:, 4 * low + i, j * 128:j * 128 + 128],
                                                zq[low][:, 2 * i:2 * i + 2, j * 128:j * 128 + 128],
                                                start=True, stop=True)
                    last.then_inc(low_full if low else ring_full, 1)

            def mix(n):
                low = n == 4
                pe.wait_ge(pbd_ready, n - 2)
                pe.wait_ge(proj_read, 24)
                for i in range(4):
                    g = 4 * low + i
                    o = bank(i if low else ring("mix3", i), HPG, T)
                    for j in range(TT):
                        last = nc.tensor.matmul(o[:, :, j * 128:j * 128 + 128], v[:, j, g * D:(g + 1) * D],
                                                pbd[low][:, 2 * i + j, :, :], start=True, stop=True)
                    last.then_inc(low_full if low else ring_full, 1)

            project(0)
            pe.wait_ge(ld_wkn, 16)
            for i in range(4):
                nc.tensor.matmul(bank(ring("center", i)), const("center"), wkn[:, i * 512:(i + 1) * 512],
                                 start=True, stop=True).then_inc(ring_full, 1)
            project(1)
            turn(0)
            cross_queries(0)
            project(2)
            turn(1)
            cross_queries(1)
            project(3)
            turn(2)
            project(4)
            turn(3)
            project(5)
            scores(3)
            turn(4)
            scores(4)
            mix(3)
            mix(4)
            o = bank(ring("core"), TT, C)
            for j in range(TT):
                for i in range(NH):
                    if j == 0 and i % 8 == 0:
                        pe.wait_ge(wpc_split, i // 8 + 1)
                    if j == 0 and i % 4 == 0:
                        pe.wait_ge(catc_odd if i // 4 % 2 else catc_even, i // 8 + 1)
                    cat = catc_r[:, i, j * 128:j * 128 + 128]
                    nc.tensor.matmul(o[:, j, :], cat, wpc_hi[i // 8][:, i % 8, :], start=i == 0, stop=False)
                    last = nc.tensor.matmul(o[:, j, :], cat, wpc_lo[:, i, :], start=False, stop=i == NH - 1)
            last.then_inc(ring_full, 1)
            nc.tensor.matmul(bank(0)[:, 0:128], ident, ident, start=True, stop=True).then_inc(front_over, 1)
            loop_pe(pe)
            tail_pe(pe)

        @block.scalar
        def _(act):
            step = Steps(act, act_step)
            nc.scalar.preload_act_table_set("natural_log_exp_and_others")
            act.wait_ge(front_over, 1)

            def read_ring(name, i, dst, **kw):
                u = RING_AT[name] + i
                act.wait_ge(ring_full, u + 1)
                nc.scalar.activation(dst, bank(4 + u % 4, *dst.shape[1:]) if len(dst.shape) > 2 else bank(4 + u % 4),
                                     ACT.Copy, **kw).then_inc(ring_read["act"], 1)

            def read_chunk(n):
                for q in range(4):
                    j, hf = q // 2, q % 2
                    act.wait_ge(proj_full, 4 * n + q + 1)
                    if n == 1 and q == 0:
                        act.wait_ge(ring_full, RING_AT["center"] + 4)
                    if n == 2 and q == 0:
                        act.wait_ge(ring_full, RING_AT["turn0"] + 4)
                    if n == 3 and q == 0:
                        act.wait_ge(ring_full, RING_AT["turn1"] + 4)
                    if n == 4 and q == 0:
                        act.wait_ge(ring_full, RING_AT["turn2"] + 4)
                    dst = v if n == 5 else raw[RAW_SLOT[n]]
                    nc.scalar.activation(dst[:, j, hf * 512:hf * 512 + 512], bank(q), ACT.Copy,
                                         scale=col("w_scale", VARIANT[n])).then_inc(proj_read, 1)

            def cross_queries(n):
                for i in range(4):
                    read_ring(f"beta{n}", i, beta[:, 8 * n + 2 * i:8 * n + 2 * i + 2, :])
                for i in range(8):
                    g, c = i // CT, i % CT
                    u, h0 = RING_AT[f"A{n}"] + i, 8 * n + 2 * g
                    act.wait_ge(ring_full, u + 1)
                    nc.scalar.activation(A[:, :, c, h0 * S:(h0 + 2) * S].rearrange("p b (h s) -> p b h s", h=2),
                                         bank(4 + u % 4, 2, B, S).rearrange("p h b s -> p b h s"), ACT.Copy)\
                        .then_inc(ring_read["act"], 1)

            def normalise(n):
                k = ZORDER.index(n)
                act_rstd(act, step, NH, k + 2, src=nt[:, 0:NH], scale=1.0 / D)
                act.wait_ge(deviations, k + 1)
                for i in range(8):
                    hd = raw[RAW_SLOT[n]][:, 1, i * D:(i + 1) * D]
                    last = nc.scalar.activation(hd, hd, ACT.Identity, scale=rs[:, 8 + i:9 + i], bias=nbias[:, 8 + i:9 + i])
                last.then_inc(z_act, 1)

            def read_turn(n, dst, w, b):
                for i in range(4):
                    if n == 4:
                        act.wait_ge(low_full, i + 1)
                        src = bank(i, 2, T)
                    else:
                        act.wait_ge(ring_full, RING_AT[f"turn{n}"] + i + 1)
                        src = bank(4 + (RING_AT[f"turn{n}"] + i) % 4, 2, T)
                    nc.scalar.activation(dst[:, 2 * i:2 * i + 2, :], src, ACT.Identity, scale=col(w), bias=col(b))\
                        .then_inc(low_read["act"] if n == 4 else ring_read["act"], 1)

            act_rstd(act, step, TT, 0)
            act_rstd(act, step, TT, 1)
            read_chunk(0)
            for i in range(4):
                read_ring("center", i, wkc[:, 2 * i:2 * i + 2, :])
            normalise(0)
            read_chunk(1)
            read_turn(0, zlnT, "qxln_w", "qxln_b")
            cross_queries(0)
            normalise(1)
            read_chunk(2)
            read_turn(1, zlnT, "qxln_w", "qxln_b")
            cross_queries(1)
            normalise(2)
            read_chunk(3)
            read_turn(2, kT, "kln_w", "kln_b")
            normalise(3)
            read_chunk(4)
            act.wait_ge(ring_full, RING_AT["A1"] + 8)
            act.wait_ge(wk_centered, 1)
            nc.scalar.activation(wk_hi, wkT, ACT.Copy).then_inc(wk_hi_ready, 1)
            read_turn(3, zlnT, "qln_w", "qln_b")
            normalise(4)
            read_chunk(5)
            read_turn(4, zq[1], "qln_w", "qln_b")
            def core_exponentials(n):
                act.wait_ge(shifted_core, n + 1)
                nc.scalar.activation(at_p[n], at_s[n], ACT.Exp, scale=SCALE).then_inc(exp_core, 1)

            def smooth(n):
                for i in range(4):
                    if n:
                        act.wait_ge(low_full, 8 + i + 1)
                        src = bank(i, HPG, T)
                    else:
                        act.wait_ge(ring_full, RING_AT["mix3"] + i + 1)
                        src = bank(4 + (RING_AT["mix3"] + i) % 4, HPG, T)
                    for a in range(HPG):
                        hd = 8 * n + 2 * i + a
                        last = nc.scalar.activation(y_all[n][:, 2 * i + a, :], src[:, a, :], ACT.Copy,
                                                    scale=inv_smooth[:, hd:hd + 1])
                    last.then_inc(y_core if n else ring_read["act"], 1)

            core_exponentials(0)
            act.wait_ge(ld_ctxT[0], 16)
            nc.scalar.activation(ctx_hi[0], ctxT[0], ACT.Copy).then_inc(ctx_hi_ready, 1)
            core_exponentials(1)
            smooth(0)
            act.wait_ge(ld_wpc, 16)
            act.wait_ge(low_full, 8)
            for i in range(2):
                nc.scalar.activation(wpc_hi[i], wpc[:, 8 * i:8 * i + 8, :], ACT.Copy).then_inc(wpc_hi_ready, 1)
            smooth(1)
            read_ring("core", 0, core)
            nc.scalar.activation(nt[:, 31:32], nt[:, 0:1], ACT.Copy).then_inc(front_over, 1)
            loop_act(act, step)
            tail_act(act, step)

        @block.gpsimd
        def _(pool):
            step = Steps(pool, pool_step)
            nc.gpsimd.memset(eps, EPS).then_inc(front_over, 1)
            pool.wait_ge(ring_full, RING_AT["A1"] + 8)
            nc.gpsimd.memset(pbd[0], 0.0).then_inc(pbd_zero, 1)
            pool.wait_ge(low_full, 4)
            nc.gpsimd.memset(pbd[1], 0.0).then_inc(pbd_zero, 1)
            def finish_rounding(n):
                pool.wait_ge(rounded, n + 1)
                m, t = rounding[n % 2]
                nc.gpsimd.tensor_tensor(catc_flat[n], t, m, ALU.subtract).then_inc(catc_even, 1)

            pool.wait_ge(wk_hi_ready, 1)
            nc.gpsimd.tensor_tensor(wk_lo, wkT, wk_hi, ALU.subtract).then_inc(wk_split, 1)
            pool.wait_ge(ctx_hi_ready, 1)
            nc.gpsimd.tensor_tensor(ctx_lo[0], ctxT[0], ctx_hi[0], ALU.subtract).then_inc(ctx_split, 1)
            for i in range(2):
                pool.wait_ge(wpc_hi_ready, i + 1)
                nc.gpsimd.tensor_tensor(wpc_lo[:, 8 * i:8 * i + 8, :], wpc[:, 8 * i:8 * i + 8, :], wpc_hi[i],
                                        ALU.subtract).then_inc(wpc_split, 1)
                if i == 0:
                    finish_rounding(0)
            finish_rounding(2)
            pool.wait_ge(front_over, 4)
            loop_pool(pool, step)
            tail_pool(pool, step)

        @block.vector
        def _(dve):
            step = Steps(dve, dve_step)
            dve.wait_ge(ld_x, 16)
            h0 = raw[0][:, :, 0:C]
            step(token_norm(dve, step, x, h0, 0))
            token_norm(dve, step, h0, h0, 1).then_inc(ln_done, 1)
            dve.wait_ge(ld_const, 32)
            step(nc.vector.reciprocal(inv_scale, vec[:, COL["in_scale"]]))
            step(nc.vector.reciprocal(inv_smooth, vec[:, COL["smooth"]]))
            nc.vector.tensor_copy(bk, col("kxln_b").broadcast_to([128, 128])).then_inc(bk_ready, 1)
            dve.wait_ge(ring_full, RING_AT["lnT"] + 4)
            o = bank(4 + RING_AT["lnT"] % 4, CT, T)
            for c in range(CT):
                last = nc.vector.tensor_scalar(lnT[:, c, :], o[:, c, :], col("ln_w", c), col("ln_b", c),
                                               ALU.mult, ALU.add)
            last.then_inc(ring_read["dve"], 4)
            dve.wait_ge(ring_read["dve"], 4)

            def scaled_input(n):
                yv = y_bf[:, 0:CT * T].rearrange("p (c t) -> p c t", c=CT)
                for c in range(CT):
                    last = nc.vector.tensor_scalar(yv[:, c, :], lnT[:, c, :], inv_scale[:, n * CT + c:n * CT + c + 1],
                                                   FP8_MAX, ALU.mult, ALU.min)
                step(last)
                step(nc.vector.tensor_scalar(y_bf[:, 0:CT * T], y_bf[:, 0:CT * T], -FP8_MAX, None, ALU.max))
                step(round_fp8(step, CT * T, t_fp[:, 0:CT * T]))
                for c in range(CT):
                    last = nc.vector.tensor_scalar(xs[:, n, c, :], t_fp[:, c * T:(c + 1) * T],
                                                   col("in_scale", n * CT + c), None, ALU.mult)
                last.then_inc(xs_ready, 1)
                dve.wait_ge(xs_ready, SCALED.index(n) + 1)

            scaled_input(0)

            def norm_heads(n):
                k = ZORDER.index(n)
                r = raw[RAW_SLOT[n]]
                for j in range(TT):
                    dve.wait_ge(proj_read, 4 * n + 2 * j + 2)
                    for i in range(8):
                        last = nc.vector.bn_stats(st[:, 8 * j + i, :], r[:, j, i * D:(i + 1) * D])
                step(last)
                step(nc.vector.tensor_tensor(mv[:, :, 0], st[:, :, 1], st[:, :, 4], ALU.add))
                step(nc.vector.tensor_tensor(mv[:, :, 1], st[:, :, 1], st[:, :, 4], ALU.subtract))
                step(nc.vector.tensor_tensor(nt[:, 0:NH], st[:, :, 2], st[:, :, 5], ALU.add))
                step(nc.vector.scalar_tensor_tensor(mv[:, :, 1], mv[:, :, 1], D / 4.0, mv[:, :, 1], ALU.mult, ALU.mult))
                nc.vector.tensor_tensor(nt[:, 0:NH], nt[:, 0:NH], mv[:, :, 1], ALU.add).then_inc(ln_var, 1)
                dve.wait_ge(ln_var, k + 3)
                step(nc.vector.tensor_scalar(var[:, 0:NH], nt[:, 0:NH], 1.0 / D, EPS, ALU.mult, ALU.add))
                dve.wait_ge(ln_rstd, k + 3)
                newton(dve, step, rs[:, 0:NH], rs0[:, 0:NH], var[:, 0:NH], nt[:, 0:NH])
                nc.vector.scalar_tensor_tensor(nbias, mv[:, :, 0], -0.5, rs[:, 0:NH], ALU.mult, ALU.mult)\
                    .then_inc(deviations, 1)
                dve.wait_ge(deviations, k + 1)
                for i in range(8):
                    hd = r[:, 0, i * D:(i + 1) * D]
                    last = nc.vector.tensor_scalar(hd, hd, rs[:, i:i + 1], nbias[:, i:i + 1], ALU.mult, ALU.add)
                last.then_inc(z_ready, 1)
                dve.wait_ge(z_ready, k + 1)
                dve.wait_ge(z_act, k + 1)

            def read_turn_cross(n):
                u0 = RING_AT[f"turn{n}"]
                if n:
                    dve.wait_ge(ring_full, RING_AT[f"A{n - 1}"] + 8)
                for i in range(4):
                    dve.wait_ge(ring_read["act"], reads("act", u0 + i + 1))
                    last = nc.vector.tensor_scalar(uT[:, 2 * i:2 * i + 2, :], zlnT[:, 2 * i:2 * i + 2, :],
                                                   col("kxln_w"), None, ALU.mult)
                last.then_inc(u_ready, 1)

            norm_heads(0)
            scaled_input(1)
            read_turn_cross(0)
            norm_heads(1)
            scaled_input(3)
            read_turn_cross(1)
            scaled_input(2)
            dve.wait_ge(ld_wkT, 16)
            heads = wkT.rearrange("p c (g d) -> p (c g) d", g=G)
            step(nc.vector.tensor_reduce(nt[:, 0:CT * G], heads, AX, ALU.add))
            step(nc.vector.tensor_scalar(nt[:, 0:CT * G], nt[:, 0:CT * G], 1.0 / D, None, ALU.mult))
            nc.vector.tensor_tensor(heads, heads, nt[:, 0:CT * G].unsqueeze(2).broadcast_to([128, CT * G, D]),
                                    ALU.subtract).then_inc(wk_centered, 1)
            norm_heads(2)
            norm_heads(3)
            norm_heads(4)

            def core_scores(low):
                if low:
                    dve.wait_ge(low_full, 8)
                else:
                    dve.wait_ge(ring_full, RING_AT["scores3"] + 4)
                sc = PS[:, 2048 * (1 - low):2048 * (2 - low)].rearrange("p (a q) -> p a q", a=8)
                for b4 in range(4):
                    q0 = 32 * b4
                    src = sc[q0:q0 + 32].rearrange("p a (h q) -> p (a h) q", h=2)[:, :, q0:q0 + 32]
                    last = nc.vector.transpose(at_s[low][q0:q0 + 32], src)
                if low:
                    step(last)
                else:
                    last.then_inc(ring_read["dve"], 4)
                    dve.wait_ge(ring_read["dve"], reads("dve", RING_AT["scores3"] + 4))
                step(nc.vector.tensor_reduce(amax[:, 0:16], at_s[low], AX, ALU.max))
                nc.vector.tensor_tensor(at_s[low], at_s[low], amax[:, 0:16].unsqueeze(2).broadcast_to([128, 16, 32]),
                                        ALU.subtract).then_inc(shifted_core, 1)

            def core_weights(low):
                dve.wait_ge(exp_core, low + 1)
                step(nc.vector.tensor_reduce(asum[:, 0:16], at_p[low], AX, ALU.add))
                step(nc.vector.reciprocal(asum[:, 0:16], asum[:, 0:16]))
                step(nc.vector.tensor_tensor(at_p[low], at_p[low], asum[:, 0:16].unsqueeze(2)
                                             .broadcast_to([128, 16, 32]), ALU.mult))
                dve.wait_ge(pbd_zero, low + 1)
                pb = pbd[low].rearrange("p a h q -> p (a h) q")
                for b4 in range(4):
                    q0 = 32 * b4
                    last = nc.vector.transpose(pb[q0:q0 + 32, :, q0:q0 + 32], at_p[low][q0:q0 + 32])
                last.then_inc(pbd_ready, 1)

            core_scores(0)
            core_weights(0)
            core_scores(1)
            core_weights(1)
            for n in range(4):
                if n < 2:
                    dve.wait_ge(ring_read["act"], reads("act", RING_AT["mix3"] + 2 * n + 2))
                else:
                    dve.wait_ge(y_core, 2 * n - 2)
                y4 = y_all[n // 2][:, 4 * (n % 2):4 * (n % 2) + 4, :].rearrange("p a t -> p (a t)")
                step(nc.vector.tensor_scalar(y_bf, y4, FP8_MAX, -FP8_MAX, ALU.min, ALU.max))
                m, t = rounding[n % 2]
                if n > 1:
                    dve.wait_ge(catc_odd if n % 2 else catc_even, 1)
                step(nc.vector.tensor_scalar(e_bf.bitcast(u16), y_bf.bitcast(u16), 0x7F80, None, ALU.bitwise_and))
                step(nc.vector.tensor_scalar(m, e_bf, FP8_MIN_NORMAL, ROUND, ALU.max, ALU.mult))
                nc.vector.tensor_tensor(t, y_bf, m, ALU.add).then_inc(rounded, 1)
                dve.wait_ge(rounded, n + 1)
                if n % 2:
                    nc.vector.tensor_tensor(catc_flat[n], t, m, ALU.subtract).then_inc(catc_odd, 1)
            nc.vector.memset(nt[:, 29:30], 0.0).then_inc(front_over, 1)
            loop_dve(dve, step)
            tail_dve(dve, step)


def kernel(**inputs):
    import numpy as np
    import concourse.bacc as bacc
    from concourse.bass_utils import run_bass_kernel_spmd

    a = {k: np.asarray(v) for k, v in inputs.items()}
    f32 = np.float32

    def tiles(w):
        return w.reshape(-1, 128, w.shape[-1]).transpose(1, 0, 2)

    def column(v, n):
        return np.asarray(v).reshape(n, 128).T

    X, M = "L0_xattn_", "L0_attn_"
    cols = [column(a[X + "ln_w"], CT), column(a[X + "ln_b"], CT)]
    cols += [column(a[X + n + "_in_scale"], CT) for n in ("qx", "k", "v", "q")]
    cols += [column(a[X + n], 1) for n in ("qln_w", "qln_b", "kln_w", "kln_b", "qxln_w", "qxln_b", "kxln_w", "kxln_b")]
    cols += [column(a[X + "proj_smooth"], 2 * NH)]
    cols += [tiles(a[M + "conv_w"][:, 0, :]).reshape(128, 8), column(a[M + "conv_b"], CT),
             column(a[M + "D"], CT)]
    for n in ("wqx_scale", "wk_scale", "wv_scale", "wq_scale", "proj_w_scale", "proj_in_scale"):
        cols += [np.broadcast_to(a[X + n].reshape(1, 1), (128, 1))]
    cols += [np.broadcast_to(a["L1_ffn_lut"].reshape(1, LUTN), (128, LUTN))]
    cols += [np.concatenate([a[M + "A_log"], np.zeros(64, f32)]).reshape(128, 1)]
    vectors = np.ascontiguousarray(np.concatenate(cols, 1))
    assert vectors.shape == (128, NVEC), vectors.shape

    d = np.arange(128) % 32
    inv = 1.0 / 10000.0 ** (np.arange(0, 8, 2, dtype=f32) / f32(8))
    ang = (np.arange(S, dtype=f32)[None, :] * np.where(d < 8, inv.astype(f32)[np.minimum(d // 2, 3)], 0)[:, None]).astype(f32)
    cos, sin = np.cos(ang), np.sin(ang)
    sin = sin * np.where(d % 2 == 0, -1.0, 1.0)[:, None]
    cos, sin = (np.broadcast_to(t[:, None, :], (128, B, S)).reshape(128, T) for t in (cos, sin))
    consts = np.ascontiguousarray(np.concatenate([
        np.eye(128), np.ones((128, 128)), np.eye(128) - 1.0 / D, cos, sin,
        np.broadcast_to(np.arange(LUTN)[None, :], (128, LUTN))], 1).astype(f32))

    chunks = [a[X + "wqx"][:1024], a[X + "wqx"][1024:], a[X + "wk"], a[X + "wq"][:1024], a[X + "wq"][1024:], a[X + "wv"]]
    wkv = a[X + "w_kv_x"]
    ctx = a["ctx_2048"]
    swap = np.array([1, 0, 3, 2, 5, 4, 7, 6] + list(range(8, 16)))

    def heads(w, n):
        w = w.reshape(C, 4, n, 16).transpose(0, 2, 1, 3)
        return w

    def padded(w):
        z = np.zeros(w.shape[:-1] + (32,), f32)
        z[..., :16] = w
        return z.reshape(C, -1)

    wq, wk, wv = heads(a["L1_attn_Wq"], 4), heads(a["L1_attn_Wk"], 1), heads(a["L1_attn_Wv"], 1)
    wo = np.zeros((4, 4, 32, C), f32)
    wo[:, :, :16] = a["L1_attn_Wo"].reshape(4, 4, 16, C).transpose(1, 0, 2, 3)
    pad = np.full((C, IPAD - INTER), LUTN, np.int32)
    idx = [np.concatenate([a["L1_ffn_gate_idx"].astype(np.int32).T, pad], 1),
           np.concatenate([a["L1_ffn_up_idx"].astype(np.int32).T, pad], 1),
           np.concatenate([a["L1_ffn_down_idx"].astype(np.int32).T, pad.T], 0)]
    idx = np.stack([tiles(t).reshape(128, CT * IPAD) for t in idx], 1)
    wx = a[M + "Wxproj"].T
    wx = np.concatenate([wx[:, :2 * SSM], np.broadcast_to(wx[:, 2 * SSM:], (C, SSM)), a[M + "Winproj"].T], 1)
    mask = a["mask_BxS2_bk0"].view(np.int32)
    arrays = {
        "consts": consts, "vectors": vectors, "x": tiles(a["x"].reshape(T, C)),
        "wk_nat": wkv[:1024].reshape(G, D, C).transpose(1, 0, 2).reshape(128, G * C),
        "chunks": np.stack([tiles(w.T) for w in chunks]),
        "wkT": tiles(wkv[:1024].T), "wvT": tiles(wkv[1024:].T), "wproj": tiles(a[X + "wproj"].T),
        "ctxT": ctx.reshape(B, NK, CT, 128).transpose(0, 3, 2, 1), "ctx": ctx.reshape(B, KT, 128, C).transpose(0, 2, 1, 3),
        "idx": idx, "ssm_in": tiles(wx), "ssm_out": a[M + "Woutproj"].T, "router": tiles(a["L0_ffn_Wr"]),
        "gate_up": np.stack([a["L0_ffn_" + n].reshape(NE, CT, 128, C).transpose(0, 2, 1, 3).reshape(NE, 128, CT * C)
                             for n in ("Wg", "Wu")], 2),
        "down": a["L0_ffn_Wd"].reshape(NE, CT, 128, C).transpose(2, 0, 1, 3).reshape(128, NE, CT * C),
        "mask": mask,
        "wq_rot": np.stack([tiles(padded(wq)), tiles(padded(wq[..., swap]))], 1),
        "wk_rot": np.stack([tiles(padded(wk)), tiles(padded(wk[..., swap]))], 1),
        "wv_rot": tiles(padded(wv)), "wo_rot": wo.reshape(4, 128, C).transpose(1, 0, 2),
    }
    nc = bacc.Bacc("TRN2", target_bir_lowering=False, num_devices=1)
    io, sent = {}, {}
    for name, v in arrays.items():
        v = np.ascontiguousarray(v)
        sent["in_" + name] = v
        io[name] = nc.dram_tensor("in_" + name, v.shape, mybir.dt.from_np(v.dtype), kind="ExternalInput").ap()
    out = nc.dram_tensor("out_x", (128, TT, C), fp32, kind="ExternalOutput").ap()
    build(nc, io, out)
    r = run_bass_kernel_spmd(nc, [sent], core_ids=[0])
    return r.results[0]["out_x"].transpose(1, 0, 2).reshape(B, S, C)
```
